# Optimizing a Trainium2 kernel written in Bass

```python
import numpy as np
import jax
import jax.numpy as jnp

def _softmax(x, axis=-1):
    return jax.nn.softmax(x, axis=axis)

def _gelu(x):
    return jax.nn.gelu(x, approximate=True)

def _silu(x):
    return jax.nn.silu(x)

def _sigmoid(x):
    return jax.nn.sigmoid(x)

def _layernorm(x, axis=-1, eps=1e-05):
    m = jnp.mean(x, axis=axis, keepdims=True)
    v = jnp.var(x, axis=axis, keepdims=True)
    return (x - m) / jnp.sqrt(v + eps)

def _scatter_add(tgt, idx, src, axis=0):
    return tgt.at[idx].add(src)

def _segment_sum(src, seg, n):
    return jax.ops.segment_sum(src, seg, n)
kernel_name = 'mk_conv_attn_hybrid_d2_conv_nchw512_r4_289ad9'

def setup_inputs(seed: int=0):
    np.random.seed(seed)
    _w = jnp.asarray

    def _rec_inputs():
        import jax
        import jax.numpy as jnp
        _gk = jax.random.key(seed)
        x = -0.000125 + 0.9999 * jax.random.normal(jax.random.fold_in(_gk, 1), (16, 128, 16, 16), jnp.float32)
        return x
    x = _rec_inputs()

    def _L0_conv_setup():
        import jax, jax.numpy as jnp
        import numpy as np
        B, C, H, W = (16, 128, 16, 16)
        D = C // 8
        key = jax.random.key(seed)
        ks = jax.random.split(key, 8)
        s = 0.02
        x = jax.random.normal(ks[0], (B, C, H, W), dtype=jnp.float32)
        Wq = jax.random.normal(ks[1], (D, C), dtype=jnp.float32) * s
        bq = jnp.zeros((D,), dtype=jnp.float32)
        Wk = jax.random.normal(ks[2], (D, C), dtype=jnp.float32) * s
        bk = jnp.zeros((D,), dtype=jnp.float32)
        Wv = jax.random.normal(ks[3], (C, C), dtype=jnp.float32) * s
        bv = jnp.zeros((C,), dtype=jnp.float32)
        gamma = jnp.full((1,), 0.5, dtype=jnp.float32)
        return {'x': x, 'Wq': Wq, 'bq': bq, 'Wk': Wk, 'bk': bk, 'Wv': Wv, 'bv': bv, 'gamma': gamma}
    _L0_conv_all = _L0_conv_setup()
    _L0_conv_in = {k: v for k, v in _L0_conv_all.items() if k in ('Wq', 'bq', 'Wk', 'bk', 'Wv', 'bv', 'gamma')}
    del _L0_conv_all

    def _L1_attn_setup():
        import jax, jax.numpy as jnp
        import numpy as np
        HIDDEN = 128
        NUM_HEADS = 8
        HEAD_DIM = HIDDEN // NUM_HEADS
        SCALE = float(np.sqrt(HEAD_DIM))
        key = jax.random.key(seed)
        ks = jax.random.split(key, 5)
        B, S = (4, 512)
        x = jax.random.normal(ks[0], (B, S, HIDDEN), dtype=jnp.float32)
        w_std = 1.0 / np.sqrt(HIDDEN)
        Wq = jax.random.normal(ks[1], (HIDDEN, HIDDEN), dtype=jnp.float32) * w_std
        Wk = jax.random.normal(ks[2], (HIDDEN, HIDDEN), dtype=jnp.float32) * w_std
        Wv = jax.random.normal(ks[3], (HIDDEN, HIDDEN), dtype=jnp.float32) * w_std
        Wo = jax.random.normal(ks[4], (HIDDEN, HIDDEN), dtype=jnp.float32) * w_std
        return {'x': x, 'Wq': Wq, 'Wk': Wk, 'Wv': Wv, 'Wo': Wo}
    _L1_attn_all = _L1_attn_setup()
    _L1_attn_in = {k: v for k, v in _L1_attn_all.items() if k in ('Wq', 'Wk', 'Wv', 'Wo')}
    del _L1_attn_all

    def _L1_ffn_setup():
        import jax, jax.numpy as jnp
        import numpy as np
        B, S, D = (4, 512, 128)
        E, H, K = (8, 256, 2)

        def _moe_forward(x, router_w, router_b, w1, b1, wg, bg, wv, bv, w2, b2):
            b, s, d = x.shape
            xf = x.reshape(-1, d)
            T = xf.shape[0]
            scores = xf @ router_w + router_b
            probs = jax.nn.softmax(scores, axis=-1)
            topk_p, topk_i = jax.lax.top_k(probs, K)
            gates = jnp.zeros((T, E), xf.dtype).at[jnp.arange(T)[:, None], topk_i].set(topk_p)
            h = jnp.einsum('td,edh->teh', xf, w1) + b1[None]
            gated = jax.nn.silu(jnp.einsum('teh,ehf->tef', h, wg) + bg[None]) * (jnp.einsum('teh,ehf->tef', h, wv) + bv[None])
            y = jnp.einsum('tef,efd->ted', gated, w2) + b2[None]
            out = jnp.einsum('ted,te->td', y, gates)
            return out.reshape(b, s, d)
        key = jax.random.key(seed)
        ks = jax.random.split(key, 8)
        s_in = 0.02
        return {'x': jax.random.normal(ks[0], (B, S, D), jnp.float32), 'router_w': jax.random.normal(ks[1], (D, E), jnp.float32) * s_in, 'router_b': jnp.zeros((E,), jnp.float32), 'w1': jax.random.normal(ks[2], (E, D, H), jnp.float32) * s_in, 'b1': jnp.zeros((E, H), jnp.float32), 'wg': jax.random.normal(ks[3], (E, H, H), jnp.float32) * s_in, 'bg': jnp.zeros((E, H), jnp.float32), 'wv': jax.random.normal(ks[4], (E, H, H), jnp.float32) * s_in, 'bv': jnp.zeros((E, H), jnp.float32), 'w2': jax.random.normal(ks[5], (E, H, D), jnp.float32) * s_in, 'b2': jnp.zeros((E, D), jnp.float32)}
    _L1_ffn_all = _L1_ffn_setup()
    _L1_ffn_in = {k: v for k, v in _L1_ffn_all.items() if k in ('router_w', 'router_b', 'w1', 'b1', 'wg', 'bg', 'wv', 'bv', 'w2', 'b2')}
    del _L1_ffn_all
    return {'x': x, 'L0_conv_Wq': _L0_conv_in['Wq'], 'L0_conv_bq': _L0_conv_in['bq'], 'L0_conv_Wk': _L0_conv_in['Wk'], 'L0_conv_bk': _L0_conv_in['bk'], 'L0_conv_Wv': _L0_conv_in['Wv'], 'L0_conv_bv': _L0_conv_in['bv'], 'L0_conv_gamma': _L0_conv_in['gamma'], 'L1_attn_Wq': _L1_attn_in['Wq'], 'L1_attn_Wk': _L1_attn_in['Wk'], 'L1_attn_Wv': _L1_attn_in['Wv'], 'L1_attn_Wo': _L1_attn_in['Wo'], 'L1_ffn_router_w': _L1_ffn_in['router_w'], 'L1_ffn_router_b': _L1_ffn_in['router_b'], 'L1_ffn_w1': _L1_ffn_in['w1'], 'L1_ffn_b1': _L1_ffn_in['b1'], 'L1_ffn_wg': _L1_ffn_in['wg'], 'L1_ffn_bg': _L1_ffn_in['bg'], 'L1_ffn_wv': _L1_ffn_in['wv'], 'L1_ffn_bv': _L1_ffn_in['bv'], 'L1_ffn_w2': _L1_ffn_in['w2'], 'L1_ffn_b2': _L1_ffn_in['b2']}

def reference(x, L0_conv_Wq, L0_conv_bq, L0_conv_Wk, L0_conv_bk, L0_conv_Wv, L0_conv_bv, L0_conv_gamma, L1_attn_Wq, L1_attn_Wk, L1_attn_Wv, L1_attn_Wo, L1_ffn_router_w, L1_ffn_router_b, L1_ffn_w1, L1_ffn_b1, L1_ffn_wg, L1_ffn_bg, L1_ffn_wv, L1_ffn_bv, L1_ffn_w2, L1_ffn_b2):
    import jax
    import jax.numpy as jnp

    def _L0_conv_ref(x, Wq, bq, Wk, bk, Wv, bv, gamma):
        import jax, jax.numpy as jnp
        import numpy as np
        B, C, H, W = (16, 128, 16, 16)
        D = C // 8
        b, c, h, w = x.shape
        n = h * w
        xf = x.reshape(b, c, n)
        q = jnp.einsum('bcn,dc->bdn', xf, Wq) + bq[None, :, None]
        k = jnp.einsum('bcn,dc->bdn', xf, Wk) + bk[None, :, None]
        v = jnp.einsum('bcn,oc->bon', xf, Wv) + bv[None, :, None]
        vk = jnp.einsum('bcn,bdn->bcd', v, k)
        out = jnp.einsum('bcd,bdn->bcn', vk, q)
        out = out.reshape(b, c, h, w)
        return gamma * out + x

    def _L1_attn_ref(x, Wq, Wk, Wv, Wo):
        import jax, jax.numpy as jnp
        import numpy as np
        HIDDEN = 128
        NUM_HEADS = 8
        HEAD_DIM = HIDDEN // NUM_HEADS
        SCALE = float(np.sqrt(HEAD_DIM))
        B, S, D = x.shape
        H, Hd = (NUM_HEADS, HEAD_DIM)
        q = (x @ Wq.T).reshape(B, S, H, Hd).transpose(0, 2, 1, 3)
        k = (x @ Wk.T).reshape(B, S, H, Hd).transpose(0, 2, 1, 3)
        v = (x @ Wv.T).reshape(B, S, H, Hd).transpose(0, 2, 1, 3)
        attn = jnp.einsum('bhqd,bhkd->bhqk', q, k) / SCALE
        attn = jax.nn.softmax(attn, axis=-1)
        out = jnp.einsum('bhqk,bhkd->bhqd', attn, v)
        out = out.transpose(0, 2, 1, 3).reshape(B, S, D)
        return out @ Wo.T

    def _L1_ffn_ref(x, router_w, router_b, w1, b1, wg, bg, wv, bv, w2, b2):
        import jax, jax.numpy as jnp
        import numpy as np
        B, S, D = (4, 512, 128)
        E, H, K = (8, 256, 2)

        def _moe_forward(x, router_w, router_b, w1, b1, wg, bg, wv, bv, w2, b2):
            b, s, d = x.shape
            xf = x.reshape(-1, d)
            T = xf.shape[0]
            scores = xf @ router_w + router_b
            probs = jax.nn.softmax(scores, axis=-1)
            topk_p, topk_i = jax.lax.top_k(probs, K)
            gates = jnp.zeros((T, E), xf.dtype).at[jnp.arange(T)[:, None], topk_i].set(topk_p)
            h = jnp.einsum('td,edh->teh', xf, w1) + b1[None]
            gated = jax.nn.silu(jnp.einsum('teh,ehf->tef', h, wg) + bg[None]) * (jnp.einsum('teh,ehf->tef', h, wv) + bv[None])
            y = jnp.einsum('tef,efd->ted', gated, w2) + b2[None]
            out = jnp.einsum('ted,te->td', y, gates)
            return out.reshape(b, s, d)
        return _moe_forward(x, router_w, router_b, w1, b1, wg, bg, wv, bv, w2, b2)

    def _gn(v, G=32, eps=1e-05):
        B_, C_, H_, W_ = v.shape
        g = v.reshape(B_, G, C_ // G, H_, W_)
        m = jnp.mean(g, axis=(2, 3, 4), keepdims=True)
        s = jnp.var(g, axis=(2, 3, 4), keepdims=True)
        return ((g - m) / jnp.sqrt(s + eps)).reshape(v.shape)

    def _ln_c(v, eps=1e-06):
        m = jnp.mean(v, axis=1, keepdims=True)
        s = jnp.var(v, axis=1, keepdims=True)
        return (v - m) / jnp.sqrt(s + eps)

    def _ln_t(v, eps=1e-05):
        m = jnp.mean(v, axis=-1, keepdims=True)
        s = jnp.var(v, axis=-1, keepdims=True)
        return (v - m) / jnp.sqrt(s + eps)

    def _to_tokens(v):
        B_, C_, H_, W_ = v.shape
        return v.reshape(B_, C_, H_ * W_).transpose(0, 2, 1)

    def _from_tokens(t, like):
        B_, C_, H_, W_ = like.shape
        return t.transpose(0, 2, 1).reshape(B_, C_, H_, W_)
    x = x + _L0_conv_ref(_gn(x), L0_conv_Wq, L0_conv_bq, L0_conv_Wk, L0_conv_bk, L0_conv_Wv, L0_conv_bv, L0_conv_gamma)
    t = _to_tokens(x)
    t = t + _L1_attn_ref(_ln_t(t), L1_attn_Wq, L1_attn_Wk, L1_attn_Wv, L1_attn_Wo)
    t = t + _L1_ffn_ref(_ln_t(t), L1_ffn_router_w, L1_ffn_router_b, L1_ffn_w1, L1_ffn_b1, L1_ffn_wg, L1_ffn_bg, L1_ffn_wv, L1_ffn_bv, L1_ffn_w2, L1_ffn_b2)
    x = _from_tokens(t, x)
    return x

_drawn_inputs = setup_inputs


def setup_inputs(seed=0):
    import zlib

    import numpy as np

    out = dict(_drawn_inputs(seed))
    spreads = {'L0_conv_bq': (0.0, 0.1),
     'L0_conv_bk': (0.0, 0.1),
     'L0_conv_bv': (0.0, 0.1),
     'L1_ffn_router_b': (0.0, 0.8),
     'L1_ffn_b1': (0.0, 0.8),
     'L1_ffn_bg': (0.0, 0.8),
     'L1_ffn_bv': (0.0, 0.8),
     'L1_ffn_b2': (0.0, 2.0)}
    factors = {'L1_ffn_router_w': 7.192,
     'L1_ffn_w1': 8.0,
     'L1_ffn_wg': 8.0,
     'L1_ffn_wv': 8.0,
     'L1_ffn_w2': 8.0}
    for name, (base, spread) in spreads.items():
        noise = np.random.default_rng([zlib.crc32(name.encode()), seed]).standard_normal(out[name].shape)
        drawn = base * np.exp(spread * noise) if base else spread * noise
        out[name] = jnp.asarray(drawn.astype(out[name].dtype))
    for name, factor in factors.items():
        out[name] = (out[name] * factor).astype(out[name].dtype)
    return out
```

```python
from contextlib import ExitStack

import concourse.bass as bass
import numpy as np
from concourse import mybir

F32 = mybir.dt.float32
F32R = mybir.dt.float32r
BF16 = mybir.dt.bfloat16
U32 = mybir.dt.uint32
I32 = mybir.dt.int32
ALU = mybir.AluOpType
ACT = mybir.ActivationFunctionType
AX = mybir.AxisListType

B = 16
C = 128
N = 256
P = 128
TPB = N // P
NT = B * TPB
TOK = B * N
KD = 16
H = 8
HD = 16
E = 8
TOP = 2
FF = 256
GN_EPS = 1e-5
LN_EPS = 1e-5
SCALE = 0.25
RING = 3
STACK = 6 * HD
QROWS = STACK + 3
LOADS = 12
FIRST, LAST = 8, 16
ROW = C + 2
SLOTS = TOK + P
MAXT = TOK // P
ST = 72
assert ST >= TOP * TOK // P + E - 1
ROUTE = 23
CLD = 16 * 22
SPARE = ST - TOP * TOK // P
PADS = E + SPARE
CST = 3 * P + 2 * E + MAXT + E * E + ST


def need(eng, sem, items, per=1, cap=None):
    v = items * per
    if isinstance(v, int):
        if cap is not None:
            v = min(v, cap * per)
        if v <= 0:
            return
    eng.wait_ge(sem, v)


def done(eng, sem, images, per=1, extra=0):
    v = images * per + extra
    if isinstance(v, int):
        v = min(v, B * per)
        if v <= 0:
            return
    eng.wait_ge(sem, v)


def waits_after(eng, met, waits, most=None):
    values = []
    for _, items, *more in waits:
        per = more[0] if more else 1
        v = items * per + (more[1] if len(more) > 1 else 0)
        if not isinstance(v, int):
            eng.lower_val(v)
        elif most is not None:
            v = min(v, most * per)
        values.append(v)
    eng.wait_ge(*met)
    for w, v in zip(waits, values):
        if not isinstance(v, int) or v > 0:
            eng.wait_ge(w[0], v)


def done_after(eng, met, *waits):
    waits_after(eng, met, waits, B)


def need_after(eng, met, *waits):
    waits_after(eng, met, waits)


def live(b):
    return not isinstance(b, int) or 0 <= b < B


def folds(t):
    return isinstance(t, int) and 0 <= t < E


def within(j):
    return not isinstance(j, int) or 0 <= j < ST


def in_lane(i, lane, lanes=4):
    return (i - lane) * (16 // lanes) + 16


def pick(t, i, n=1):
    return t[:, bass.ds(i, n), :].rearrange("p a n -> p (a n)")


def steps(eng, step, last):
    for t in range(FIRST):
        step(t, t % 2)
    with eng.Fori(FIRST, LAST - 1, 2) as i:
        for u in range(2):
            step(i + u, u)
    for t in range(LAST, last):
        step(t, t % 2)


def tiles(eng, tile, after, before=0, at_once=4):
    for j in range(before, 8):
        tile(j, j % at_once)
    with eng.Fori(8, ST - at_once, at_once) as i:
        for u in range(at_once):
            tile(i + u, u)
    for j in range(ST - at_once, ST + after):
        tile(j, j % at_once)


def constants():
    row = np.arange(P)
    pad = np.zeros((PADS, P, ROW), np.float32)
    pad[:, :, C + 1] = TOP * TOK + np.arange(PADS * P).reshape(PADS, P)
    small = [E - np.arange(E), SLOTS * np.arange(E), P * np.arange(MAXT),
             np.tril(np.ones((E, E))).ravel(), np.arange(ST)]
    small = np.broadcast_to(np.concatenate(small).astype(np.float32), (P, 2 * E + MAXT + E * E + ST))
    parts = [np.eye(P), np.kron(np.eye(P // 4), np.full((4, 4), 0.25)), np.triu(np.ones((P, P)), 1)]
    cst = np.concatenate([a.astype(np.float32) for a in parts] + [small], axis=1)
    tok = row[:, None, None] + P * np.arange(NT)[None, None, :] + TOK * np.arange(TOP)[None, :, None]
    return cst, tok.astype(np.float32), pad

def hybrid_block(nc, x, Wv_t, Wk_t, Wq_t, bv, bk, bq, gamma, aWq_t, aWk_t, aWv_t, aWo_t, router_w, router_b,
                 w1_t, b1, wg, bg, wv, bv2, w2, b2, cst, target, pad, out):
    ctx = ExitStack()
    with ctx:
        def sb(name, shape, dt=F32):
            return ctx.enter_context(nc.sbuf_tensor(name, shape, dt))

        def ps(name, shape, dt=F32):
            return ctx.enter_context(nc.psum_tensor(name, shape, dt))

        def sem(name):
            return ctx.enter_context(nc.semaphore(name))

        X = sb("X", [P, B, N])
        T = sb("T", [P, NT, C])
        Ah = sb("Ah", [P, E, 2 * FF], F32R)
        Al = sb("Al", [P, E, 2 * FF], F32R)
        bias = sb("bias", [P, E, 2 * FF])
        w2s = sb("w2s", [P, E, FF // P, C])
        b2s = sb("b2s", [P, E, C])
        wkv = sb("wkv", [C, C + KD])
        wq = sb("wq", [C, KD])
        bkv_b = sb("bkv_b", [P, C + KD])
        bq_c = sb("bq_c", [KD, 1])
        gamma_c = sb("gamma_c", [KD, 1])
        awq = sb("awq", [C, C])
        awk = sb("awk", [C, C])
        awv = sb("awv", [C, C])
        awo = sb("awo", [P, 2, C])
        rw = sb("rw", [C, E])
        rb_b = sb("rb_b", [P, E])
        cs = sb("cs", [P, CST])
        tgt = sb("tgt", [P, 2, NT])
        idb = sb("idb", [P, P], BF16)
        tri = sb("tri", [P, P], BF16)
        ones = sb("ones", [P, P], BF16)
        neg_half = sb("neg_half", [P, B])
        gstat = sb("gstat", [P, B, 6])
        gagg = sb("gagg", [P, B, 2])
        gtmp = sb("gtmp", [P, B])
        gall = sb("gall", [P, B, 2])
        gvar = sb("gvar", [P, B])
        grstd = sb("grstd", [P, B])
        gshift = sb("gshift", [P, B])
        grstd1 = sb("grstd1", [P, B])
        xn = [sb(f"xn{p}", [P, N]) for p in range(2)]
        xs = [sb(f"xs{p}", [P, N]) for p in range(2)]
        kvT = [sb(f"kvT{p}", [P, TPB, C + KD]) for p in range(2)]
        qz = [sb(f"qz{p}", [P, N]) for p in range(2)]
        vkz = [sb(f"vkz{p}", [P, C]) for p in range(2)]
        x1 = [sb(f"x1{p}", [P, N]) for p in range(2)]
        st1 = [sb(f"st1{p}", [P, TPB, 6]) for p in range(2)]
        ag1 = [sb(f"ag1{p}", [P, TPB, 2]) for p in range(2)]
        ve1 = [sb(f"ve1{p}", [P, TPB]) for p in range(2)]
        rs1 = [sb(f"rs1{p}", [P, TPB]) for p in range(2)]
        tn1 = [sb(f"tn1{p}", [P, TPB, C]) for p in range(2)]
        xnT = [sb(f"xnT{p}", [P, N]) for p in range(2)]
        parts = [sb(f"parts{p}", [P, 3, 2 * N], BF16) for p in range(2)]
        rest = [sb(f"rest{p}", [P, 2 * N]) for p in range(2)]
        vaug = [sb(f"vaug{p}", [P, TPB, H, 32]) for p in range(2)]
        mneg = [sb(f"mneg{p}", [P, H, TPB]) for p in range(2)]
        mrest = [sb(f"mrest{p}", [P, H * TPB]) for p in range(2)]
        mparts = [sb(f"mparts{p}", [P, 3, H * TPB], BF16) for p in range(2)]
        mrow = [sb(f"mrow{p}", [3 * H * TPB, P], BF16) for p in range(2)]
        oT = [sb(f"oT{p}", [P, 16, 32]) for p in range(2)]
        rden = [sb(f"rden{p}", [P, 16]) for p in range(2)]
        onrm = [sb(f"onrm{p}", [P, 16, 32]) for p in range(2)]
        ao = [sb(f"ao{p}", [P, 2, N]) for p in range(2)]
        st2 = [sb(f"st2{p}", [P, TPB, 6]) for p in range(2)]
        ag2 = [sb(f"ag2{p}", [P, TPB, 2]) for p in range(2)]
        ve2 = [sb(f"ve2{p}", [P, TPB]) for p in range(2)]
        rs2 = [sb(f"rs2{p}", [P, TPB]) for p in range(2)]
        rows = [sb(f"rows{p}", [P, 2, TPB, ROW]) for p in range(2)]
        x2T = [sb(f"x2T{p}", [P, N]) for p in range(2)]
        lg = [sb(f"lg{p}", [P, TPB, E]) for p in range(2)]
        lmax = [sb(f"lmax{p}", [P, TPB, 1]) for p in range(2)]
        lsub = [sb(f"lsub{p}", [P, TPB, E]) for p in range(2)]
        lexp = [sb(f"lexp{p}", [P, TPB, E]) for p in range(2)]
        lsum = [sb(f"lsum{p}", [P, TPB, 1]) for p in range(2)]
        linv = [sb(f"linv{p}", [P, TPB, 1]) for p in range(2)]
        prb = [sb(f"prb{p}", [P, 2, TPB, E]) for p in range(2)]
        gates = [sb(f"gates{p}", [P, 2, TPB, 1]) for p in range(2)]
        hit = [sb(f"hit{p}", [P, 2, TPB, E]) for p in range(2)]
        best = [sb(f"best{p}", [P, 2, TPB, 1]) for p in range(2)]
        onehot = [sb(f"onehot{p}", [P, 2, TPB, E]) for p in range(2)]
        mask = [sb(f"mask{p}", [P, TPB, E], BF16) for p in range(2)]
        cum = [sb(f"cum{p}", [P, TPB, E], BF16) for p in range(2)]
        slot = [sb(f"slot{p}", [P, TPB, E]) for p in range(2)]
        pickd = [sb(f"pickd{p}", [P, 2, TPB, E]) for p in range(2)]
        dest = [sb(f"dest{p}", [P, 2, TPB], U32) for p in range(2)]
        w1s = sb("w1s", [P, FF // P, C])
        wgv = sb("wgv", [P, FF // P, 2 * FF])
        b1s = sb("b1s", [P, FF // P])
        cend = sb("cend", [P, E], BF16)
        cnt = sb("cnt", [P, E])
        cnt_i = sb("cnt_i", [P, E], I32)
        tiles_e = sb("tiles_e", [P, E])
        upto = sb("upto", [P, E, E])
        ends = sb("ends", [P, E])
        te = sb("te", [P, ST])
        tstart = sb("tstart", [P, ST])
        toff = sb("toff", [P, ST])
        toff2 = sb("toff2", [P, ST])
        table_e = sb("table_e", [P, ST], I32)
        table_b = sb("table_b", [P, ST], I32)
        qst = sb("qst", [P, RING, H * N], BF16)
        kst = sb("kst", [P, RING, H * N], BF16)
        vring = sb("vring", [P, RING, TPB * C])
        prob = sb("prob", [P, H, TPB, N])

        MX = [ps(f"MX{i}", [P, 2, N]) for i in range(2)]
        EX = [ps(f"EX{i}", [P, 2, N]) for i in range(2)]
        PV = ps("PV", [P, 2, N])
        W = [ps(f"W{i}", [P, 512]) for i in range(3)]

        scr = nc.dram_tensor("qk_parts", (B, P, 3, 2 * N), BF16, kind="Internal").ap()
        slots = nc.dram_tensor("slots", (E * SLOTS + SPARE * P, ROW), F32, kind="Internal").ap()
        res = nc.dram_tensor("res", (TOP * TOK + PADS * P, C), F32, kind="Internal").ap()
        rows2 = [r[:, 0, :, 0:C] for r in rows]
        ident = cs[:, 0:P]
        gavg = cs[:, P:2 * P]
        K0 = 3 * P
        prefer = cs[:, K0:K0 + E]
        first_slot = cs[:, K0 + E:K0 + 2 * E]
        step128 = cs[:, K0 + 2 * E:K0 + 2 * E + MAXT]
        upto_c = cs[:, K0 + 2 * E + MAXT:K0 + 2 * E + MAXT + E * E]
        tile_no = cs[:, K0 + 2 * E + MAXT + E * E:CST]

        xt = [kvT[k % 2][:, k // 2, 0:ROW] for k in range(4)]
        ttarget = sb("ttarget", [P, 8], U32)
        tgate = sb("tgate", [P, 8])
        xh = [sb(f"xh{p}", [P, P], F32R) for p in range(2)]
        xl = [sb(f"xl{p}", [P, P], F32R) for p in range(2)]
        gv = rest
        sg = xs
        gt = xn
        gT = x1
        yb = vkz
        ys = [tn1[k % 2][:, k // 2, :] for k in range(4)]
        y0 = X[:].rearrange("p b n -> p (b n)").rearrange("p (t c) -> p t c", c=C)
        spare = prob[:].rearrange("p h k n -> p (h k n)")
        past = spare[:, 0:ST * E].rearrange("p (j e) -> p j e", e=E)
        pastn = spare[:, ST * E:2 * ST * E].rearrange("p (j e) -> p j e", e=E)
        cmp_ = spare[:, 2 * ST * E:2 * ST * E + E * MAXT].rearrange("p (e j) -> p e j", e=E)
        y1 = prob[:].rearrange("p h k n -> p (h k n)").rearrange("p (t c) -> p t c", c=C)
        fin = [xnT[p] for p in range(2)]

        names = """x_ld c_ld cb_ld z_pool z_dve g_bn g_ag g_sq g_m2 g_mm g_all g_sqm g_var g_eps g_rstd g_shift idb_ok
            xn_ok xs_ok kv_mm kv_ok q_mm q_ok vk_mm vk_ok out_mm x1_ok t1_mm T_ok bn1 agg1 ve1_ok rs1_ok
            tn1_ok t2_mm xnT_ok qk_mm hi_ok rest_ok mid_ok lo_ok v_mm v_ok vaug_ok parts_st stack_ld
            mx_mm mx_ok mp0 mr0 mp1 mp2 mT_mm mT_ok mrow_ld ex_mm ex_ok pv_mm oT_ok rden_ok onrm_ok ao_ok
            wo_mm t2_ok bn2 agg2 ve2_ok rs2_ok tn2_ok t3_mm x2T_ok rt_mm lg_ok
            z_cum ones_ok w_ld fold_ld fold_mm Ah_ok Al_ok fbias_mm bias_ok route lexp_ok rank_mm copy_ok tag_ok gate_ok
            row_st cend_ok cnt_mm cnt_ok tab tab_ok pad_st slot_ld0 slot_ld1 slot_ld2 slot_ld3 xT_mm xh_ok xl_ok gv_mm gv_ok sg_ok gt_ok gT_mm
            gT_ok y_mm yb_ok ys_ok res_st0 res_st1
            res_st2 res_st3 sum0 sum1 fin_mm fin_ok out_st0 out_st1 tgate_ok ttarget_ok y_ld0 y_ld1 y_ld2 y_ld3""".split()
        s = {n: sem(n) for n in names}

        block = ctx.enter_context(nc.Block())

        @block.sync
        def _(sp):
            for g in range(4):
                sp.dma_start(X[:, 4 * g:4 * g + 4, :],
                             x[4 * g:4 * g + 4].rearrange("b c n -> c b n")).then_inc(s["x_ld"], 16)

            sp.wait_ge(s["x_ld"], 64)
            sp.dma_start(w2s[:], w2.rearrange("e (k f) c -> f e k c", f=P)).then_inc(s["w_ld"], 16)

            def load_expert(e):
                need(sp, s["fbias_mm"], e)
                sp.dma_start(w1s[:], w1_t[bass.ds(e, 1)].rearrange("o (k f) d -> f (o k) d", f=P)
                             ).then_inc(s["fold_ld"], 16)
                for n, w in enumerate((wg, wv)):
                    sp.dma_start(wgv[:, :, n * FF:(n + 1) * FF],
                                 w[bass.ds(e, 1)].rearrange("o (k f) n -> f (o k) n", f=P)
                                 ).then_inc(s["fold_ld"], 16)
                sp.dma_start(b1s[:], b1[bass.ds(e, 1)].rearrange("o f k -> (o f) k")).then_inc(s["fold_ld"], 16)

            sp.dma_start(slots[E * SLOTS:, :].rearrange("(t p) c -> t p c", p=P), pad[E:]).then_inc(s["pad_st"], 16)
            load_expert(0)
            for n, v in enumerate((bg, bv2)):
                sp.dma_start(bias[:, :, n * FF:(n + 1) * FF], v.partition_broadcast(P)).then_inc(s["w_ld"], 16)
            sp.dma_start(b2s[:], b2.partition_broadcast(P)).then_inc(s["w_ld"], 16)

            def step(t, p):
                b, q = t - 1, 1 - p
                if live(b):
                    ring = b % RING if isinstance(b, int) else sp.snap(b % RING)
                    done(sp, s["hi_ok"], b + 1)
                    done(sp, s["mid_ok"], b + 1)
                    done(sp, s["lo_ok"], b + 1)
                    sp.dma_start(scr[bass.ds(b, 1)].rearrange("o p a t -> (o p) a t"),
                                 parts[q][:]).then_inc(s["parts_st"], 16)
                    done_after(sp, (s["x_ld"], 64), (s["parts_st"], b + 1, 16),
                               (s["ex_mm"], b - RING + 1, H))
                    src = scr[bass.ds(b, 1)].rearrange("o (h d) a t -> a (o d) h t", d=HD)
                    for dst, half, order in ((kst, 1, (0, 1, 2, 0, 1, 0)), (qst, 0, (0, 0, 0, 1, 1, 2))):
                        for r, part in enumerate(order):
                            d = dst[r * HD:(r + 1) * HD, bass.ds(ring, 1), :]
                            sp.dma_start(d.rearrange("p o (h t) -> p (o h) t", h=H),
                                         src[part][:, :, half * N:(half + 1) * N]
                                         ).then_inc(s["stack_ld"], 16)
                b, q = t - 3, 1 - p
                if live(b):
                    ring = b % RING if isinstance(b, int) else sp.snap(b % RING)
                    done(sp, s["mT_ok"], b + 1)
                    for part in range(3):
                        d = qst[STACK + part:STACK + part + 1, bass.ds(ring, 1), :]
                        sp.dma_start(d.rearrange("p o (r t) -> p (o r) t", t=P),
                                     mrow[q][part * H * TPB:(part + 1) * H * TPB, :]
                                     ).then_inc(s["mrow_ld"], 16)
                if folds(t) and folds(t + 1):
                    load_expert(t + 1)

            steps(sp, step, B + 4)
            sp.wait_ge(s["cnt_ok"], 1)
            sp.wait_ge(s["c_ld"], CLD)
            for e in range(E):
                n_e = sp.value_load(cnt_i[0:1, e:e + 1], min_val=0, max_val=TOK)
                sp.dma_start(slots[bass.ds(n_e + e * SLOTS, P), :], pad[e]).then_inc(s["pad_st"], 16)

            sp.wait_ge(s["vk_mm"], B)
            sp.wait_ge(s["pad_st"], 16 * (E + 1))
            sp.wait_ge(s["row_st"], 16 * 4 * B)
            sp.wait_ge(s["tab_ok"], 2)

            def load_tile(j, r):
                need(sp, s["xT_mm"], j - 3)
                need(sp, s["tgate_ok"], j - 3)
                need(sp, s["ttarget_ok"], j - 3)
                first = sp.value_load(table_b[0:1, bass.ds(j, 1)], min_val=0, max_val=E * SLOTS + (SPARE - 1) * P)
                sp.dma_start(xt[r], slots[bass.ds(first, P), :]).then_inc(s[f"slot_ld{r}"], 16)

            tiles(sp, load_tile, 0)

            for lane in range(4):
                sp.wait_ge(s[f"res_st{lane}"], 16 * ST // 4)
            sp.wait_ge(s["xs_ok"], B)
            sp.wait_ge(s["pv_mm"], 2 * B)
            for g in range(4):
                for n, y in enumerate((y0, y1)):
                    sp.dma_start(y[:, g * (NT // 4):(g + 1) * (NT // 4), :],
                                 res[n * TOK + g * (TOK // 4):n * TOK + (g + 1) * (TOK // 4), :].rearrange(
                                     "(t p) c -> p t c", p=P)).then_inc(s[f"y_ld{g}"], 16)

            def store(b, p):
                need(sp, s["fin_ok"], b + 1)
                sp.dma_start(out[bass.ds(b, 1)].rearrange("o c n -> (o c) n"), fin[p][:]).then_inc(s[f"out_st{p}"], 16)

            with sp.Fori(0, B - 1, 2) as i:
                for u in range(2):
                    store(i + u, u)
            for p in range(2):
                sp.wait_ge(s[f"out_st{p}"], 16 * B // 2)

        @block.gpsimd
        def _(pool):
            for p in range(2):
                pool.memset(vaug[p][:], 0.0).then_inc(s["z_pool"], 1)
            pool.wait_ge(s["z_pool"], 2)
            for p in range(2):
                pool.memset(vaug[p][:, :, :, HD:HD + 1], 1.0).then_inc(s["z_pool"], 1)
            pool.memset(neg_half[:], -0.5).then_inc(s["z_pool"], 1)
            pool.wait_ge(s["z_pool"], 5)
            pool.memset(kst[STACK:P, :, :], 1.0).then_inc(s["z_pool"], 1)
            pool.wait_ge(s["z_pool"], 6)
            pool.memset(ones[:], 1.0).then_inc(s["ones_ok"], 1)
            pool.wait_ge(s["g_eps"], 1)
            pool.tensor_tensor(grstd[:], gvar[:], neg_half[:], ALU.pow).then_inc(s["g_rstd"], 1)
            met = (s["z_pool"], 6)

            def step(t, p):
                o = 1 - p
                b, q = t - 7, o
                if live(b):
                    done_after(pool, met, (s["route"], b + 1, ROUTE), (s["copy_ok"], b + 1),
                               (s["tag_ok"], b + 1), (s["gate_ok"], b + 1))
                    for n in range(2):
                        for k in range(TPB):
                            pool.indirect_dma_start(
                                out=slots, out_offset=bass.IndirectOffsetOnAxis(ap=dest[q][:, n, k:k + 1], axis=0),
                                in_=rows[q][:, n, k, :], in_offset=None).then_inc(s["row_st"], 16)
                b, q = t - 5, o
                if live(b):
                    done(pool, s["rden_ok"], b + 1)
                    done(pool, s["ao_ok"], b - 1)
                    pool.tensor_tensor(onrm[q][:], oT[q][:],
                                       rden[q][:].rearrange("p (a o) -> p a o", o=1).broadcast_to([P, 16, 32]),
                                       ALU.mult).then_inc(s["onrm_ok"], 1)
                b, q = t - 1, o
                if live(b):
                    done(pool, s["mid_ok"], b + 1)
                    done(pool, s["parts_st"], b - 1, 16)
                    pool.tensor_tensor(parts[q][:, 2, :], rest[q][:], parts[q][:, 1, :],
                                       ALU.subtract).then_inc(s["lo_ok"], 1)
                b, q = t - 5, o
                if live(b):
                    root(b, q, ve2, rs2, "ve2_ok", "rs2_ok", "tn2_ok")
                b, q = t - 3, o
                if live(b):
                    m = mneg[q][:].rearrange("p h k -> p (h k)")
                    done_after(pool, met, (s["mx_ok"], b + 1, H), (s["mT_mm"], b - 1))
                    pool.tensor_scalar(mparts[q][:, 0, :], m, 1.0, 0.0, ALU.mult, ALU.add).then_inc(s["mp0"], 1)
                    done(pool, s["mp0"], b + 1)
                    pool.tensor_tensor(mrest[q][:], m, mparts[q][:, 0, :], ALU.subtract).then_inc(s["mr0"], 1)
                    done_after(pool, met, (s["mr0"], b + 1))
                    pool.tensor_scalar(mparts[q][:, 1, :], mrest[q][:], 1.0, 0.0, ALU.mult,
                                       ALU.add).then_inc(s["mp1"], 1)
                    done(pool, s["mp1"], b + 1)
                    pool.tensor_tensor(mparts[q][:, 2, :], mrest[q][:], mparts[q][:, 1, :],
                                       ALU.subtract).then_inc(s["mp2"], 1)
                b, q = t, p
                if live(b):
                    root(b, q, ve1, rs1, "ve1_ok", "rs1_ok", "tn1_ok")

            def root(b, q, ve, rs, ve_ok, rs_ok, used):
                done(pool, s[used], b - 1, TPB)
                done(pool, s[ve_ok], b + 1)
                pool.tensor_tensor(rs[q][:], ve[q][:], neg_half[:, 0:TPB], ALU.pow).then_inc(s[rs_ok], 1)

            steps(pool, step, B + 7)

            def scatter(j, r):
                i, q = j, r
                if within(i):
                    need_after(pool, met, (s["ys_ok"], i + 1), (s["ttarget_ok"], i + 1))
                    pool.indirect_dma_start(
                        out=res, out_offset=bass.IndirectOffsetOnAxis(ap=ttarget[:, q:q + 1], axis=0),
                        in_=ys[q % 4], in_offset=None).then_inc(s[f"res_st{q % 4}"], 16)
                i, q = j + 4, (r + 4) % 8
                if within(i):
                    need_after(pool, met, (s[f"slot_ld{q % 4}"], in_lane(i, q % 4)))
                    pool.tensor_scalar(ttarget[:, q:q + 1], xt[q % 4][:, C + 1:C + 2], 1.0, 0.0, ALU.mult,
                                       ALU.add).then_inc(s["ttarget_ok"], 1)

            tiles(pool, scatter, 0, -4, 8)

        @block.scalar
        def _(act):
            loads = [(cs[:], cst), (wkv[:, 0:C], Wv_t), (wkv[:, C:], Wk_t), (wq[:], Wq_t),
                     (bkv_b[:, 0:C], bv.partition_broadcast(P)), (bkv_b[:, C:], bk.partition_broadcast(P)),
                     (bq_c[:], bq.rearrange("(d o) -> d o", o=1)), (gamma_c[:], gamma.partition_broadcast(KD)),
                     (awq[:], aWq_t), (awk[:], aWk_t), (awv[:], aWv_t), (rw[:], router_w),
                     (rb_b[:], router_b.partition_broadcast(P)), (tgt[:], target)]
            act.wait_ge(s["z_dve"], 5)
            for h in range(H):
                loads.append((awo[32 * (h % 4):32 * (h % 4) + HD, h // 4, :], aWo_t[h * HD:(h + 1) * HD, :]))
            for d, src in loads:
                act.dma_start(d, src).then_inc(s["c_ld"], 16)

            def head_exp(b, h):
                done(act, s["ex_mm"], b, H, h + 1)
                done(act, s["pv_mm"], b - 1, 2, h // 4 + 1)
                act.activation(prob[:, h, :, :], EX[h % 2][:], ACT.Exp, scale=SCALE).then_inc(s["ex_ok"], 1)

            def norm_x(b, p):
                done(act, s["q_mm"], b - 1)
                act.activation(xn[p][:], pick(X, b), ACT.Identity, scale=grstd[:, bass.ds(b, 1)],
                               bias=gshift[:, bass.ds(b, 1)]).then_inc(s["xn_ok"], 1)
                done(act, s["x1_ok"], b - 1)
                act.activation(xs[p][:], pick(X, b), ACT.Identity, scale=grstd1[:, bass.ds(b, 1)],
                               bias=gshift[:, bass.ds(b, 1)]).then_inc(s["xs_ok"], 1)

            def step(t, p):
                o = 1 - p
                if live(t):
                    norm_x(t, p)
                b, q = t - 1, o
                if live(b):
                    done(act, s["t2_mm"], b + 1)
                    done(act, s["v_mm"], b - 1)
                    act.copy(xnT[q][:], W[0][:, 0:N]).then_inc(s["xnT_ok"], 1)
                b, q = t, p
                if live(b):
                    done(act, s["q_mm"], b + 1)
                    done(act, s["out_mm"], b - 1)
                    act.activation(qz[q][0:KD, :], W[2][0:KD, 0:N], ACT.Identity,
                                   bias=bq_c[:]).then_inc(s["q_ok"], 1)
                if live(t - 4):
                    head_exp(t - 4, 0)
                b, q = t - 6, p
                if live(b):
                    done(act, s["route"], b, ROUTE, 2)
                    act.activation(lexp[q][:], lsub[q][:], ACT.Exp).then_inc(s["lexp_ok"], 1)
                b, q = t - 1, o
                if live(b):
                    done(act, s["qk_mm"], b + 1)
                    done(act, s["parts_st"], b - 1, 16)
                    act.copy(parts[q][:, 0, :], W[0][:]).then_inc(s["hi_ok"], 1)
                if live(t - 4):
                    head_exp(t - 4, 1)
                b, q = t, p
                if live(b):
                    done(act, s["vk_mm"], b + 1)
                    done(act, s["out_mm"], b - 1)
                    act.activation(vkz[q][0:KD, :], W[1][0:KD, 0:C], ACT.Copy,
                                   scale=gamma_c[:]).then_inc(s["vk_ok"], 1)
                b, q = t - 1, o
                if live(b):
                    done(act, s["rest_ok"], b + 1)
                    act.copy(parts[q][:, 1, :], rest[q][:]).then_inc(s["mid_ok"], 1)
                if live(t - 4):
                    head_exp(t - 4, 2)
                b, q = t - 4, p
                if live(b):
                    done(act, s["v_ok"], b + 1)
                    done(act, s["pv_mm"], b - 1, 2)
                    act.copy(vaug[q][:, :, :, 0:HD].rearrange("p k h d -> p (k h) d"),
                             pick(vring, b % RING).rearrange("p (r d) -> p r d", d=HD)
                             ).then_inc(s["vaug_ok"], 1)
                b, q = t - 1, o
                if live(b):
                    done(act, s["v_mm"], b + 1)
                    done(act, s["vaug_ok"], b - RING + 1)
                    act.copy(pick(vring, b % RING), W[2][:, 0:N]).then_inc(s["v_ok"], 1)
                if live(t - 4):
                    head_exp(t - 4, 3)
                    head_exp(t - 4, 4)
                b, q = t, p
                if live(b):
                    done(act, s["t1_mm"], b + 1)
                    act.copy(pick(T, TPB * b, TPB), W[2][:, 0:N]).then_inc(s["T_ok"], 1)
                if live(t - 4):
                    head_exp(t - 4, 5)
                if folds(t):
                    need(act, s["fold_mm"], t + 1)
                    act.copy(pick(Ah, t), W[1][:]).then_inc(s["Ah_ok"], 1)
                if live(t - 4):
                    head_exp(t - 4, 6)
                b, q = t - 5, o
                if live(b):
                    done(act, s["t3_mm"], b + 1)
                    done(act, s["rt_mm"], b - 1)
                    act.copy(x2T[q][:], W[0][:, 0:N]).then_inc(s["x2T_ok"], 1)
                    act.copy(rows[q][:, 1, :, 0:C], rows[q][:, 0, :, 0:C]).then_inc(s["copy_ok"], 1)
                    act.copy(rows[q][:, :, :, C + 1], tgt[:, :, bass.ds(TPB * b, TPB)]).then_inc(s["tag_ok"], 1)
                if live(t - 4):
                    head_exp(t - 4, 7)
                b, q = t - 3, o
                if live(b):
                    done(act, s["mT_mm"], b + 1)
                    done(act, s["mrow_ld"], b - 1, 48)
                    act.copy(mrow[q][:], W[2][0:3 * H * TPB, 0:P // 2].bitcast(BF16)).then_inc(s["mT_ok"], 1)

            assert CLD == 16 * len(loads)
            act.wait_ge(s["c_ld"], CLD)
            act.wait_ge(s["g_shift"], 2)
            steps(act, step, B + 6)

            def tile(j, r):
                p = r % 2
                i, q = j + 1, 1 - p
                if within(i):
                    need(act, s["xT_mm"], i + 1)
                    need(act, s["gv_mm"], i - 1)
                    act.copy(xh[q][:], MX[q][:, 0, 0:P]).then_inc(s["xh_ok"], 1)
                    act.copy(tgate[:, bass.ds(i % 8, 1)], xt[(r + 1) % 4][:, C:C + 1]).then_inc(s["tgate_ok"], 1)
                i, q = j, p
                if within(i):
                    need(act, s["gv_ok"], i + 1)
                    need(act, s["gt_ok"], i - 1)
                    act.activation(sg[q][:], gv[q][:, 0:FF], ACT.Silu).then_inc(s["sg_ok"], 1)
                i, q = j - 2, p
                if within(i):
                    need(act, s["gT_mm"], i + 1)
                    need(act, s["y_mm"], i - 1)
                    act.copy(gT[q][:], (PV[:, 0, :], W[0][:, 0:FF])[q]).then_inc(s["gT_ok"], 1)
                i, q = j - 3, (r + 1) % 4
                if within(i):
                    need(act, s["yb_ok"], i + 1)
                    if not isinstance(i, int) or i >= 4:
                        act.wait_ge(s[f"res_st{q}"], in_lane(i - 4, q))
                    act.activation(ys[q], yb[q % 2][:], ACT.Copy, scale=tgate[:, bass.ds(i % 8, 1)]).then_inc(s["ys_ok"], 1)

            tiles(act, tile, 3, -1)

            def finish(b, p):
                need(act, s["fin_mm"], b + 1)
                if not isinstance(b, int) or b >= 2:
                    act.wait_ge(s[f"out_st{p}"], in_lane(b - 2, p, 2))
                act.copy(fin[p][:], MX[p][:, 0, :]).then_inc(s["fin_ok"], 1)

            for b in range(2):
                finish(b, b)
            with act.Fori(2, B - 1, 2) as i:
                for u in range(2):
                    finish(i + u, u)

        @block.vector
        def _(dve):
            for z in (awo, qz[0], qz[1], vkz[0], vkz[1]):
                dve.memset(z[:], 0.0).then_inc(s["z_dve"], 1)
            for z in (cum[1], mask[1]):
                dve.memset(z[:], 0.0).then_inc(s["z_cum"], 1)
            for b in range(B):
                if b == 0:
                    dve.wait_ge(s["x_ld"], 64)
                dve.bn_stats(gstat[:, b, :], X[:, b, :]).then_inc(s["g_bn"], 1)
            dve.wait_ge(s["g_bn"], B)
            for b in range(B):
                dve.bn_aggr(gagg[:, b, :], gstat[:, b, :]).then_inc(s["g_ag"], 1)
            dve.wait_ge(s["g_ag"], B)
            dve.tensor_tensor(gtmp[:], gagg[:, :, 0], gagg[:, :, 0], ALU.mult).then_inc(s["g_sq"], 1)
            dve.wait_ge(s["g_sq"], 1)
            dve.tensor_tensor(gagg[:, :, 1], gagg[:, :, 1], gtmp[:], ALU.add).then_inc(s["g_m2"], 1)
            dve.wait_ge(s["g_mm"], 1)
            dve.tensor_copy(gall[:].rearrange("p b k -> p (b k)"), W[0][:, 0:2 * B]).then_inc(s["g_all"], 1)
            dve.wait_ge(s["g_all"], 1)
            dve.tensor_tensor(gtmp[:], gall[:, :, 0], gall[:, :, 0], ALU.mult).then_inc(s["g_sqm"], 1)
            dve.wait_ge(s["g_sqm"], 1)
            dve.tensor_tensor(gvar[:], gall[:, :, 1], gtmp[:], ALU.subtract).then_inc(s["g_var"], 1)
            dve.wait_ge(s["g_var"], 1)
            dve.tensor_scalar(gvar[:], gvar[:], GN_EPS, None, ALU.add).then_inc(s["g_eps"], 1)
            dve.wait_ge(s["g_rstd"], 1)
            dve.scalar_tensor_tensor(gshift[:], gall[:, :, 0], -1.0, grstd[:], ALU.mult,
                                     ALU.mult).then_inc(s["g_shift"], 1)
            dve.tensor_scalar(grstd1[:], grstd[:], 1.0, None, ALU.add).then_inc(s["g_shift"], 1)
            dve.wait_ge(s["c_ld"], CLD)
            dve.tensor_copy(idb[:], ident).then_inc(s["idb_ok"], 1)
            dve.tensor_copy(tri[:], cs[:, 2 * P:3 * P]).then_inc(s["idb_ok"], 1)
            dve.wait_ge(s["z_cum"], 2)

            def over(v, n):
                return v.broadcast_to([P, v.shape[1], n])

            def along(v, k):
                return v.rearrange("p (o n) -> p o n", o=1).broadcast_to([P, k, v.shape[1]])

            def router(b, q):
                n = [0]

                def did(ins):
                    n[0] += 1
                    ins.then_inc(s["route"], 1)

                def wait():
                    done(dve, s["route"], b, ROUTE, n[0])

                done(dve, s["row_st"], b - 1, 64)
                did(dve.tensor_reduce(lmax[q][:], lg[q][:], AX.X, ALU.max))
                wait()
                did(dve.tensor_tensor(lsub[q][:], lg[q][:], over(lmax[q][:], E), ALU.subtract))
                yield
                done(dve, s["lexp_ok"], b + 1)
                did(dve.tensor_reduce(lsum[q][:], lexp[q][:], AX.X, ALU.add))
                wait()
                did(dve.reciprocal(linv[q][:], lsum[q][:]))
                wait()
                did(dve.tensor_tensor(prb[q][:, 0], lexp[q][:], over(linv[q][:], E), ALU.mult))
                for c in range(2):
                    wait()
                    if c == 1:
                        did(dve.scalar_tensor_tensor(prb[q][:, 1], onehot[q][:, 0], -2.0, prb[q][:, 0],
                                                     ALU.mult, ALU.add))
                        wait()
                    did(dve.tensor_reduce(gates[q][:, c], prb[q][:, c], AX.X, ALU.max))
                    yield
                    wait()
                    did(dve.tensor_tensor(hit[q][:, c], prb[q][:, c], over(gates[q][:, c], E), ALU.is_equal))
                    wait()
                    did(dve.tensor_tensor(pickd[q][:, c], hit[q][:, c], along(prefer, TPB), ALU.mult))
                    wait()
                    did(dve.tensor_reduce(best[q][:, c], pickd[q][:, c], AX.X, ALU.max))
                    yield
                    wait()
                    did(dve.tensor_tensor(onehot[q][:, c], pickd[q][:, c], over(best[q][:, c], E), ALU.is_equal))
                wait()
                did(dve.tensor_tensor(mask[q][:], onehot[q][:, 0], onehot[q][:, 1], ALU.add))
                did(dve.tensor_tensor(cum[q][:, 0], cum[1 - q][:, 1], mask[1 - q][:, 1], ALU.add))
                wait()
                did(dve.tensor_tensor(cum[q][:, 1], cum[q][:, 0], mask[q][:, 0], ALU.add))
                done(dve, s["copy_ok"], b + 1)
                dve.tensor_copy(rows[q][:, :, :, C], gates[q][:].rearrange("p c k o -> p c (k o)")
                                ).then_inc(s["gate_ok"], 1)
                yield
                done(dve, s["rank_mm"], b + 1)
                did(dve.tensor_tensor(slot[q][:], W[2][:, 0:TPB * E].rearrange("p (k e) -> p k e", k=TPB),
                                      along(first_slot, TPB), ALU.add))
                wait()
                for c in range(2):
                    did(dve.tensor_tensor(pickd[q][:, c], onehot[q][:, c], slot[q][:], ALU.mult))
                wait()
                with nc.allow_low_precision(reason="slots are whole numbers, summed in float32"):
                    did(dve.tensor_reduce(dest[q][:].rearrange("p c k -> p (c k)"),
                                          pickd[q][:].rearrange("p c k e -> p (c k) e"), AX.X, ALU.add))
                assert n[0] == ROUTE
                yield

            met = (s["x_ld"], 64)

            def row_max(b, p, c):
                k, pair = c // 4, c % 4
                done(dve, s["mx_mm"], b, H, c + 1)
                if c == 0:
                    done(dve, s["mp2"], b - 1)
                dve.tensor_reduce(mneg[p][:, 2 * pair:2 * pair + 2, k], MX[c % 2][:], AX.X, ALU.max,
                                  negate=True).then_inc(s["mx_ok"], 1)

            def stats(b, q, st, ag, ve, ready, bn, agg, ve_ok, used):
                done_after(dve, met, (s[ready], b + 1))
                for k in range(TPB):
                    dve.bn_stats(st[q][:, k, :], pick(T, TPB * b + k)).then_inc(s[bn], 1)
                for k in range(TPB):
                    done_after(dve, met, (s[used], b - 1, TPB), (s[bn], b, TPB, k + 1))
                    dve.bn_aggr(ag[q][:, k, :], st[q][:, k, :]).then_inc(s[agg], 1)
                done(dve, s[agg], b + 1, TPB)
                dve.tensor_scalar(ve[q][:], ag[q][:, :, 1], LN_EPS, None, ALU.add).then_inc(s[ve_ok], 1)

            def layer_norm(b, q, rs, tn, ag, rs_ok, tn_ok, used):
                done(dve, s[rs_ok], b + 1)
                done(dve, s[used], b - 1)
                for k in range(TPB):
                    dve.tensor_scalar(tn[:, k, :], pick(T, TPB * b + k), ag[q][:, k, 0:1],
                                      rs[q][:, k:k + 1], ALU.subtract, ALU.mult).then_inc(s[tn_ok], 1)

            def step(t, p):
                o = 1 - p
                if live(t - 1):
                    layer_norm(t - 1, o, rs1, tn1[o], ag1, "rs1_ok", "tn1_ok", "t2_mm")
                b, q = t - 5, o
                if live(b):
                    done(dve, s["pv_mm"], b + 1, 2)
                    done(dve, s["onrm_ok"], b - 1)
                    dve.transpose(oT[q][:].rearrange("p a r -> p (a r)"),
                                  PV[:].rearrange("p a n -> p (a n)")).then_inc(s["oT_ok"], 1)
                    done(dve, s["oT_ok"], b + 1)
                    dve.reciprocal(rden[q][:], oT[q][:, :, HD]).then_inc(s["rden_ok"], 1)
                b, q = t - 6, p
                if live(b):
                    done(dve, s["rt_mm"], b + 1)
                    dve.tensor_tensor(lg[q][:], W[1][:, 0:TPB * E].rearrange("p (k e) -> p k e", k=TPB),
                                      along(rb_b[:], TPB), ALU.add).then_inc(s["lg_ok"], 1)
                    done(dve, s["lg_ok"], b + 1)
                    route = router(b, q)
                else:
                    route = iter(())
                m = live(t - 3)
                next(route, None)
                if m:
                    row_max(t - 3, o, 0)
                    row_max(t - 3, o, 1)
                b, q = t, p
                if live(b):
                    done(dve, s["kv_mm"], b + 1)
                    done(dve, s["vk_mm"], b - 1)
                    dve.tensor_tensor(kvT[q][:], W[1][:, 0:TPB * (C + KD)].rearrange("p (k n) -> p k n", k=TPB),
                                      bkv_b[:].rearrange("p (o n) -> p o n", o=1).broadcast_to([P, TPB, C + KD]),
                                      ALU.add).then_inc(s["kv_ok"], 1)
                next(route, None)
                if m:
                    row_max(t - 3, o, 2)
                b, q = t - 1, o
                if live(b):
                    done(dve, s["hi_ok"], b + 1)
                    done(dve, s["lo_ok"], b - 1)
                    dve.tensor_tensor(rest[q][:], W[0][:], parts[q][:, 0, :], ALU.subtract).then_inc(s["rest_ok"], 1)
                next(route, None)
                if m:
                    row_max(t - 3, o, 3)
                b, q = t - 5, o
                if live(b):
                    done(dve, s["onrm_ok"], b + 1)
                    done(dve, s["wo_mm"], b - 1)
                    dve.transpose(ao[q][:].rearrange("p a n -> p (a n)"),
                                  onrm[q][:].rearrange("p a r -> p (a r)")).then_inc(s["ao_ok"], 1)
                next(route, None)
                if m:
                    row_max(t - 3, o, 4)
                b, q = t - 5, o
                if live(b):
                    done(dve, s["wo_mm"], b + 1)
                    dve.tensor_tensor(pick(T, TPB * b, TPB), pick(T, TPB * b, TPB), W[0][:, 0:N],
                                      ALU.add).then_inc(s["t2_ok"], 1)
                next(route, None)
                if m:
                    row_max(t - 3, o, 5)
                b, q = t, p
                if live(b):
                    done(dve, s["out_mm"], b + 1)
                    done(dve, s["xs_ok"], b + 1)
                    done(dve, s["t1_mm"], b - 1)
                    dve.tensor_tensor(x1[q][:], W[1][:, 0:N], xs[q][:], ALU.add).then_inc(s["x1_ok"], 1)
                b, q = t - 5, o
                if live(b):
                    stats(b, q, st2, ag2, ve2, "t2_ok", "bn2", "agg2", "ve2_ok", "tn2_ok")
                next(route, None)
                if m:
                    row_max(t - 3, o, 6)
                    row_max(t - 3, o, 7)
                b, q = t - 5, o
                if live(b):
                    done(dve, s["row_st"], b - 1, 64)
                    done(dve, s["copy_ok"], b - 1)
                    layer_norm(b, q, rs2, rows2[q], ag2, "rs2_ok", "tn2_ok", "t3_mm")
                if folds(t):
                    need(dve, s["Ah_ok"], t + 1)
                    dve.tensor_tensor(pick(Al, t), W[1][:], pick(Ah, t).bitcast(F32),
                                      ALU.subtract).then_inc(s["Al_ok"], 1)
                b, q = t, p
                if live(b):
                    stats(b, q, st1, ag1, ve1, "T_ok", "bn1", "agg1", "ve1_ok", "tn1_ok")
                for _ in route:
                    pass
                if folds(t):
                    need(dve, s["fbias_mm"], t + 1)
                    dve.tensor_tensor(pick(bias, t), W[0][:], pick(bias, t),
                                      ALU.add).then_inc(s["bias_ok"], 1)

            dve.wait_ge(s["w_ld"], 64)
            steps(dve, step, B + 6)

            n_tab = [0]

            def tab(ins):
                n_tab[0] += 1
                ins.then_inc(s["tab"], 1)
                dve.wait_ge(s["tab"], n_tab[0])

            dve.tensor_tensor(cend[:], cum[1][:, 1], mask[1][:, 1], ALU.add).then_inc(s["cend_ok"], 1)
            dve.wait_ge(s["cnt_mm"], 1)
            dve.wait_ge(s["pv_mm"], 2 * B)
            tab(dve.tensor_copy(cnt[:], W[0][:, 0:E]))
            dve.tensor_copy(cnt_i[:], cnt[:]).then_inc(s["cnt_ok"], 1)
            tab(dve.tensor_tensor(cmp_, cnt[:].rearrange("p (e o) -> p e o", o=1).broadcast_to([P, E, MAXT]),
                                  along(step128, E), ALU.is_gt))
            tab(dve.tensor_reduce(tiles_e[:], cmp_, AX.X, ALU.add))
            tab(dve.tensor_tensor(upto[:], along(tiles_e[:], E), upto_c.rearrange("p (a b) -> p a b", a=E),
                                  ALU.mult))
            tab(dve.tensor_reduce(ends[:], upto[:], AX.X, ALU.add))
            tab(dve.tensor_tensor(past, tile_no.rearrange("p (j o) -> p j o", o=1).broadcast_to([P, ST, E]),
                                  along(ends[:], ST), ALU.is_ge))
            tab(dve.tensor_reduce(te[:], past, AX.X, ALU.add))
            tab(dve.tensor_tensor(pastn, past, along(tiles_e[:], ST), ALU.mult))
            tab(dve.tensor_reduce(tstart[:], pastn, AX.X, ALU.add))
            tab(dve.tensor_tensor(toff[:], tile_no, tstart[:], ALU.subtract))
            tab(dve.tensor_scalar(toff2[:], toff[:], float(P), None, ALU.mult))
            dve.scalar_tensor_tensor(table_b[:], te[:], float(SLOTS), toff2[:], ALU.mult,
                                     ALU.add).then_inc(s["tab_ok"], 1)
            dve.tensor_scalar(table_e[:], te[:], float(E - 1), None, ALU.min).then_inc(s["tab_ok"], 1)
            dve.wait_ge(s["tab_ok"], 2)

            def tile(j, r):
                p = r % 2
                i, q = j, p
                if within(i):
                    e = dve.value_load(table_e[0:1, bass.ds(i, 1)], min_val=0, max_val=E - 1)
                    need(dve, s["gv_mm"], i + 1)
                    need(dve, s["gt_ok"], i - 1)
                    need(dve, s["sg_ok"], i - 1)
                    dve.tensor_tensor(gv[q][:], EX[q][:].rearrange("p a n -> p (a n)"), pick(bias, e),
                                      ALU.add).then_inc(s["gv_ok"], 1)
                i, q = j + 1, 1 - p
                if within(i):
                    need(dve, s["xh_ok"], i + 1)
                    need(dve, s["gv_mm"], i - 1)
                    dve.tensor_tensor(xl[q][:], MX[q][:, 0, 0:P], xh[q][:].bitcast(F32),
                                      ALU.subtract).then_inc(s["xl_ok"], 1)
                i, q = j, p
                if within(i):
                    need(dve, s["sg_ok"], i + 1)
                    need(dve, s["gT_mm"], i - 1)
                    dve.tensor_tensor(gt[q][:], sg[q][:], gv[q][:, FF:], ALU.mult).then_inc(s["gt_ok"], 1)
                i, q = j - 3, 1 - p
                if within(i):
                    e = dve.value_load(table_e[0:1, bass.ds(i, 1)], min_val=0, max_val=E - 1)
                    need(dve, s["y_mm"], i + 1)
                    need(dve, s["ys_ok"], i - 1)
                    dve.tensor_tensor(yb[q][:], W[1 + q][:, 0:C], pick(b2s, e), ALU.add).then_inc(s["yb_ok"], 1)

            tiles(dve, tile, 3, -1)

            for g in range(8):
                if g % 2 == 0:
                    dve.wait_ge(s[f"y_ld{g // 2}"], 32)
                v = slice(g * (NT // 8), (g + 1) * (NT // 8))
                dve.tensor_tensor(y0[:, v, :], y0[:, v, :], y1[:, v, :], ALU.add).then_inc(s["sum0"], 1)
                dve.wait_ge(s["sum0"], g + 1)
                dve.tensor_tensor(y0[:, v, :], y0[:, v, :], T[:, v, :], ALU.add).then_inc(s["sum1"], 1)

        @block.tensor
        def _(pe):
            pe.wait_ge(s["c_ld"], CLD)
            pe.wait_ge(s["g_m2"], 1)
            pe.matmul(W[0][:, 0:2 * B], gavg, gagg[:].rearrange("p b k -> p (b k)"),
                      start=True, stop=True).then_inc(s["g_mm"], 1)
            pe.wait_ge(s["g_all"], 1)
            pe.wait_ge(s["z_pool"], 6)
            pe.wait_ge(s["z_dve"], 5)
            pe.wait_ge(s["idb_ok"], 2)
            pe.wait_ge(s["ones_ok"], 1)

            def stack(t, b, h, lo=0, n=N, rows=STACK):
                v = t[0:rows, bass.ds(b % RING, 1), h * N + lo:h * N + lo + n]
                return v.rearrange("p o n -> p (o n)")

            def max_scores(b, c):
                k, pair = c // 4, c % 4
                if c == 0:
                    done(pe, s["stack_ld"], b + 1, 16 * LOADS)
                done(pe, s["mx_ok"], b, H, c - 1)
                for u in range(2):
                    h = 2 * pair + u
                    mm = pe.matmul(MX[c % 2][:, u, :], stack(qst, b, h, k * P, P), stack(kst, b, h),
                                   start=True, stop=True)
                mm.then_inc(s["mx_mm"], 1)

            def exp_scores(b, h):
                if h == 0:
                    done(pe, s["mrow_ld"], b + 1, 48)
                done(pe, s["ex_ok"], b, H, h - 1)
                for k in range(TPB):
                    mm = pe.matmul(EX[h % 2][:, k, :], stack(kst, b, h, k * P, P, QROWS),
                                   stack(qst, b, h, rows=QROWS), start=True, stop=True)
                mm.then_inc(s["ex_mm"], 1)

            def weigh(b, q, g):
                if g == 0:
                    done(pe, s["vaug_ok"], b + 1)
                    done(pe, s["oT_ok"], b)
                done(pe, s["ex_ok"], b, H, 4 * g + 4)
                for k in range(TPB):
                    for j in range(4):
                        mm = pe.matmul(PV[32 * j:32 * j + 32, g, :], vaug[q][:, k, 4 * g + j, :],
                                       prob[:, 4 * g + j, k, :], start=(k == 0), stop=(k == TPB - 1))
                mm.then_inc(s["pv_mm"], 1)

            def folded(ok, t):
                need(pe, ok, t if isinstance(t, int) else E, cap=E)

            def step(t, p):
                o = 1 - p
                m, e = live(t - 3), live(t - 4)
                b, q = t - 6, p
                if live(b):
                    done(pe, s["x2T_ok"], b + 1)
                    done(pe, s["x1_ok"], t)
                    folded(s["Al_ok"], t)
                    for k in range(TPB):
                        mm = pe.matmul(W[1][:, k * E:(k + 1) * E], x2T[q][:, k * P:(k + 1) * P], rw[:],
                                       start=True, stop=True)
                    mm.then_inc(s["rt_mm"], 1)
                if m:
                    max_scores(t - 3, 0)
                b, q = t - 1, o
                if live(b):
                    done(pe, s["tn1_ok"], b + 1, TPB)
                    done(pe, s["x2T_ok"], t - 5)
                    folded(s["bias_ok"], t)
                    for k in range(TPB):
                        mm = pe.transpose(W[0][:, k * P:(k + 1) * P], tn1[q][:, k, :], ident)
                    mm.then_inc(s["t2_mm"], 1)
                if m:
                    max_scores(t - 3, 1)
                b, q = t, p
                if live(b):
                    done(pe, s["xn_ok"], b + 1)
                    done(pe, s["lg_ok"], t - 5)
                    folded(s["Al_ok"], t)
                    for k in range(TPB):
                        mm = pe.matmul(W[1][:, k * (C + KD):(k + 1) * (C + KD)], xn[q][:, k * P:(k + 1) * P],
                                       wkv[:], start=True, stop=True)
                    mm.then_inc(s["kv_mm"], 1)
                    done(pe, s["mT_ok"], t - 3)
                    pe.matmul(W[2][0:KD, 0:N], wq[:], xn[q][:], start=True, stop=True).then_inc(s["q_mm"], 1)
                if e:
                    exp_scores(t - 4, 0)
                if m:
                    max_scores(t - 3, 2)
                b, q = t - 1, o
                if live(b):
                    done(pe, s["xnT_ok"], b + 1)
                    pe.matmul(W[0][:, 0:N], awq[:], xnT[q][:], start=True, stop=True)
                    pe.matmul(W[0][:, N:2 * N], awk[:], xnT[q][:], start=True, stop=True).then_inc(s["qk_mm"], 1)
                if e:
                    exp_scores(t - 4, 1)
                if m:
                    max_scores(t - 3, 3)
                b, q = t, p
                if live(b):
                    done(pe, s["kv_ok"], b + 1)
                    for k in range(TPB):
                        mm = pe.matmul(W[1][0:KD, 0:C], kvT[q][:, k, C:C + KD], kvT[q][:, k, 0:C],
                                       start=(k == 0), stop=(k == TPB - 1))
                    mm.then_inc(s["vk_mm"], 1)
                if e:
                    exp_scores(t - 4, 2)
                if m:
                    max_scores(t - 3, 4)
                b, q = t - 1, o
                if live(b):
                    done(pe, s["q_ok"], t + 1)
                    for k in range(TPB):
                        mm = pe.matmul(W[2][:, k * C:(k + 1) * C], xnT[q][:, k * P:(k + 1) * P], awv[:],
                                       start=True, stop=True)
                    mm.then_inc(s["v_mm"], 1)
                if e:
                    exp_scores(t - 4, 3)
                if m:
                    max_scores(t - 3, 5)
                b, q = t - 5, o
                if live(b):
                    done(pe, s["ao_ok"], b + 1)
                    done(pe, s["rest_ok"], t)
                    for k in range(TPB):
                        for g in range(2):
                            mm = pe.matmul(W[0][:, k * C:(k + 1) * C], ao[q][:, g, k * P:(k + 1) * P],
                                           awo[:, g, :], start=(g == 0), stop=(g == 1))
                    mm.then_inc(s["wo_mm"], 1)
                b, q = t, p
                if live(b):
                    done(pe, s["vk_ok"], b + 1)
                    done(pe, s["q_ok"], b + 1)
                    pe.matmul(W[1][:, 0:N], vkz[q][:], qz[q][:], start=True, stop=True).then_inc(s["out_mm"], 1)
                if e:
                    exp_scores(t - 4, 4)
                if m:
                    max_scores(t - 3, 6)
                b, q = t, p
                if live(b):
                    done(pe, s["x1_ok"], b + 1)
                    done(pe, s["v_ok"], t)
                    for k in range(TPB):
                        mm = pe.transpose(W[2][:, k * P:(k + 1) * P], x1[q][:, k * P:(k + 1) * P], ident)
                    mm.then_inc(s["t1_mm"], 1)
                if e:
                    exp_scores(t - 4, 5)
                if folds(t):
                    pe.wait_ge(s["fold_ld"], (t + 1) * 64)
                    done(pe, s["x1_ok"], t + 1)
                    for k in range(FF // P):
                        mm = pe.matmul(W[1][:], w1s[:, k, :], wgv[:, k, :], start=(k == 0), stop=(k == FF // P - 1))
                    mm.then_inc(s["fold_mm"], 1)
                if m:
                    max_scores(t - 3, 7)
                if e:
                    weigh(t - 4, p, 0)
                    exp_scores(t - 4, 6)
                b, q = t - 5, o
                if live(b):
                    done(pe, s["tn2_ok"], b + 1, TPB)
                    done(pe, s["t2_ok"], b + 1)
                    for k in range(TPB):
                        mm = pe.transpose(W[0][:, k * P:(k + 1) * P], rows2[q][:, k, :], ident)
                    mm.then_inc(s["t3_mm"], 1)
                if e:
                    exp_scores(t - 4, 7)
                    weigh(t - 4, p, 1)
                b, q = t - 6, p
                if live(b):
                    done(pe, s["route"], b, ROUTE, ROUTE - 4)
                    done(pe, s["T_ok"], t + 1)
                    pe.matmul(W[2][:, 0:TPB * E], tri[:], mask[q][:].rearrange("p k e -> p (k e)"),
                              start=True, stop=False)
                    pe.matmul(W[2][:, 0:TPB * E], ones[:], cum[q][:].rearrange("p k e -> p (k e)"),
                              start=False, stop=True).then_inc(s["rank_mm"], 1)
                if folds(t):
                    done(pe, s["x2T_ok"], t - 4)
                    if t < 5:
                        done(pe, s["rest_ok"], t)
                    for k in range(FF // P):
                        mm = pe.matmul(W[0][:], b1s[:, k:k + 1].broadcast_to([P, P]), wgv[:, k, :],
                                       start=(k == 0), stop=(k == FF // P - 1))
                    mm.then_inc(s["fbias_mm"], 1)
                b, q = t - 3, o
                if m:
                    done_after(pe, (s["c_ld"], CLD), (s["mp2"], b + 1), (s["T_ok"], t + 1),
                               *[(s["route"], t - 6, ROUTE, ROUTE - 3)] * live(t - 6))
                    pe.transpose(W[2][0:3 * H * TPB, 0:P // 2].bitcast(BF16),
                                 mparts[q][:].rearrange("p a r -> p (a r)"), idb[:]).then_inc(s["mT_mm"], 1)

            steps(pe, step, B + 7)

            pe.wait_ge(s["cend_ok"], 1)
            pe.wait_ge(s["x2T_ok"], B)
            pe.matmul(W[0][:, 0:E], ones[:], cend[:], start=True, stop=True).then_inc(s["cnt_mm"], 1)
            pe.wait_ge(s["tab_ok"], 2)
            pe.wait_ge(s["w_ld"], 64)

            def tile(j, r):
                p = r % 2
                i, q = j, p
                if within(i):
                    e = pe.value_load(table_e[0:1, bass.ds(i, 1)], min_val=0, max_val=E - 1)
                    need(pe, s["xl_ok"], i + 1)
                    need(pe, s["gv_ok"], i - 1)
                    o = EX[q][:].rearrange("p a n -> p (a n)")
                    pe.matmul(o, xh[q][:], pick(Ah, e), start=True, stop=False)
                    pe.matmul(o, xh[q][:], pick(Al, e), start=False, stop=False)
                    pe.matmul(o, xl[q][:], pick(Ah, e), start=False, stop=True).then_inc(s["gv_mm"], 1)
                i, q = j + 2, (r + 2) % 4
                if within(i):
                    pe.wait_ge(s[f"slot_ld{q}"], in_lane(i, q))
                    need(pe, s["xl_ok"], i - 1)
                    pe.transpose(MX[q % 2][:, 0, 0:P], xt[q][:, 0:C], ident).then_inc(s["xT_mm"], 1)
                i, q = j - 2, p
                if within(i):
                    need(pe, s["gt_ok"], i + 1)
                    need(pe, s["gT_ok"], i - 1)
                    for k in range(FF // P):
                        o = (PV[:, 0, :], W[0][:, 0:FF])[q]
                        mm = pe.transpose(o[:, k * P:(k + 1) * P], gt[q][:, k * P:(k + 1) * P], ident)
                    mm.then_inc(s["gT_mm"], 1)
                i, q = j - 3, 1 - p
                if within(i):
                    e = pe.value_load(table_e[0:1, bass.ds(i, 1)], min_val=0, max_val=E - 1)
                    need(pe, s["gT_ok"], i + 1)
                    need(pe, s["yb_ok"], i - 1)
                    for k in range(FF // P):
                        mm = pe.matmul(W[1 + q][:, 0:C], gT[q][:, k * P:(k + 1) * P],
                                       w2s[:, bass.ds(e, 1), k, :].rearrange("p o c -> p (o c)"),
                                       start=(k == 0), stop=(k == FF // P - 1))
                    mm.then_inc(s["y_mm"], 1)

            tiles(pe, tile, 3, -2)

            def finish(b, p):
                pe.wait_ge(s["sum1"], b // 2 + 1)
                need(pe, s["fin_ok"], b - 1)
                for k in range(TPB):
                    mm = pe.transpose(MX[p][:, 0, k * P:(k + 1) * P],
                                      y0[:, bass.ds(TPB * b + k, 1), :].rearrange("p o c -> p (o c)"), ident)
                mm.then_inc(s["fin_mm"], 1)

            for b in range(B):
                finish(b, b % 2)


def kernel(**inputs):
    import concourse.bacc as _bacc
    from concourse.bass_utils import run_bass_kernel_spmd as _run

    a = {k: np.asarray(v) for k, v in inputs.items()}
    cst, target, pad = constants()
    arrays = {
        "x": a["x"].reshape(B, C, N),
        "Wv_t": a["L0_conv_Wv"].T, "Wk_t": a["L0_conv_Wk"].T, "Wq_t": a["L0_conv_Wq"].T,
        "bv": a["L0_conv_bv"], "bk": a["L0_conv_bk"], "bq": a["L0_conv_bq"], "gamma": a["L0_conv_gamma"],
        "aWq_t": a["L1_attn_Wq"].T, "aWk_t": a["L1_attn_Wk"].T, "aWv_t": a["L1_attn_Wv"].T,
        "aWo_t": a["L1_attn_Wo"].T,
        "router_w": a["L1_ffn_router_w"], "router_b": a["L1_ffn_router_b"],
        "w1_t": a["L1_ffn_w1"].transpose(0, 2, 1), "b1": a["L1_ffn_b1"].reshape(E, FF // P, P).transpose(0, 2, 1),
        "wg": a["L1_ffn_wg"], "bg": a["L1_ffn_bg"], "wv": a["L1_ffn_wv"], "bv2": a["L1_ffn_bv"],
        "w2": a["L1_ffn_w2"], "b2": a["L1_ffn_b2"],
        "cst": cst, "target": target, "pad": pad,
    }
    nc = _bacc.Bacc("TRN2", target_bir_lowering=False, num_devices=1)
    aps = {}
    for name, v in arrays.items():
        arrays[name] = v = np.ascontiguousarray(v)
        aps[name] = nc.dram_tensor(f"in_{name}", v.shape, mybir.dt.from_np(v.dtype), kind="ExternalInput").ap()
    out = nc.dram_tensor("out_0_dram", (B, C, N), F32, kind="ExternalOutput").ap()
    hybrid_block(nc, out=out, **aps)
    r = _run(nc, [{f"in_{name}": v for name, v in arrays.items()}], core_ids=[0])
    return r.results[0]["out_0_dram"].reshape(B, C, 16, 16)
```

```python
from contextlib import ExitStack

import concourse.bass as bass
import numpy as np
from concourse import mybir

F32 = mybir.dt.float32
F32R = mybir.dt.float32r
BF16 = mybir.dt.bfloat16
U32 = mybir.dt.uint32
I32 = mybir.dt.int32
ALU = mybir.AluOpType
ACT = mybir.ActivationFunctionType
AX = mybir.AxisListType

B = 16
C = 128
N = 256
P = 128
TPB = N // P
NT = B * TPB
TOK = B * N
KD = 16
H = 8
HD = 16
E = 8
TOP = 2
FF = 256
GN_EPS = 1e-5
LN_EPS = 1e-5
SCALE = 0.25
RING = 3
STACK = 6 * HD
QROWS = STACK + 3
LOADS = 6
FIRST, LAST = 8, 14
ROW = C + 2
SLOTS = TOK + P
MAXT = TOK // P
ST = 72
assert ST >= TOP * TOK // P + E - 1
ROUTE = 23
CLD = 16 * 22
SPARE = ST - TOP * TOK // P
PADS = E + SPARE
CST = 3 * P + 4 + 2 * E + MAXT + E * E + ST


def need(eng, sem, items, per=1, cap=None):
    v = items * per
    if isinstance(v, int):
        if cap is not None:
            v = min(v, cap * per)
        if v <= 0:
            return
    eng.wait_ge(sem, v)


def done(eng, sem, images, per=1, extra=0):
    v = images * per + extra
    if isinstance(v, int):
        v = min(v, B * per)
        if v <= 0:
            return
    eng.wait_ge(sem, v)


def waits_after(eng, met, waits, most=None):
    values = []
    for _, items, *more in waits:
        per = more[0] if more else 1
        v = items * per + (more[1] if len(more) > 1 else 0)
        if not isinstance(v, int):
            eng.lower_val(v)
        elif most is not None:
            v = min(v, most * per)
        values.append(v)
    eng.wait_ge(*met)
    for w, v in zip(waits, values):
        if not isinstance(v, int) or v > 0:
            eng.wait_ge(w[0], v)


def done_after(eng, met, *waits):
    waits_after(eng, met, waits, B)


def need_after(eng, met, *waits):
    waits_after(eng, met, waits)


def part(t, a):
    return t[:, a:6 - a:5 - 2 * a, :]


def halves(t):
    return t[:].rearrange("p (a n) -> p a n", a=2)


def live(b):
    return not isinstance(b, int) or 0 <= b < B


def folds(t):
    return isinstance(t, int) and 0 <= t < E


def within(j):
    return not isinstance(j, int) or 0 <= j < ST


def in_lane(i, lane, lanes=4):
    return (i - lane) * (16 // lanes) + 16


def pick(t, i, n=1):
    return t[:, bass.ds(i, n), :].rearrange("p a n -> p (a n)")


def steps(eng, step, last):
    for t in range(FIRST):
        step(t, t % 2)
    with eng.Fori(FIRST, LAST - 1, 2) as i:
        for u in range(2):
            step(i + u, u)
    for t in range(LAST, last):
        step(t, t % 2)


def tiles(eng, tile, after, before=0, at_once=4):
    for j in range(before, 8):
        tile(j, j % at_once)
    with eng.Fori(8, ST - at_once, at_once) as i:
        for u in range(at_once):
            tile(i + u, u)
    for j in range(ST - at_once, ST + after):
        tile(j, j % at_once)


def tiles_by_four(eng, tile, packed, after, before):
    def load(g):
        experts = eng.value_load(packed[0:1, bass.ds(g, 1)], min_val=0, max_val=E ** 8 - 1)
        for r in range(4):
            for back in (0, 3):
                eng.lower_val(expert_of(experts, r, back))
        return experts

    for j in range(before, 8):
        if j % 4 == 0:
            experts = load(j // 4)
        tile(j, j % 4, experts if j >= 0 else None)
    with eng.Fori(8, ST - 4, 4) as i:
        experts = load(i // 4)
        for u in range(4):
            tile(i + u, u, experts)
    for j in range(ST - 4, ST + after):
        if j % 4 == 0:
            experts = load(j // 4)
        tile(j, j % 4, experts)


def expert_of(experts, r, back=0):
    return (experts // E ** (4 + r - back)) % E


def constants():
    row = np.arange(P)
    pad = np.zeros((PADS, P, ROW), np.float32)
    pad[:, :, C + 1] = TOP * TOK + np.arange(PADS * P).reshape(PADS, P)
    small = [E - np.arange(E), SLOTS * np.arange(E), P * np.arange(MAXT),
             np.tril(np.ones((E, E))).ravel(), np.arange(ST), E ** np.arange(4)]
    small = np.broadcast_to(np.concatenate(small).astype(np.float32), (P, CST - 3 * P))
    parts = [np.eye(P), np.kron(np.eye(P // 4), np.full((4, 4), 0.25)), np.triu(np.ones((P, P)), 1)]
    cst = np.concatenate([a.astype(np.float32) for a in parts] + [small], axis=1)
    tok = row[:, None, None] + P * np.arange(NT)[None, None, :] + TOK * np.arange(TOP)[None, :, None]
    return cst, tok.astype(np.float32), pad

def hybrid_block(nc, x, Wv_t, Wk_t, Wq_t, bv, bk, bq, gamma, aWq_t, aWk_t, aWv_t, aWo_t, router_w, router_b,
                 w1_t, b1, wg, bg, wv, bv2, w2, b2, cst, target, pad, out):
    ctx = ExitStack()
    with ctx:
        def sb(name, shape, dt=F32):
            return ctx.enter_context(nc.sbuf_tensor(name, shape, dt))

        def ps(name, shape, dt=F32):
            return ctx.enter_context(nc.psum_tensor(name, shape, dt))

        def sem(name):
            return ctx.enter_context(nc.semaphore(name))

        X = sb("X", [P, B, N])
        T = sb("T", [P, NT, C])
        Ah = sb("Ah", [P, E, 2 * FF], F32R)
        Al = sb("Al", [P, E, 2 * FF], F32R)
        bias = sb("bias", [P, E, 2 * FF])
        w2s = sb("w2s", [P, E, FF // P, C])
        b2s = sb("b2s", [P, E, C])
        wkv = sb("wkv", [C, C + KD])
        wq = sb("wq", [C, KD])
        bkv_b = sb("bkv_b", [P, C + KD])
        bq_c = sb("bq_c", [KD, 1])
        gamma_c = sb("gamma_c", [KD, 1])
        awq = sb("awq", [C, C])
        awk = sb("awk", [C, C])
        awv = sb("awv", [C, C])
        awo = sb("awo", [P, 2, C])
        rw = sb("rw", [C, E])
        rb_b = sb("rb_b", [P, E])
        cs = sb("cs", [P, CST])
        tgt = sb("tgt", [P, 2, NT])
        idb = sb("idb", [P, P], BF16)
        tri = sb("tri", [P, P], BF16)
        ones = sb("ones", [P, P], BF16)
        neg_half = sb("neg_half", [P, B])
        gstat = sb("gstat", [P, B, 6])
        gagg = sb("gagg", [P, B, 2])
        gtmp = sb("gtmp", [P, B])
        gall = sb("gall", [P, B, 2])
        gvar = sb("gvar", [P, B])
        grstd = sb("grstd", [P, B])
        gshift = sb("gshift", [P, B])
        grstd1 = sb("grstd1", [P, B])
        xn = [sb(f"xn{p}", [P, N]) for p in range(2)]
        xs = [sb(f"xs{p}", [P, N]) for p in range(2)]
        kvT = [sb(f"kvT{p}", [P, TPB, C + KD]) for p in range(2)]
        qz = [sb(f"qz{p}", [P, N]) for p in range(2)]
        vkz = [sb(f"vkz{p}", [P, C]) for p in range(2)]
        x1 = [sb(f"x1{p}", [P, N]) for p in range(2)]
        st1 = [sb(f"st1{p}", [P, TPB, 6]) for p in range(2)]
        ag1 = [sb(f"ag1{p}", [P, TPB, 2]) for p in range(2)]
        ve1 = [sb(f"ve1{p}", [P, TPB]) for p in range(2)]
        rs1 = [sb(f"rs1{p}", [P, TPB]) for p in range(2)]
        tn1 = [sb(f"tn1{p}", [P, TPB, C]) for p in range(2)]
        xnT = [sb(f"xnT{p}", [P, N]) for p in range(2)]
        parts = [sb(f"parts{p}", [P, 6, N], BF16) for p in range(2)]
        rest = [sb(f"rest{p}", [P, 2 * N]) for p in range(2)]
        vaug = [sb(f"vaug{p}", [P, TPB, H, 32]) for p in range(2)]
        mneg = [sb(f"mneg{p}", [P, H, TPB]) for p in range(2)]
        mrest = [sb(f"mrest{p}", [P, H * TPB]) for p in range(2)]
        mparts = [sb(f"mparts{p}", [P, 3, H * TPB], BF16) for p in range(2)]
        mrow = [sb(f"mrow{p}", [3 * H * TPB, P], BF16) for p in range(2)]
        oT = [sb(f"oT{p}", [P, 16, 32]) for p in range(2)]
        rden = [sb(f"rden{p}", [P, 16]) for p in range(2)]
        onrm = [sb(f"onrm{p}", [P, 16, 32]) for p in range(2)]
        ao = [sb(f"ao{p}", [P, 2, N]) for p in range(2)]
        st2 = [sb(f"st2{p}", [P, TPB, 6]) for p in range(2)]
        ag2 = [sb(f"ag2{p}", [P, TPB, 2]) for p in range(2)]
        ve2 = [sb(f"ve2{p}", [P, TPB]) for p in range(2)]
        rs2 = [sb(f"rs2{p}", [P, TPB]) for p in range(2)]
        rows = [sb(f"rows{p}", [P, 2, TPB, ROW]) for p in range(2)]
        x2T = [sb(f"x2T{p}", [P, N]) for p in range(2)]
        lg = [sb(f"lg{p}", [P, TPB, E]) for p in range(2)]
        lmax = [sb(f"lmax{p}", [P, TPB, 1]) for p in range(2)]
        lsub = [sb(f"lsub{p}", [P, TPB, E]) for p in range(2)]
        lexp = [sb(f"lexp{p}", [P, TPB, E]) for p in range(2)]
        lsum = [sb(f"lsum{p}", [P, TPB, 1]) for p in range(2)]
        linv = [sb(f"linv{p}", [P, TPB, 1]) for p in range(2)]
        prb = [sb(f"prb{p}", [P, 2, TPB, E]) for p in range(2)]
        gates = [sb(f"gates{p}", [P, 2, TPB, 1]) for p in range(2)]
        hit = [sb(f"hit{p}", [P, 2, TPB, E]) for p in range(2)]
        best = [sb(f"best{p}", [P, 2, TPB, 1]) for p in range(2)]
        onehot = [sb(f"onehot{p}", [P, 2, TPB, E]) for p in range(2)]
        mask = [sb(f"mask{p}", [P, TPB, E], BF16) for p in range(2)]
        cum = [sb(f"cum{p}", [P, TPB, E], BF16) for p in range(2)]
        slot = [sb(f"slot{p}", [P, TPB, E]) for p in range(2)]
        pickd = [sb(f"pickd{p}", [P, 2, TPB, E]) for p in range(2)]
        dest = [sb(f"dest{p}", [P, 2, TPB], U32) for p in range(2)]
        w1s = sb("w1s", [P, FF // P, C])
        wgv = sb("wgv", [P, FF // P, 2 * FF])
        b1s = sb("b1s", [P, FF // P])
        cend = sb("cend", [P, E], BF16)
        cnt = sb("cnt", [P, E])
        cnt_i = sb("cnt_i", [P, E], I32)
        tiles_e = sb("tiles_e", [P, E])
        upto = sb("upto", [P, E, E])
        ends = sb("ends", [P, E])
        te = sb("te", [P, ST])
        tstart = sb("tstart", [P, ST])
        toff = sb("toff", [P, ST])
        toff2 = sb("toff2", [P, ST])
        te1 = sb("te1", [P, ST])
        te4 = sb("te4", [P, ST // 4, 4])
        four = sb("four", [P, ST // 4 + 2])
        packed = sb("packed", [P, ST // 4 + 1], I32)
        table_b = sb("table_b", [P, ST], I32)
        qst = sb("qst", [P, RING, H * N], BF16)
        kst = sb("kst", [P, RING, H * N], BF16)
        vring = sb("vring", [P, RING, TPB * C])
        prob = sb("prob", [P, H, TPB, N])

        MX = [ps(f"MX{i}", [P, 2, N]) for i in range(2)]
        EX = [ps(f"EX{i}", [P, 2, N]) for i in range(2)]
        PV = ps("PV", [P, 2, N])
        W = [ps(f"W{i}", [P, 512]) for i in range(3)]

        scr = nc.dram_tensor("qk_parts", (B, 6, P, N), BF16, kind="Internal").ap()
        slots = nc.dram_tensor("slots", (E * SLOTS + SPARE * P, ROW), F32, kind="Internal").ap()
        res = nc.dram_tensor("res", (TOP * TOK + PADS * P, C), F32, kind="Internal").ap()
        rows2 = [r[:, 0, :, 0:C] for r in rows]
        ident = cs[:, 0:P]
        gavg = cs[:, P:2 * P]
        K0 = 3 * P
        prefer = cs[:, K0:K0 + E]
        first_slot = cs[:, K0 + E:K0 + 2 * E]
        step128 = cs[:, K0 + 2 * E:K0 + 2 * E + MAXT]
        upto_c = cs[:, K0 + 2 * E + MAXT:K0 + 2 * E + MAXT + E * E]
        tile_no = cs[:, K0 + 2 * E + MAXT + E * E:CST - 4]
        powers = cs[:, CST - 4:CST]

        xt = [kvT[k % 2][:, k // 2, 0:ROW] for k in range(4)]
        tag = sb("tag", [P, 8, 2])
        ttarget = sb("ttarget", [P, 8], U32)
        xh = [sb(f"xh{p}", [P, P], F32R) for p in range(2)]
        xl = [sb(f"xl{p}", [P, P], F32R) for p in range(2)]
        gv = rest
        sg = xs
        gt = xn
        gT = x1
        yb = vkz
        ys = [tn1[k % 2][:, k // 2, :] for k in range(4)]
        y0 = X[:].rearrange("p b n -> p (b n)").rearrange("p (t c) -> p t c", c=C)
        spare = prob[:].rearrange("p h k n -> p (h k n)")
        past = spare[:, 0:ST * E].rearrange("p (j e) -> p j e", e=E)
        pastn = spare[:, ST * E:2 * ST * E].rearrange("p (j e) -> p j e", e=E)
        cmp_ = spare[:, 2 * ST * E:2 * ST * E + E * MAXT].rearrange("p (e j) -> p e j", e=E)
        y1 = prob[:].rearrange("p h k n -> p (h k n)").rearrange("p (t c) -> p t c", c=C)
        fin = [xnT[p] for p in range(2)]

        names = """x_ld c_ld cb_ld z_pool z_dve z_four g_bn g_ag g_sq g_m2 g_mm g_all g_sqm g_var g_eps g_rstd g_shift idb_ok
            xn_ok xs_ok kv_mm kv_ok q_mm q_ok vk_mm vk_ok out_mm x1_ok t1_mm T_ok bn1 agg1 ve1_ok rs1_ok
            tn1_ok t2_mm xnT_ok qk_mm hi_ok rest_ok mid_ok lo_ok v_mm v_ok vaug_ok parts_st stack_ld
            mx_mm mx_ok mp0 mr0 mp1 mp2 mT_mm mT_ok mrow_ld ex_mm ex_ok pv_mm oT_ok rden_ok onrm_ok ao_ok
            wo_mm t2_ok bn2 agg2 ve2_ok rs2_ok tn2_ok t3_mm x2T_ok rt_mm lg_ok
            z_cum ones_ok w_ld fold_ld fold_mm Ah_ok Al_ok fbias_mm bias_ok route lexp_ok rank_mm copy_ok tag_ok gate_ok
            row_st0 row_st1 cend_ok cnt_mm cnt_ok tab tab_ok pad_st slot_ld0 slot_ld1 slot_ld2 slot_ld3 xT_mm xh_ok xl_ok gv_mm gv_ok sg_ok gt_ok gT_mm
            gT_ok y_mm yb_ok ys_ok res_st0 res_st1
            res_st2 res_st3 sum0 sum1 fin_mm fin_ok out_st0 out_st1 tags_ok ttarget_ok y_ld0 y_ld1 y_ld2 y_ld3""".split()
        s = {n: sem(n) for n in names}

        block = ctx.enter_context(nc.Block())

        @block.sync
        def _(sp):
            for g in range(4):
                sp.dma_start(X[:, 4 * g:4 * g + 4, :],
                             x[4 * g:4 * g + 4].rearrange("b c n -> c b n")).then_inc(s["x_ld"], 16)

            sp.wait_ge(s["x_ld"], 64)
            sp.dma_start(w2s[:], w2.rearrange("e (k f) c -> f e k c", f=P)).then_inc(s["w_ld"], 16)

            def load_expert(e):
                need(sp, s["fbias_mm"], e)
                sp.dma_start(w1s[:], w1_t[bass.ds(e, 1)].rearrange("o (k f) d -> f (o k) d", f=P)
                             ).then_inc(s["fold_ld"], 16)
                for n, w in enumerate((wg, wv)):
                    sp.dma_start(wgv[:, :, n * FF:(n + 1) * FF],
                                 w[bass.ds(e, 1)].rearrange("o (k f) n -> f (o k) n", f=P)
                                 ).then_inc(s["fold_ld"], 16)
                sp.dma_start(b1s[:], b1[bass.ds(e, 1)].rearrange("o f k -> (o f) k")).then_inc(s["fold_ld"], 16)

            sp.dma_start(slots[E * SLOTS:, :].rearrange("(t p) c -> t p c", p=P), pad[E:]).then_inc(s["pad_st"], 16)
            load_expert(0)
            for n, v in enumerate((bg, bv2)):
                sp.dma_start(bias[:, :, n * FF:(n + 1) * FF], v.partition_broadcast(P)).then_inc(s["w_ld"], 16)
            sp.dma_start(b2s[:], b2.partition_broadcast(P)).then_inc(s["w_ld"], 16)

            def step(t, p):
                b, q = t - 4, p
                if live(b):
                    ring = b % RING if isinstance(b, int) else sp.snap(b % RING)
                    done(sp, s["mT_ok"], b + 1)
                    for part in range(3):
                        d = qst[STACK + part:STACK + part + 1, bass.ds(ring, 1), :]
                        sp.dma_start(d.rearrange("p o (r t) -> p (o r) t", t=P),
                                     mrow[q][part * H * TPB:(part + 1) * H * TPB, :]
                                     ).then_inc(s["mrow_ld"], 16)
                b = t - 2
                if live(b):
                    ring = b % RING if isinstance(b, int) else sp.snap(b % RING)
                    done_after(sp, (s["x_ld"], 64), (s["parts_st"], b + 1, 16),
                               (s["ex_mm"], b - RING + 1, H))
                    src = scr[bass.ds(b, 1)].rearrange("o a (d h) t -> (o a d) h t", h=H)
                    for dst, runs in ((qst, ((0, 3), (0, 2), (0, 1))), (kst, ((3, 6), (4, 6), (5, 6)))):
                        row = 0
                        for lo, hi in runs:
                            n = (hi - lo) * HD
                            sp.dma_start(dst[row:row + n, bass.ds(ring, 1), :].rearrange("p o (h t) -> p (o h) t", h=H),
                                         src[lo * HD:hi * HD]).then_inc(s["stack_ld"], 16)
                            row += n
                b, q = t - 1, 1 - p
                if live(b):
                    done(sp, s["hi_ok"], b + 1)
                    done(sp, s["mid_ok"], b + 1)
                    done(sp, s["lo_ok"], b + 1)
                    sp.dma_start(scr[bass.ds(b, 1)].rearrange("o a p t -> (o p) a t"),
                                 parts[q][:]).then_inc(s["parts_st"], 16)
                if folds(t) and folds(t + 1):
                    load_expert(t + 1)

            steps(sp, step, B + 5)
            sp.wait_ge(s["cnt_ok"], 1)
            sp.wait_ge(s["c_ld"], CLD)
            for e in range(E):
                n_e = sp.value_load(cnt_i[0:1, e:e + 1], min_val=0, max_val=TOK)
                sp.dma_start(slots[bass.ds(n_e + e * SLOTS, P), :], pad[e]).then_inc(s["pad_st"], 16)

            sp.wait_ge(s["vk_mm"], B)
            sp.wait_ge(s["pad_st"], 16 * (E + 1))
            for p in range(2):
                sp.wait_ge(s[f"row_st{p}"], 16 * 4 * B // 2)
            sp.wait_ge(s["tab_ok"], 2)

            def load_tile(j, r):
                need(sp, s["xT_mm"], j - 3)
                need(sp, s["tags_ok"], j - 3)
                first = sp.value_load(table_b[0:1, bass.ds(j, 1)], min_val=0, max_val=E * SLOTS + (SPARE - 1) * P)
                sp.dma_start(xt[r], slots[bass.ds(first, P), :]).then_inc(s[f"slot_ld{r}"], 16)

            tiles(sp, load_tile, 0)

            for lane in range(4):
                sp.wait_ge(s[f"res_st{lane}"], 16 * ST // 4)
            sp.wait_ge(s["xs_ok"], B)
            sp.wait_ge(s["pv_mm"], 2 * B)
            for g in range(4):
                for n, y in enumerate((y0, y1)):
                    sp.dma_start(y[:, g * (NT // 4):(g + 1) * (NT // 4), :],
                                 res[n * TOK + g * (TOK // 4):n * TOK + (g + 1) * (TOK // 4), :].rearrange(
                                     "(t p) c -> p t c", p=P)).then_inc(s[f"y_ld{g}"], 16)

            def store(b, p):
                need(sp, s["fin_ok"], b + 1)
                sp.dma_start(out[bass.ds(b, 1)].rearrange("o c n -> (o c) n"), fin[p][:]).then_inc(s[f"out_st{p}"], 16)

            with sp.Fori(0, B - 1, 2) as i:
                for u in range(2):
                    store(i + u, u)
            for p in range(2):
                sp.wait_ge(s[f"out_st{p}"], 16 * B // 2)

        @block.gpsimd
        def _(pool):
            for p in range(2):
                pool.memset(vaug[p][:], 0.0).then_inc(s["z_pool"], 1)
            pool.wait_ge(s["z_pool"], 2)
            for p in range(2):
                pool.memset(vaug[p][:, :, :, HD:HD + 1], 1.0).then_inc(s["z_pool"], 1)
            pool.memset(neg_half[:], -0.5).then_inc(s["z_pool"], 1)
            pool.wait_ge(s["z_pool"], 5)
            pool.memset(kst[STACK:P, :, :], 1.0).then_inc(s["z_pool"], 1)
            pool.wait_ge(s["z_pool"], 6)
            pool.memset(ones[:], 1.0).then_inc(s["ones_ok"], 1)
            pool.wait_ge(s["g_eps"], 1)
            pool.tensor_tensor(grstd[:], gvar[:], neg_half[:], ALU.pow).then_inc(s["g_rstd"], 1)
            met = (s["z_pool"], 6)

            def scatter_rows(b, q, n):
                done_after(pool, met, (s["route"], b + 1, ROUTE), (s["copy_ok"], b + 1),
                           (s["tag_ok"], b + 1), (s["gate_ok"], b + 1))
                for k in range(TPB):
                    pool.indirect_dma_start(
                        out=slots, out_offset=bass.IndirectOffsetOnAxis(ap=dest[q][:, n, k:k + 1], axis=0),
                        in_=rows[q][:, n, k, :], in_offset=None).then_inc(s[f"row_st{q}"], 16)

            def step(t, p):
                o = 1 - p
                b, q = t - 5, o
                if live(b):
                    done(pool, s["rden_ok"], b + 1)
                    done(pool, s["ao_ok"], b - 1)
                    pool.tensor_tensor(onrm[q][:], oT[q][:],
                                       rden[q][:].rearrange("p (a o) -> p a o", o=1).broadcast_to([P, 16, 32]),
                                       ALU.mult).then_inc(s["onrm_ok"], 1)
                if live(t - 7):
                    scatter_rows(t - 7, o, 0)
                b, q = t - 1, o
                if live(b):
                    done(pool, s["mid_ok"], b + 1)
                    done(pool, s["parts_st"], b - 1, 16)
                    pool.tensor_tensor(part(parts[q], 2), halves(rest[q]), part(parts[q], 1),
                                       ALU.subtract).then_inc(s["lo_ok"], 1)
                if live(t - 7):
                    scatter_rows(t - 7, o, 1)
                b, q = t - 5, o
                if live(b):
                    root(b, q, ve2, rs2, "ve2_ok", "rs2_ok", "tn2_ok")
                b, q = t - 3, o
                if live(b):
                    m = mneg[q][:].rearrange("p h k -> p (h k)")
                    done_after(pool, met, (s["mx_ok"], b + 1, H), (s["mT_mm"], b - 1))
                    pool.tensor_scalar(mparts[q][:, 0, :], m, 1.0, 0.0, ALU.mult, ALU.add).then_inc(s["mp0"], 1)
                    done(pool, s["mp0"], b + 1)
                    pool.tensor_tensor(mrest[q][:], m, mparts[q][:, 0, :], ALU.subtract).then_inc(s["mr0"], 1)
                    done_after(pool, met, (s["mr0"], b + 1))
                    pool.tensor_scalar(mparts[q][:, 1, :], mrest[q][:], 1.0, 0.0, ALU.mult,
                                       ALU.add).then_inc(s["mp1"], 1)
                    done(pool, s["mp1"], b + 1)
                    pool.tensor_tensor(mparts[q][:, 2, :], mrest[q][:], mparts[q][:, 1, :],
                                       ALU.subtract).then_inc(s["mp2"], 1)
                b, q = t, p
                if live(b):
                    root(b, q, ve1, rs1, "ve1_ok", "rs1_ok", "tn1_ok")

            def root(b, q, ve, rs, ve_ok, rs_ok, used):
                done(pool, s[used], b - 1, TPB)
                done(pool, s[ve_ok], b + 1)
                pool.tensor_tensor(rs[q][:], ve[q][:], neg_half[:, 0:TPB], ALU.pow).then_inc(s[rs_ok], 1)

            steps(pool, step, B + 7)

            def scatter(j, r):
                if within(j):
                    need_after(pool, met, (s["tags_ok"], j + 1))
                    pool.tensor_scalar(ttarget[:, r:r + 1], tag[:, r, 1:2], 1.0, 0.0, ALU.mult,
                                       ALU.add).then_inc(s["ttarget_ok"], 1)
                    need_after(pool, met, (s["ys_ok"], j + 1), (s["ttarget_ok"], j + 1))
                    pool.indirect_dma_start(
                        out=res, out_offset=bass.IndirectOffsetOnAxis(ap=ttarget[:, r:r + 1], axis=0),
                        in_=ys[r % 4], in_offset=None).then_inc(s[f"res_st{r % 4}"], 16)

            tiles(pool, scatter, 0, 0, 8)

        @block.scalar
        def _(act):
            loads = [(cs[:], cst), (wkv[:, 0:C], Wv_t), (wkv[:, C:], Wk_t), (wq[:], Wq_t),
                     (bkv_b[:, 0:C], bv.partition_broadcast(P)), (bkv_b[:, C:], bk.partition_broadcast(P)),
                     (bq_c[:], bq.rearrange("(d o) -> d o", o=1)), (gamma_c[:], gamma.partition_broadcast(KD)),
                     (awq[:], aWq_t), (awk[:], aWk_t), (awv[:], aWv_t), (rw[:], router_w),
                     (rb_b[:], router_b.partition_broadcast(P)), (tgt[:], target)]
            act.wait_ge(s["z_dve"], 5)
            for h in range(H):
                loads.append((awo[32 * (h % 4):32 * (h % 4) + HD, h // 4, :], aWo_t[h * HD:(h + 1) * HD, :]))
            for d, src in loads:
                act.dma_start(d, src).then_inc(s["c_ld"], 16)

            def head_exp(b, h):
                done(act, s["ex_mm"], b, H, h + 1)
                done(act, s["pv_mm"], b - 1, 2, h // 4 + 1)
                act.activation(prob[:, h, :, :], EX[h % 2][:], ACT.Exp, scale=SCALE).then_inc(s["ex_ok"], 1)

            def norm_x(b, p):
                done(act, s["q_mm"], b - 1)
                act.activation(xn[p][:], pick(X, b), ACT.Identity, scale=grstd[:, bass.ds(b, 1)],
                               bias=gshift[:, bass.ds(b, 1)]).then_inc(s["xn_ok"], 1)
                done(act, s["x1_ok"], b - 1)
                act.activation(xs[p][:], pick(X, b), ACT.Identity, scale=grstd1[:, bass.ds(b, 1)],
                               bias=gshift[:, bass.ds(b, 1)]).then_inc(s["xs_ok"], 1)

            def step(t, p):
                o = 1 - p
                e = live(t - 4)
                b, q = t - 6, p
                if live(b):
                    done(act, s["t3_mm"], b + 1)
                    done(act, s["rt_mm"], b - 1)
                    act.copy(x2T[q][:], W[2][:, 0:N]).then_inc(s["x2T_ok"], 1)
                b, q = t - 1, o
                if live(b):
                    done(act, s["t2_mm"], b + 1)
                    done(act, s["v_mm"], b - 1)
                    act.copy(xnT[q][:], W[0][:, 0:N]).then_inc(s["xnT_ok"], 1)
                b, q = t, p
                if live(b):
                    done(act, s["q_mm"], b + 1)
                    done(act, s["out_mm"], b - 1)
                    act.activation(qz[q][0:KD, :], W[2][0:KD, 0:N], ACT.Identity,
                                   bias=bq_c[:]).then_inc(s["q_ok"], 1)
                    done(act, s["vk_mm"], b + 1)
                    act.activation(vkz[q][0:KD, :], W[1][0:KD, 0:C], ACT.Copy,
                                   scale=gamma_c[:]).then_inc(s["vk_ok"], 1)
                b, q = t - 1, o
                if live(b):
                    done(act, s["qk_mm"], b + 1)
                    done(act, s["parts_st"], b - 1, 16)
                    act.copy(part(parts[q], 0), halves(W[0])).then_inc(s["hi_ok"], 1)
                b, q = t - 6, p
                if live(b):
                    done(act, s["tn2_ok"], b + 1, TPB)
                    act.copy(rows[q][:, 1, :, 0:C], rows[q][:, 0, :, 0:C]).then_inc(s["copy_ok"], 1)
                    act.copy(rows[q][:, :, :, C + 1], tgt[:, :, bass.ds(TPB * b, TPB)]).then_inc(s["tag_ok"], 1)
                b, q = t - 1, o
                if live(b):
                    done(act, s["rest_ok"], b + 1)
                    act.copy(part(parts[q], 1), halves(rest[q])).then_inc(s["mid_ok"], 1)
                b, q = t - 4, p
                if live(b):
                    done(act, s["v_ok"], b + 1)
                    done(act, s["pv_mm"], b - 1, 2)
                    act.copy(vaug[q][:, :, :, 0:HD].rearrange("p k h d -> p (k h) d"),
                             pick(vring, b % RING).rearrange("p (r d) -> p r d", d=HD)
                             ).then_inc(s["vaug_ok"], 1)
                b, q = t - 1, o
                if live(b):
                    done(act, s["v_mm"], b + 1)
                    done(act, s["vaug_ok"], b - RING + 1)
                    act.copy(pick(vring, b % RING), W[2][:, 0:N]).then_inc(s["v_ok"], 1)
                if live(t + 1):
                    norm_x(t + 1, o)
                if e:
                    head_exp(t - 4, 0)
                b, q = t - 6, p
                if live(b):
                    done(act, s["route"], b, ROUTE, 2)
                    act.activation(lexp[q][:], lsub[q][:], ACT.Exp).then_inc(s["lexp_ok"], 1)
                if e:
                    head_exp(t - 4, 1)
                    head_exp(t - 4, 2)
                b, q = t, p
                if live(b):
                    done(act, s["t1_mm"], b + 1)
                    act.copy(pick(T, TPB * b, TPB), W[2][:, 0:N]).then_inc(s["T_ok"], 1)
                if e:
                    for h in range(3, 6):
                        head_exp(t - 4, h)
                if folds(t):
                    need(act, s["fold_mm"], t + 1)
                    act.copy(pick(Ah, t), W[1][:]).then_inc(s["Ah_ok"], 1)
                if e:
                    head_exp(t - 4, 6)
                    head_exp(t - 4, 7)
                b, q = t - 3, o
                if live(b):
                    done(act, s["mT_mm"], b + 1)
                    done(act, s["mrow_ld"], b - 1, 48)
                    act.copy(mrow[q][:], W[2][0:3 * H * TPB, 0:P // 2].bitcast(BF16)).then_inc(s["mT_ok"], 1)

            assert CLD == 16 * len(loads)
            act.wait_ge(s["c_ld"], CLD)
            act.wait_ge(s["g_shift"], 2)
            norm_x(0, 0)
            steps(act, step, B + 6)

            def tile(j, r):
                p = r % 2
                i, q = j + 2, p
                if within(i):
                    need(act, s["xT_mm"], i + 1)
                    need(act, s["gv_mm"], i - 1)
                    act.copy(xh[q][:], MX[q][:, 0, 0:P]).then_inc(s["xh_ok"], 1)
                    need(act, s["ttarget_ok"], i - 7)
                    act.copy(pick(tag, i % 8), xt[(r + 2) % 4][:, C:C + 2]).then_inc(s["tags_ok"], 1)
                i, q = j, p
                if within(i):
                    need(act, s["gv_ok"], i + 1)
                    need(act, s["gt_ok"], i - 1)
                    act.activation(sg[q][:], gv[q][:, 0:FF], ACT.Silu).then_inc(s["sg_ok"], 1)
                i, q = j - 2, p
                if within(i):
                    need(act, s["gT_mm"], i + 1)
                    need(act, s["y_mm"], i - 1)
                    act.copy(gT[q][:], (PV[:, 0, :], W[0][:, 0:FF])[q]).then_inc(s["gT_ok"], 1)
                i, q = j - 3, (r + 1) % 4
                if within(i):
                    need(act, s["yb_ok"], i + 1)
                    if not isinstance(i, int) or i >= 4:
                        act.wait_ge(s[f"res_st{q}"], in_lane(i - 4, q))
                    act.activation(ys[q], yb[q % 2][:], ACT.Copy, scale=pick(tag, i % 8)[:, 0:1]).then_inc(s["ys_ok"], 1)

            tiles(act, tile, 3, -2)

            def finish(b, p):
                need(act, s["fin_mm"], b + 1)
                if not isinstance(b, int) or b >= 2:
                    act.wait_ge(s[f"out_st{p}"], in_lane(b - 2, p, 2))
                act.copy(fin[p][:], MX[p][:, 0, :]).then_inc(s["fin_ok"], 1)

            for b in range(2):
                finish(b, b)
            with act.Fori(2, B - 1, 2) as i:
                for u in range(2):
                    finish(i + u, u)

        @block.vector
        def _(dve):
            for z in (awo, qz[0], qz[1], vkz[0], vkz[1]):
                dve.memset(z[:], 0.0).then_inc(s["z_dve"], 1)
            for z in (cum[1], mask[1]):
                dve.memset(z[:], 0.0).then_inc(s["z_cum"], 1)
            for b in range(B):
                if b == 0:
                    dve.wait_ge(s["x_ld"], 64)
                dve.bn_stats(gstat[:, b, :], X[:, b, :]).then_inc(s["g_bn"], 1)
            dve.wait_ge(s["g_bn"], B)
            for b in range(B):
                dve.bn_aggr(gagg[:, b, :], gstat[:, b, :]).then_inc(s["g_ag"], 1)
            dve.wait_ge(s["g_ag"], B)
            dve.tensor_tensor(gtmp[:], gagg[:, :, 0], gagg[:, :, 0], ALU.mult).then_inc(s["g_sq"], 1)
            dve.wait_ge(s["g_sq"], 1)
            dve.tensor_tensor(gagg[:, :, 1], gagg[:, :, 1], gtmp[:], ALU.add).then_inc(s["g_m2"], 1)
            dve.wait_ge(s["g_mm"], 1)
            dve.tensor_copy(gall[:].rearrange("p b k -> p (b k)"), W[0][:, 0:2 * B]).then_inc(s["g_all"], 1)
            dve.wait_ge(s["g_all"], 1)
            dve.tensor_tensor(gtmp[:], gall[:, :, 0], gall[:, :, 0], ALU.mult).then_inc(s["g_sqm"], 1)
            dve.wait_ge(s["g_sqm"], 1)
            dve.tensor_tensor(gvar[:], gall[:, :, 1], gtmp[:], ALU.subtract).then_inc(s["g_var"], 1)
            dve.wait_ge(s["g_var"], 1)
            dve.tensor_scalar(gvar[:], gvar[:], GN_EPS, None, ALU.add).then_inc(s["g_eps"], 1)
            dve.wait_ge(s["g_rstd"], 1)
            dve.scalar_tensor_tensor(gshift[:], gall[:, :, 0], -1.0, grstd[:], ALU.mult,
                                     ALU.mult).then_inc(s["g_shift"], 1)
            dve.tensor_scalar(grstd1[:], grstd[:], 1.0, None, ALU.add).then_inc(s["g_shift"], 1)
            dve.wait_ge(s["c_ld"], CLD)
            dve.tensor_copy(idb[:], ident).then_inc(s["idb_ok"], 1)
            dve.tensor_copy(tri[:], cs[:, 2 * P:3 * P]).then_inc(s["idb_ok"], 1)
            dve.wait_ge(s["z_cum"], 2)

            def over(v, n):
                return v.broadcast_to([P, v.shape[1], n])

            def along(v, k):
                return v.rearrange("p (o n) -> p o n", o=1).broadcast_to([P, k, v.shape[1]])

            def rows_sent(b, q):
                if not isinstance(b, int) or b >= 0:
                    dve.wait_ge(s[f"row_st{q}"], TOP * TPB * in_lane(b, q, 2))

            def router(b, q):
                n = [0]

                def did(ins):
                    n[0] += 1
                    ins.then_inc(s["route"], 1)

                def wait():
                    done(dve, s["route"], b, ROUTE, n[0])

                rows_sent(b - 2, q)
                did(dve.tensor_reduce(lmax[q][:], lg[q][:], AX.X, ALU.max))
                wait()
                did(dve.tensor_tensor(lsub[q][:], lg[q][:], over(lmax[q][:], E), ALU.subtract))
                yield
                done(dve, s["lexp_ok"], b + 1)
                did(dve.tensor_reduce(lsum[q][:], lexp[q][:], AX.X, ALU.add))
                wait()
                did(dve.reciprocal(linv[q][:], lsum[q][:]))
                wait()
                did(dve.tensor_tensor(prb[q][:, 0], lexp[q][:], over(linv[q][:], E), ALU.mult))
                for c in range(2):
                    wait()
                    if c == 1:
                        did(dve.scalar_tensor_tensor(prb[q][:, 1], onehot[q][:, 0], -2.0, prb[q][:, 0],
                                                     ALU.mult, ALU.add))
                        wait()
                    did(dve.tensor_reduce(gates[q][:, c], prb[q][:, c], AX.X, ALU.max))
                    yield
                    wait()
                    did(dve.tensor_tensor(hit[q][:, c], prb[q][:, c], over(gates[q][:, c], E), ALU.is_equal))
                    wait()
                    did(dve.tensor_tensor(pickd[q][:, c], hit[q][:, c], along(prefer, TPB), ALU.mult))
                    wait()
                    did(dve.tensor_reduce(best[q][:, c], pickd[q][:, c], AX.X, ALU.max))
                    yield
                    wait()
                    did(dve.tensor_tensor(onehot[q][:, c], pickd[q][:, c], over(best[q][:, c], E), ALU.is_equal))
                wait()
                did(dve.tensor_tensor(mask[q][:], onehot[q][:, 0], onehot[q][:, 1], ALU.add))
                did(dve.tensor_tensor(cum[q][:, 0], cum[1 - q][:, 1], mask[1 - q][:, 1], ALU.add))
                wait()
                did(dve.tensor_tensor(cum[q][:, 1], cum[q][:, 0], mask[q][:, 0], ALU.add))
                done(dve, s["copy_ok"], b + 1)
                dve.tensor_copy(rows[q][:, :, :, C], gates[q][:].rearrange("p c k o -> p c (k o)")
                                ).then_inc(s["gate_ok"], 1)
                yield
                done(dve, s["rank_mm"], b + 1)
                did(dve.tensor_tensor(slot[q][:], W[2][:, 0:TPB * E].rearrange("p (k e) -> p k e", k=TPB),
                                      along(first_slot, TPB), ALU.add))
                wait()
                for c in range(2):
                    did(dve.tensor_tensor(pickd[q][:, c], onehot[q][:, c], slot[q][:], ALU.mult))
                wait()
                with nc.allow_low_precision(reason="slots are whole numbers, summed in float32"):
                    did(dve.tensor_reduce(dest[q][:].rearrange("p c k -> p (c k)"),
                                          pickd[q][:].rearrange("p c k e -> p (c k) e"), AX.X, ALU.add))
                assert n[0] == ROUTE
                yield

            met = (s["x_ld"], 64)

            def row_max(b, p, c):
                k, pair = c // 4, c % 4
                done(dve, s["mx_mm"], b, H, c + 1)
                if c == 0:
                    done(dve, s["mp2"], b - 1)
                dve.tensor_reduce(mneg[p][:, 2 * pair:2 * pair + 2, k], MX[c % 2][:], AX.X, ALU.max,
                                  negate=True).then_inc(s["mx_ok"], 1)

            def stats(b, q, st, ag, ve, ready, bn, agg, ve_ok, used):
                done_after(dve, met, (s[ready], b + 1))
                for k in range(TPB):
                    dve.bn_stats(st[q][:, k, :], pick(T, TPB * b + k)).then_inc(s[bn], 1)
                for k in range(TPB):
                    done_after(dve, met, (s[used], b - 1, TPB), (s[bn], b, TPB, k + 1))
                    dve.bn_aggr(ag[q][:, k, :], st[q][:, k, :]).then_inc(s[agg], 1)
                done(dve, s[agg], b + 1, TPB)
                dve.tensor_scalar(ve[q][:], ag[q][:, :, 1], LN_EPS, None, ALU.add).then_inc(s[ve_ok], 1)

            def layer_norm(b, q, rs, tn, ag, rs_ok, tn_ok, used):
                done(dve, s[rs_ok], b + 1)
                done(dve, s[used], b - 1)
                for k in range(TPB):
                    dve.tensor_scalar(tn[:, k, :], pick(T, TPB * b + k), ag[q][:, k, 0:1],
                                      rs[q][:, k:k + 1], ALU.subtract, ALU.mult).then_inc(s[tn_ok], 1)

            def step(t, p):
                o = 1 - p
                m = live(t - 3)

                def row_maxima(*cs):
                    if m:
                        for c in cs:
                            row_max(t - 3, o, c)

                b, q = t - 5, o
                if live(b):
                    done(dve, s["pv_mm"], b + 1, 2)
                    done(dve, s["onrm_ok"], b - 1)
                    dve.transpose(oT[q][:].rearrange("p a r -> p (a r)"),
                                  PV[:].rearrange("p a n -> p (a n)")).then_inc(s["oT_ok"], 1)
                    done(dve, s["oT_ok"], b + 1)
                    dve.reciprocal(rden[q][:], oT[q][:, :, HD]).then_inc(s["rden_ok"], 1)
                if live(t - 1):
                    layer_norm(t - 1, o, rs1, tn1[o], ag1, "rs1_ok", "tn1_ok", "t2_mm")
                row_maxima(0)
                b, q = t, p
                if live(b):
                    done(dve, s["kv_mm"], b + 1)
                    done(dve, s["vk_mm"], b - 1)
                    dve.tensor_tensor(kvT[q][:], W[1][:, 0:TPB * (C + KD)].rearrange("p (k n) -> p k n", k=TPB),
                                      bkv_b[:].rearrange("p (o n) -> p o n", o=1).broadcast_to([P, TPB, C + KD]),
                                      ALU.add).then_inc(s["kv_ok"], 1)
                row_maxima(1, 2)
                b, q = t - 5, o
                if live(b):
                    done(dve, s["onrm_ok"], b + 1)
                    done(dve, s["wo_mm"], b - 1)
                    dve.transpose(ao[q][:].rearrange("p a n -> p (a n)"),
                                  onrm[q][:].rearrange("p a r -> p (a r)")).then_inc(s["ao_ok"], 1)
                b, q = t - 1, o
                if live(b):
                    done(dve, s["hi_ok"], b + 1)
                    done(dve, s["lo_ok"], b - 1)
                    dve.tensor_tensor(halves(rest[q]), halves(W[0]), part(parts[q], 0),
                                      ALU.subtract).then_inc(s["rest_ok"], 1)
                b, q = t - 6, p
                if live(b):
                    done(dve, s["rt_mm"], b + 1)
                    dve.tensor_tensor(lg[q][:], W[1][:, 0:TPB * E].rearrange("p (k e) -> p k e", k=TPB),
                                      along(rb_b[:], TPB), ALU.add).then_inc(s["lg_ok"], 1)
                    done(dve, s["lg_ok"], b + 1)
                    route = router(b, q)
                else:
                    route = iter(())
                row_maxima(3)
                next(route, None)
                row_maxima(4)
                b, q = t, p
                if live(b):
                    done(dve, s["out_mm"], b + 1)
                    done(dve, s["xs_ok"], b + 1)
                    done(dve, s["t1_mm"], b - 1)
                    dve.tensor_tensor(x1[q][:], W[1][:, 0:N], xs[q][:], ALU.add).then_inc(s["x1_ok"], 1)
                next(route, None)
                row_maxima(5)
                b, q = t - 5, o
                if live(b):
                    done(dve, s["wo_mm"], b + 1)
                    dve.tensor_tensor(pick(T, TPB * b, TPB), pick(T, TPB * b, TPB), W[0][:, 0:N],
                                      ALU.add).then_inc(s["t2_ok"], 1)
                next(route, None)
                row_maxima(6)
                b, q = t - 5, o
                if live(b):
                    stats(b, q, st2, ag2, ve2, "t2_ok", "bn2", "agg2", "ve2_ok", "tn2_ok")
                row_maxima(7)
                next(route, None)
                next(route, None)
                if folds(t):
                    need(dve, s["Ah_ok"], t + 1)
                    dve.tensor_tensor(pick(Al, t), W[1][:], pick(Ah, t).bitcast(F32),
                                      ALU.subtract).then_inc(s["Al_ok"], 1)
                b, q = t, p
                if live(b):
                    stats(b, q, st1, ag1, ve1, "T_ok", "bn1", "agg1", "ve1_ok", "tn1_ok")
                for _ in route:
                    pass
                b, q = t - 5, o
                if live(b):
                    rows_sent(b - 2, q)
                    done(dve, s["copy_ok"], b - 1)
                    layer_norm(b, q, rs2, rows2[q], ag2, "rs2_ok", "tn2_ok", "t3_mm")
                if folds(t):
                    need(dve, s["fbias_mm"], t + 1)
                    dve.tensor_tensor(pick(bias, t), W[0][:], pick(bias, t),
                                      ALU.add).then_inc(s["bias_ok"], 1)

            dve.wait_ge(s["w_ld"], 64)
            steps(dve, step, B + 6)

            n_tab = [0]
            dve.memset(four[:], 0.0).then_inc(s["z_four"], 1)
            dve.wait_ge(s["z_four"], 1)

            def tab(ins):
                n_tab[0] += 1
                ins.then_inc(s["tab"], 1)
                dve.wait_ge(s["tab"], n_tab[0])

            dve.tensor_tensor(cend[:], cum[1][:, 1], mask[1][:, 1], ALU.add).then_inc(s["cend_ok"], 1)
            dve.wait_ge(s["cnt_mm"], 1)
            dve.wait_ge(s["pv_mm"], 2 * B)
            tab(dve.tensor_copy(cnt[:], W[0][:, 0:E]))
            dve.tensor_copy(cnt_i[:], cnt[:]).then_inc(s["cnt_ok"], 1)
            tab(dve.tensor_tensor(cmp_, cnt[:].rearrange("p (e o) -> p e o", o=1).broadcast_to([P, E, MAXT]),
                                  along(step128, E), ALU.is_gt))
            tab(dve.tensor_reduce(tiles_e[:], cmp_, AX.X, ALU.add))
            tab(dve.tensor_tensor(upto[:], along(tiles_e[:], E), upto_c.rearrange("p (a b) -> p a b", a=E),
                                  ALU.mult))
            tab(dve.tensor_reduce(ends[:], upto[:], AX.X, ALU.add))
            tab(dve.tensor_tensor(past, tile_no.rearrange("p (j o) -> p j o", o=1).broadcast_to([P, ST, E]),
                                  along(ends[:], ST), ALU.is_ge))
            tab(dve.tensor_reduce(te[:], past, AX.X, ALU.add))
            tab(dve.tensor_tensor(pastn, past, along(tiles_e[:], ST), ALU.mult))
            tab(dve.tensor_reduce(tstart[:], pastn, AX.X, ALU.add))
            tab(dve.tensor_tensor(toff[:], tile_no, tstart[:], ALU.subtract))
            tab(dve.tensor_scalar(toff2[:], toff[:], float(P), None, ALU.mult))
            dve.scalar_tensor_tensor(table_b[:], te[:], float(SLOTS), toff2[:], ALU.mult,
                                     ALU.add).then_inc(s["tab_ok"], 1)
            tab(dve.tensor_scalar(te1[:], te[:], float(E - 1), None, ALU.min))
            tab(dve.tensor_tensor(te4[:], te1[:].rearrange("p (g u) -> p g u", u=4), along(powers, ST // 4), ALU.mult))
            tab(dve.tensor_reduce(four[:, 1:ST // 4 + 1], te4[:], AX.X, ALU.add))
            dve.scalar_tensor_tensor(packed[:], four[:, 1:], float(E ** 4), four[:, 0:ST // 4 + 1], ALU.mult,
                                     ALU.add).then_inc(s["tab_ok"], 1)
            dve.wait_ge(s["tab_ok"], 2)

            def tile(j, r, experts):
                p = r % 2
                i, q = j + 1, 1 - p
                if within(i):
                    need(dve, s["xh_ok"], i + 1)
                    need(dve, s["gv_mm"], i - 1)
                    dve.tensor_tensor(xl[q][:], MX[q][:, 0, 0:P], xh[q][:].bitcast(F32),
                                      ALU.subtract).then_inc(s["xl_ok"], 1)
                i, q = j, p
                if within(i):
                    e = expert_of(experts, r)
                    need(dve, s["gt_ok"], i - 1)
                    need(dve, s["sg_ok"], i - 1)
                    need(dve, s["gv_mm"], i + 1)
                    dve.tensor_tensor(gv[q][:], EX[q][:].rearrange("p a n -> p (a n)"), pick(bias, e),
                                      ALU.add).then_inc(s["gv_ok"], 1)
                i, q = j - 1, 1 - p
                if within(i):
                    need(dve, s["sg_ok"], i + 1)
                    need(dve, s["gT_mm"], i - 1)
                    dve.tensor_tensor(gt[q][:], sg[q][:], gv[q][:, FF:], ALU.mult).then_inc(s["gt_ok"], 1)
                i, q = j - 3, 1 - p
                if within(i):
                    e = expert_of(experts, r, 3)
                    need(dve, s["ys_ok"], i - 1)
                    need(dve, s["y_mm"], i + 1)
                    dve.tensor_tensor(yb[q][:], W[1 + q][:, 0:C], pick(b2s, e), ALU.add).then_inc(s["yb_ok"], 1)

            tiles_by_four(dve, tile, packed, 3, -1)

            for g in range(8):
                if g % 2 == 0:
                    dve.wait_ge(s[f"y_ld{g // 2}"], 32)
                v = slice(g * (NT // 8), (g + 1) * (NT // 8))
                dve.tensor_tensor(y0[:, v, :], y0[:, v, :], y1[:, v, :], ALU.add).then_inc(s["sum0"], 1)
                dve.wait_ge(s["sum0"], g + 1)
                dve.tensor_tensor(y0[:, v, :], y0[:, v, :], T[:, v, :], ALU.add).then_inc(s["sum1"], 1)

        @block.tensor
        def _(pe):
            pe.wait_ge(s["c_ld"], CLD)
            pe.wait_ge(s["g_m2"], 1)
            pe.matmul(W[0][:, 0:2 * B], gavg, gagg[:].rearrange("p b k -> p (b k)"),
                      start=True, stop=True).then_inc(s["g_mm"], 1)
            pe.wait_ge(s["g_all"], 1)
            pe.wait_ge(s["z_pool"], 6)
            pe.wait_ge(s["z_dve"], 5)
            pe.wait_ge(s["idb_ok"], 2)
            pe.wait_ge(s["ones_ok"], 1)

            def stack(t, b, h, lo=0, n=N, rows=STACK):
                v = t[0:rows, bass.ds(b % RING, 1), h * N + lo:h * N + lo + n]
                return v.rearrange("p o n -> p (o n)")

            def max_scores(b, c):
                k, pair = c // 4, c % 4
                if c == 0:
                    done(pe, s["stack_ld"], b + 1, 16 * LOADS)
                done(pe, s["mx_ok"], b, H, c - 1)
                for u in range(2):
                    h = 2 * pair + u
                    mm = pe.matmul(MX[c % 2][:, u, :], stack(qst, b, h, k * P, P), stack(kst, b, h),
                                   start=True, stop=True)
                mm.then_inc(s["mx_mm"], 1)

            def exp_scores(b, h):
                if h == 0:
                    done(pe, s["mrow_ld"], b + 1, 48)
                done(pe, s["ex_ok"], b, H, h - 1)
                for k in range(TPB):
                    mm = pe.matmul(EX[h % 2][:, k, :], stack(kst, b, h, k * P, P, QROWS),
                                   stack(qst, b, h, rows=QROWS), start=True, stop=True)
                mm.then_inc(s["ex_mm"], 1)

            def weigh(b, q, g):
                if g == 0:
                    done(pe, s["vaug_ok"], b + 1)
                    done(pe, s["oT_ok"], b)
                done(pe, s["ex_ok"], b, H, 4 * g + 4)
                for k in range(TPB):
                    for j in range(4):
                        mm = pe.matmul(PV[32 * j:32 * j + 32, g, :], vaug[q][:, k, 4 * g + j, :],
                                       prob[:, 4 * g + j, k, :], start=(k == 0), stop=(k == TPB - 1))
                mm.then_inc(s["pv_mm"], 1)

            def folded(ok, t):
                need(pe, ok, t if isinstance(t, int) else E, cap=E)

            def step(t, p):
                o = 1 - p

                def maxima(*cs):
                    if live(t - 3):
                        for c in cs:
                            max_scores(t - 3, c)

                def exps(*hs):
                    if live(t - 4):
                        for h in hs:
                            exp_scores(t - 4, h)

                b, q = t - 6, p
                if live(b):
                    done(pe, s["tn2_ok"], b + 1, TPB)
                    done(pe, s["T_ok"], t)
                    done(pe, s["mT_ok"], t - 3)
                    done(pe, s["route"], b, ROUTE)
                    for k in range(TPB):
                        mm = pe.transpose(W[2][:, k * P:(k + 1) * P], rows2[q][:, k, :], ident)
                    mm.then_inc(s["t3_mm"], 1)
                maxima(0)
                b, q = t, p
                if live(b):
                    done(pe, s["xn_ok"], b + 1)
                    done(pe, s["x1_ok"], t)
                    folded(s["Al_ok"], t)
                    for k in range(TPB):
                        mm = pe.matmul(W[1][:, k * (C + KD):(k + 1) * (C + KD)], xn[q][:, k * P:(k + 1) * P],
                                       wkv[:], start=True, stop=True)
                    mm.then_inc(s["kv_mm"], 1)
                b, q = t - 1, o
                if live(b):
                    done(pe, s["tn1_ok"], b + 1, TPB)
                    done(pe, s["t2_ok"], t - 5)
                    folded(s["bias_ok"], t)
                    for k in range(TPB):
                        mm = pe.transpose(W[0][:, k * P:(k + 1) * P], tn1[q][:, k, :], ident)
                    mm.then_inc(s["t2_mm"], 1)
                maxima(1)
                b, q = t, p
                if live(b):
                    done(pe, s["x2T_ok"], t - 5)
                    done(pe, s["T_ok"], t)
                    done(pe, s["mT_ok"], t - 3)
                    pe.matmul(W[2][0:KD, 0:N], wq[:], xn[q][:], start=True, stop=True).then_inc(s["q_mm"], 1)
                    done(pe, s["kv_ok"], b + 1)
                    for k in range(TPB):
                        mm = pe.matmul(W[1][0:KD, 0:C], kvT[q][:, k, C:C + KD], kvT[q][:, k, 0:C],
                                       start=(k == 0), stop=(k == TPB - 1))
                    mm.then_inc(s["vk_mm"], 1)
                maxima(2)
                b, q = t - 1, o
                if live(b):
                    done(pe, s["xnT_ok"], b + 1)
                    pe.matmul(W[0][:, 0:N], awq[:], xnT[q][:], start=True, stop=True)
                    pe.matmul(W[0][:, N:2 * N], awk[:], xnT[q][:], start=True, stop=True).then_inc(s["qk_mm"], 1)
                b, q = t - 6, p
                if live(b):
                    done(pe, s["x2T_ok"], b + 1)
                    done(pe, s["vk_ok"], t + 1)
                    done(pe, s["x1_ok"], t)
                    folded(s["Al_ok"], t)
                    for k in range(TPB):
                        mm = pe.matmul(W[1][:, k * E:(k + 1) * E], x2T[q][:, k * P:(k + 1) * P], rw[:],
                                       start=True, stop=True)
                    mm.then_inc(s["rt_mm"], 1)
                maxima(3)
                b, q = t - 1, o
                if live(b):
                    done(pe, s["q_ok"], t + 1)
                    done(pe, s["x2T_ok"], t - 5)
                    for k in range(TPB):
                        mm = pe.matmul(W[2][:, k * C:(k + 1) * C], xnT[q][:, k * P:(k + 1) * P], awv[:],
                                       start=True, stop=True)
                    mm.then_inc(s["v_mm"], 1)
                maxima(4)
                exps(0)
                b, q = t, p
                if live(b):
                    done(pe, s["vk_ok"], b + 1)
                    done(pe, s["lg_ok"], t - 5)
                    done(pe, s["q_ok"], b + 1)
                    pe.matmul(W[1][:, 0:N], vkz[q][:], qz[q][:], start=True, stop=True).then_inc(s["out_mm"], 1)
                exps(1)
                maxima(5)
                b, q = t - 5, o
                if live(b):
                    done(pe, s["ao_ok"], b + 1)
                    done(pe, s["rest_ok"], t)
                    done(pe, s["t2_ok"], b)
                    for k in range(TPB):
                        for g in range(2):
                            mm = pe.matmul(W[0][:, k * C:(k + 1) * C], ao[q][:, g, k * P:(k + 1) * P],
                                           awo[:, g, :], start=(g == 0), stop=(g == 1))
                    mm.then_inc(s["wo_mm"], 1)
                exps(2)
                maxima(6)
                b, q = t, p
                if live(b):
                    done(pe, s["x1_ok"], b + 1)
                    done(pe, s["v_ok"], t)
                    for k in range(TPB):
                        mm = pe.transpose(W[2][:, k * P:(k + 1) * P], x1[q][:, k * P:(k + 1) * P], ident)
                    mm.then_inc(s["t1_mm"], 1)
                exps(3)
                maxima(7)
                exps(4)
                if live(t - 4):
                    weigh(t - 4, p, 0)
                exps(5)
                if folds(t):
                    pe.wait_ge(s["fold_ld"], (t + 1) * 64)
                    done(pe, s["x1_ok"], t + 1)
                    for k in range(FF // P):
                        mm = pe.matmul(W[1][:], w1s[:, k, :], wgv[:, k, :], start=(k == 0), stop=(k == FF // P - 1))
                    mm.then_inc(s["fold_mm"], 1)
                exps(6, 7)
                b, q = t - 6, p
                if live(b):
                    done(pe, s["route"], b, ROUTE, ROUTE - 4)
                    done(pe, s["T_ok"], t + 1)
                    done(pe, s["v_ok"], t)
                    pe.matmul(W[2][:, 0:TPB * E], tri[:], mask[q][:].rearrange("p k e -> p (k e)"),
                              start=True, stop=False)
                    pe.matmul(W[2][:, 0:TPB * E], ones[:], cum[q][:].rearrange("p k e -> p (k e)"),
                              start=False, stop=True).then_inc(s["rank_mm"], 1)
                if folds(t):
                    done(pe, s["t2_ok"], t - 4)
                    done(pe, s["rest_ok"], t)
                    for k in range(FF // P):
                        mm = pe.matmul(W[0][:], b1s[:, k:k + 1].broadcast_to([P, P]), wgv[:, k, :],
                                       start=(k == 0), stop=(k == FF // P - 1))
                    mm.then_inc(s["fbias_mm"], 1)
                b, q = t - 3, o
                if live(b):
                    done_after(pe, (s["c_ld"], CLD), (s["mp2"], b + 1), (s["T_ok"], t + 1), (s["v_ok"], t),
                               *[(s["route"], t - 6, ROUTE, ROUTE - 3)] * live(t - 6))
                    pe.transpose(W[2][0:3 * H * TPB, 0:P // 2].bitcast(BF16),
                                 mparts[q][:].rearrange("p a r -> p (a r)"), idb[:]).then_inc(s["mT_mm"], 1)
                if live(t - 4):
                    weigh(t - 4, p, 1)

            steps(pe, step, B + 6)

            pe.wait_ge(s["cend_ok"], 1)
            pe.wait_ge(s["x2T_ok"], B)
            pe.matmul(W[0][:, 0:E], ones[:], cend[:], start=True, stop=True).then_inc(s["cnt_mm"], 1)
            pe.wait_ge(s["tab_ok"], 2)
            pe.wait_ge(s["w_ld"], 64)

            def tile(j, r, experts):
                p = r % 2
                i, q = j, p
                if within(i):
                    e = expert_of(experts, r)
                    need(pe, s["xl_ok"], i + 1)
                    need(pe, s["gv_ok"], i - 1)
                    o = EX[q][:].rearrange("p a n -> p (a n)")
                    pe.matmul(o, xh[q][:], pick(Ah, e), start=True, stop=False)
                    pe.matmul(o, xh[q][:], pick(Al, e), start=False, stop=False)
                    pe.matmul(o, xl[q][:], pick(Ah, e), start=False, stop=True).then_inc(s["gv_mm"], 1)
                i, q = j + 3, (r + 3) % 4
                if within(i):
                    pe.wait_ge(s[f"slot_ld{q}"], in_lane(i, q))
                    need(pe, s["xl_ok"], i - 1)
                    pe.transpose(MX[q % 2][:, 0, 0:P], xt[q][:, 0:C], ident).then_inc(s["xT_mm"], 1)
                i, q = j - 2, p
                if within(i):
                    need(pe, s["gt_ok"], i + 1)
                    need(pe, s["gT_ok"], i - 1)
                    for k in range(FF // P):
                        o = (PV[:, 0, :], W[0][:, 0:FF])[q]
                        mm = pe.transpose(o[:, k * P:(k + 1) * P], gt[q][:, k * P:(k + 1) * P], ident)
                    mm.then_inc(s["gT_mm"], 1)
                i, q = j - 3, 1 - p
                if within(i):
                    e = expert_of(experts, r, 3)
                    need(pe, s["gT_ok"], i + 1)
                    need(pe, s["yb_ok"], i - 1)
                    for k in range(FF // P):
                        mm = pe.matmul(W[1 + q][:, 0:C], gT[q][:, k * P:(k + 1) * P],
                                       w2s[:, bass.ds(e, 1), k, :].rearrange("p o c -> p (o c)"),
                                       start=(k == 0), stop=(k == FF // P - 1))
                    mm.then_inc(s["y_mm"], 1)

            tiles_by_four(pe, tile, packed, 3, -3)

            def finish(b, p):
                pe.wait_ge(s["sum1"], b // 2 + 1)
                need(pe, s["fin_ok"], b - 1)
                for k in range(TPB):
                    mm = pe.transpose(MX[p][:, 0, k * P:(k + 1) * P],
                                      y0[:, bass.ds(TPB * b + k, 1), :].rearrange("p o c -> p (o c)"), ident)
                mm.then_inc(s["fin_mm"], 1)

            for b in range(B):
                finish(b, b % 2)


def kernel(**inputs):
    import concourse.bacc as _bacc
    from concourse.bass_utils import run_bass_kernel_spmd as _run

    a = {k: np.asarray(v) for k, v in inputs.items()}
    cst, target, pad = constants()

    def by_head(w):
        return w.T.reshape(C, H, HD).transpose(0, 2, 1).reshape(C, C)

    arrays = {
        "x": a["x"].reshape(B, C, N),
        "Wv_t": a["L0_conv_Wv"].T, "Wk_t": a["L0_conv_Wk"].T, "Wq_t": a["L0_conv_Wq"].T,
        "bv": a["L0_conv_bv"], "bk": a["L0_conv_bk"], "bq": a["L0_conv_bq"], "gamma": a["L0_conv_gamma"],
        "aWq_t": by_head(a["L1_attn_Wq"]), "aWk_t": by_head(a["L1_attn_Wk"]), "aWv_t": a["L1_attn_Wv"].T,
        "aWo_t": a["L1_attn_Wo"].T,
        "router_w": a["L1_ffn_router_w"], "router_b": a["L1_ffn_router_b"],
        "w1_t": a["L1_ffn_w1"].transpose(0, 2, 1), "b1": a["L1_ffn_b1"].reshape(E, FF // P, P).transpose(0, 2, 1),
        "wg": a["L1_ffn_wg"], "bg": a["L1_ffn_bg"], "wv": a["L1_ffn_wv"], "bv2": a["L1_ffn_bv"],
        "w2": a["L1_ffn_w2"], "b2": a["L1_ffn_b2"],
        "cst": cst, "target": target, "pad": pad,
    }
    nc = _bacc.Bacc("TRN2", target_bir_lowering=False, num_devices=1)
    aps = {}
    for name, v in arrays.items():
        arrays[name] = v = np.ascontiguousarray(v)
        aps[name] = nc.dram_tensor(f"in_{name}", v.shape, mybir.dt.from_np(v.dtype), kind="ExternalInput").ap()
    out = nc.dram_tensor("out_0_dram", (B, C, N), F32, kind="ExternalOutput").ap()
    hybrid_block(nc, out=out, **aps)
    r = _run(nc, [{f"in_{name}": v for name, v in arrays.items()}], core_ids=[0])
    return r.results[0]["out_0_dram"].reshape(B, C, 16, 16)
```

```python
from contextlib import ExitStack

import concourse.bass as bass
import numpy as np
from concourse import mybir

F32 = mybir.dt.float32
F32R = mybir.dt.float32r
BF16 = mybir.dt.bfloat16
U32 = mybir.dt.uint32
I32 = mybir.dt.int32
ALU = mybir.AluOpType
ACT = mybir.ActivationFunctionType
AX = mybir.AxisListType

B = 16
C = 128
N = 256
P = 128
TPB = N // P
NT = B * TPB
TOK = B * N
KD = 16
H = 8
HD = 16
E = 8
TOP = 2
FF = 256
GN_EPS = 1e-5
LN_EPS = 1e-5
SCALE = 0.25
RING = 3
STACK = 6 * HD
QROWS = STACK + 3
LOADS = 6
PART = 32
FIRST, LAST = 8, 14
ROW = C + 2
SLOTS = TOK + P
MAXT = TOK // P
ST = 72
assert ST >= TOP * TOK // P + E - 1
ROUTE = 22
GN_FIRST = 4
SPARE = ST - TOP * TOK // P
PADS = E + SPARE
FIRST_COLS = (("gavg", P), ("ident", P), ("wkv", C + KD), ("wq", KD), ("bkv", C + KD), ("bq", 1), ("gamma", 1))
LATER_COLS = (("lower", P), ("awq", C), ("awk", C), ("awv", C), ("awo", 2 * C), ("rw", E), ("rb", E),
              ("target", 2 * NT), ("prefer", E), ("first_slot", E), ("step128", MAXT), ("upto", E * E),
              ("tile_no", ST), ("powers", 4))
N_FIRST = sum(n for _, n in FIRST_COLS)
N_COLS = N_FIRST + sum(n for _, n in LATER_COLS)


def need(eng, sem, items, per=1, cap=None):
    v = items * per
    if isinstance(v, int):
        if cap is not None:
            v = min(v, cap * per)
        if v <= 0:
            return
    eng.wait_ge(sem, v)


def done(eng, sem, images, per=1, extra=0):
    v = images * per + extra
    if isinstance(v, int):
        v = min(v, B * per)
        if v <= 0:
            return
    eng.wait_ge(sem, v)


def waits_after(eng, met, waits, most=None):
    values = []
    for _, items, *more in waits:
        per = more[0] if more else 1
        v = items * per + (more[1] if len(more) > 1 else 0)
        if not isinstance(v, int):
            eng.lower_val(v)
        elif most is not None:
            v = min(v, most * per)
        values.append(v)
    eng.wait_ge(*met)
    for w, v in zip(waits, values):
        if not isinstance(v, int) or v > 0:
            eng.wait_ge(w[0], v)


def done_after(eng, met, *waits):
    waits_after(eng, met, waits, B)


def need_after(eng, met, *waits):
    waits_after(eng, met, waits)


def part(t, a):
    return t[:, a:6 - a:5 - 2 * a, :]


def halves(t):
    return t[:].rearrange("p (a n) -> p a n", a=2)


def live(b):
    return not isinstance(b, int) or 0 <= b < B


def folds(t):
    return isinstance(t, int) and 0 <= t < E


def at_step(t, at):
    return isinstance(t, int) and t == at


def within(j):
    return not isinstance(j, int) or 0 <= j < ST


def in_lane(i, lane, lanes=4):
    return (i - lane) * (16 // lanes) + 16


def pick(t, i, n=1):
    return t[:, bass.ds(i, n), :].rearrange("p a n -> p (a n)")


def steps(eng, step, last):
    for t in range(FIRST):
        step(t, t % 2)
    with eng.Fori(FIRST, LAST - 1, 2) as i:
        for u in range(2):
            step(i + u, u)
    for t in range(LAST, last):
        step(t, t % 2)


def tiles(eng, tile, after, before=0):
    for j in range(before, 8):
        tile(j, j % 8)
    with eng.Fori(8, ST - 8, 8) as i:
        for u in range(8):
            tile(i + u, u)
    for j in range(ST - 8, ST + after):
        tile(j, j % 8)


def tiles_by_four(eng, tile, packed, after, before):
    experts = [None]

    def with_experts(j, r):
        if r % 4 == 0:
            experts[0] = eng.value_load(packed[0:1, bass.ds(j // 4, 1)], min_val=0, max_val=E ** 8 - 1)
        tile(j, r % 4, experts[0])

    tiles(eng, with_experts, after, before)


def expert_of(experts, r, back=0):
    return (experts // E ** (4 + r - back)) % E


def constants():
    row = np.arange(P)
    pad = np.zeros((PADS, P, ROW), np.float32)
    pad[:, :, C + 1] = TOP * TOK + np.arange(PADS * P).reshape(PADS, P)
    tok = row[:, None, None] + P * np.arange(NT)[None, None, :] + TOK * np.arange(TOP)[None, :, None]
    tables = {
        "gavg": np.kron(np.eye(P // 4), np.full((4, 4), 0.25)), "ident": np.eye(P),
        "lower": np.triu(np.ones((P, P)), 1),
        "target": tok.reshape(P, -1), "prefer": E - np.arange(E), "first_slot": SLOTS * np.arange(E),
        "step128": P * np.arange(MAXT), "upto": np.tril(np.ones((E, E))).ravel(), "tile_no": np.arange(ST),
        "powers": E ** np.arange(4),
    }
    return {name: v.astype(np.float32) for name, v in tables.items()}, pad


def hybrid_block(nc, x, cols, w1_t, b1, wg, bg, wv, bv2, w2, b2, pad, out):
    ctx = ExitStack()
    with ctx:
        def sb(name, shape, dt=F32):
            return ctx.enter_context(nc.sbuf_tensor(name, shape, dt))

        def ps(name, shape, dt=F32):
            return ctx.enter_context(nc.psum_tensor(name, shape, dt))

        def sem(name):
            return ctx.enter_context(nc.semaphore(name))

        X = sb("X", [P, B, N])
        T = sb("T", [P, NT, C])
        Ah = sb("Ah", [P, E, 2 * FF], F32R)
        Al = sb("Al", [P, E, 2 * FF], F32R)
        bias = sb("bias", [P, E, 2 * FF])
        w2s = sb("w2s", [P, E, FF // P, C])
        b2r = sb("b2r", [P, E, C], BF16)
        cs = sb("cs", [P, N_COLS])
        idb = sb("idb", [P, P], BF16)
        tri = sb("tri", [P, P], BF16)
        ones = sb("ones", [P, P], BF16)
        neg_half = sb("neg_half", [P, B])
        gstat = sb("gstat", [P, B, 6])
        gagg = sb("gagg", [P, B, 2])
        gtmp = sb("gtmp", [P, B])
        gall = sb("gall", [P, B, 2])
        gvar = sb("gvar", [P, B])
        grstd = sb("grstd", [P, B])
        gshift = sb("gshift", [P, B])
        grstd1 = sb("grstd1", [P, B])
        xn = [sb(f"xn{p}", [P, N]) for p in range(2)]
        xs = [sb(f"xs{p}", [P, N]) for p in range(2)]
        kvT = [sb(f"kvT{p}", [P, TPB, C + KD]) for p in range(2)]
        qz = [sb(f"qz{p}", [P, N]) for p in range(2)]
        vkz = [sb(f"vkz{p}", [P, C]) for p in range(2)]
        x1 = [sb(f"x1{p}", [P, N]) for p in range(2)]
        st1 = [sb(f"st1{p}", [P, TPB, 6]) for p in range(2)]
        ag1 = [sb(f"ag1{p}", [P, TPB, 2]) for p in range(2)]
        nm1 = [sb(f"nm1{p}", [P, TPB]) for p in range(2)]
        ve1 = [sb(f"ve1{p}", [P, TPB]) for p in range(2)]
        rs1 = [sb(f"rs1{p}", [P, TPB]) for p in range(2)]
        nb1 = [sb(f"nb1{p}", [P, TPB]) for p in range(2)]
        tn1 = [sb(f"tn1{p}", [P, TPB, C]) for p in range(2)]
        xnT = [sb(f"xnT{p}", [P, N]) for p in range(2)]
        parts = [sb(f"parts{p}", [P, 6, N], BF16) for p in range(2)]
        rest = [sb(f"rest{p}", [P, 2 * N]) for p in range(2)]
        vaug = [sb(f"vaug{p}", [P, TPB, H, 32]) for p in range(2)]
        mneg = [sb(f"mneg{p}", [P, H, TPB]) for p in range(2)]
        mrest = [sb(f"mrest{p}", [P, H * TPB]) for p in range(2)]
        mparts = [sb(f"mparts{p}", [P, 3, H * TPB], BF16) for p in range(2)]
        mrow = [sb(f"mrow{p}", [3 * H * TPB, P], BF16) for p in range(2)]
        oT = [sb(f"oT{p}", [P, 16, 32]) for p in range(2)]
        rden = [sb(f"rden{p}", [P, 16]) for p in range(2)]
        onrm = [sb(f"onrm{p}", [P, 16, 32]) for p in range(2)]
        ao = [sb(f"ao{p}", [P, 2, N]) for p in range(2)]
        st2 = [sb(f"st2{p}", [P, TPB, 6]) for p in range(2)]
        ag2 = [sb(f"ag2{p}", [P, TPB, 2]) for p in range(2)]
        nm2 = [sb(f"nm2{p}", [P, TPB]) for p in range(2)]
        ve2 = [sb(f"ve2{p}", [P, TPB]) for p in range(2)]
        rs2 = [sb(f"rs2{p}", [P, TPB]) for p in range(2)]
        nb2 = [sb(f"nb2{p}", [P, TPB]) for p in range(2)]
        rows = [sb(f"rows{p}", [P, 2, TPB, ROW]) for p in range(2)]
        x2T = [sb(f"x2T{p}", [P, N]) for p in range(2)]
        lg = [sb(f"lg{p}", [P, TPB, E]) for p in range(2)]
        lneg = [sb(f"lneg{p}", [P, TPB, 1]) for p in range(2)]
        lexp = [sb(f"lexp{p}", [P, TPB, E]) for p in range(2)]
        lsum = [sb(f"lsum{p}", [P, TPB, 1]) for p in range(2)]
        linv = [sb(f"linv{p}", [P, TPB, 1]) for p in range(2)]
        prb = [sb(f"prb{p}", [P, 2, TPB, E]) for p in range(2)]
        gates = [sb(f"gates{p}", [P, 2, TPB, 1]) for p in range(2)]
        hit = [sb(f"hit{p}", [P, 2, TPB, E]) for p in range(2)]
        best = [sb(f"best{p}", [P, 2, TPB, 1]) for p in range(2)]
        onehot = [sb(f"onehot{p}", [P, 2, TPB, E]) for p in range(2)]
        mask = [sb(f"mask{p}", [P, TPB, E], BF16) for p in range(2)]
        cum = [sb(f"cum{p}", [P, TPB, E], BF16) for p in range(2)]
        slot = [sb(f"slot{p}", [P, TPB, E]) for p in range(2)]
        pickd = [sb(f"pickd{p}", [P, 2, TPB, E]) for p in range(2)]
        dest = [sb(f"dest{p}", [P, 2, TPB], U32) for p in range(2)]
        bgv = sb("bgv", [P, 2 * FF])
        w1s = sb("w1s", [P, FF // P, C])
        wgv = sb("wgv", [P, FF // P, 2 * FF])
        b1s = sb("b1s", [P, FF // P])
        cend = sb("cend", [P, E], BF16)
        cnt = sb("cnt", [P, E])
        cnt_i = sb("cnt_i", [P, E], I32)
        tiles_e = sb("tiles_e", [P, E])
        upto = sb("upto", [P, E, E])
        ends = sb("ends", [P, E])
        te = sb("te", [P, ST])
        tstart = sb("tstart", [P, ST])
        toff = sb("toff", [P, ST])
        toff2 = sb("toff2", [P, ST])
        te1 = sb("te1", [P, ST])
        te4 = sb("te4", [P, ST // 4, 4])
        four = sb("four", [P, ST // 4 + 2])
        packed = sb("packed", [P, ST // 4 + 1], I32)
        table_b = sb("table_b", [P, ST], I32)
        qst = sb("qst", [P, RING, H * N], BF16)
        kst = sb("kst", [P, RING, H * N], BF16)
        vring = sb("vring", [P, RING, TPB * C])
        prob = sb("prob", [P, H, TPB, N])

        MX = [ps(f"MX{i}", [P, 2, N]) for i in range(2)]
        EX = [ps(f"EX{i}", [P, 2, N]) for i in range(2)]
        PV = ps("PV", [P, 2, N])
        W = [ps(f"W{i}", [P, 512]) for i in range(3)]

        scr = nc.dram_tensor("qk_parts", (B, 6, P, N), BF16, kind="Internal").ap()
        slots = nc.dram_tensor("slots", (E * SLOTS + SPARE * P, ROW), F32, kind="Internal").ap()
        res = nc.dram_tensor("res", (TOP * TOK + PADS * P, C), F32, kind="Internal").ap()
        rows2 = [r[:, 0, :, 0:C] for r in rows]
        at, col = 0, {}
        for name, n in FIRST_COLS + LATER_COLS:
            col[name] = cs[:, at:at + n]
            at += n
        gavg, ident, wkv, wq, bkv_b = (col[k] for k in ("gavg", "ident", "wkv", "wq", "bkv"))
        bq_c, gamma_c = col["bq"][0:KD], col["gamma"][0:KD]
        awq, awk, awv, rw, rb_b = (col[k] for k in ("awq", "awk", "awv", "rw", "rb"))
        awo = col["awo"].rearrange("p (g c) -> p g c", g=2)
        tgt = col["target"].rearrange("p (k j) -> p k j", k=2)
        prefer = col["prefer"]
        first_slot = col["first_slot"]
        step128 = col["step128"]
        upto_c = col["upto"]
        tile_no = col["tile_no"]
        powers = col["powers"]

        xt = [kvT[k % 2][:, k // 2, 0:ROW] for k in range(4)]
        tag = sb("tag", [P, 8, 2])
        ttarget = sb("ttarget", [P, 8], U32)
        xh = [sb(f"xh{p}", [P, P], F32R) for p in range(2)]
        xl = [sb(f"xl{p}", [P, P], F32R) for p in range(2)]
        hb = rest
        sg = xs
        gt = xn
        gT = x1
        ys = [tn1[k % 2][:, k // 2, :] for k in range(4)]
        y0 = X[:].rearrange("p b n -> p (b n)").rearrange("p (t c) -> p t c", c=C)
        spare = prob[:].rearrange("p h k n -> p (h k n)")
        past = spare[:, 0:ST * E].rearrange("p (j e) -> p j e", e=E)
        pastn = spare[:, ST * E:2 * ST * E].rearrange("p (j e) -> p j e", e=E)
        cmp_ = spare[:, 2 * ST * E:2 * ST * E + E * MAXT].rearrange("p (e j) -> p e j", e=E)
        b2s, b2_rest = spare[:, 0:E * C], spare[:, E * C:2 * E * C]
        b2_parts = [spare[:, (4 + k) * E * C // 2:(5 + k) * E * C // 2].bitcast(BF16) for k in range(2)]
        y1 = prob[:].rearrange("p h k n -> p (h k n)").rearrange("p (t c) -> p t c", c=C)
        banks = [t[:].rearrange("p a n -> p (a n)") for t in (*MX, *EX)] + [
            PV[:].rearrange("p a n -> p (a n)"), W[0][:], W[1][:], W[2][:]]
        fin = [t[:].rearrange("p r n -> p (r n)").bitcast(F32)[:, 0:B // 2 * N].rearrange("p (b n) -> p b n", n=N)
               for t in (qst, kst)]

        names = """x_ld0 x_ld1 x_ld2 x_ld3 f_ld c_ld z_pool z_dve z_four g_bn g_ag g_sq g_m2 g_mm g_all g_sqm g_var
            g_eps g_rstd g_shift idb_ok xn_ok xs_ok kv_mm kv_ok q_mm q_ok vk_mm vk_ok out_mm x1_ok
            t1_mm T_ok bn1 agg1 nm1_ok ve1_ok rs1_ok nb1_ok tn1_ok t2_mm xnT_ok qk_mm hi_ok rest_ok
            mid_ok lo_ok v_mm v_ok vaug_ok parts_st stack_ld mx_mm mx_ok mp0 mr0 mp1 mp2 mT_mm mT_ok
            mrow_ld ex_mm ex_ok pv_mm oT_ok rden_ok onrm_ok ao_ok wo_mm t2_ok bn2 agg2 nm2_ok ve2_ok
            rs2_ok nb2_ok tn2_ok t3_mm x2T_ok rt_mm lg_ok z_cum z_b2 ones_ok w_ld fold_ld bgv_ld
            fold_mm Ah_ok Al_ok fbias_mm bias_ok route lexp_ok rank_mm copy_ok tag_ok gate_ok
            row_st0 row_st1 cend_ok cnt_mm cnt_ok tab tab_ok pad_st pad2_st slot_ld0 slot_ld1
            slot_ld2 slot_ld3 xT_mm xh_ok xl_ok gv_mm first_ok second_ok sg_ok gt_ok gT_mm gT_ok
            y_mm ys_ok b2_ok b2_ld res_st0 res_st1 res_st2 res_st3 sum fin_mm fin_ok out_st tags_ok
            ttarget_ok y_ld0 y_ld1 y_ld2 y_ld3""".split()
        s = {n: sem(n) for n in names}

        def pad_slots(eng, experts, pad_ok):
            eng.wait_ge(s["cnt_ok"], 1)
            for e in experts:
                n_e = eng.value_load(cnt_i[0:1, e:e + 1], min_val=0, max_val=TOK)
                eng.dma_start(slots[bass.ds(n_e + e * SLOTS, P), :], pad[e]).then_inc(s[pad_ok], 16)

        def rows_sent(eng, b, q):
            if not isinstance(b, int) or b >= 0:
                eng.wait_ge(s[f"row_st{q}"], TOP * TPB * in_lane(b, q, 2))

        block = ctx.enter_context(nc.Block())

        @block.sync
        def _(sp):
            for g in range(4):
                sp.dma_start(X[:, 4 * g:4 * g + 4, :],
                             x[4 * g:4 * g + 4].rearrange("b c n -> c b n")).then_inc(s[f"x_ld{g}"], 16)

            sp.dma_start(b2s.rearrange("p (e c) -> p e c", e=E), b2.partition_broadcast(P)).then_inc(s["b2_ld"], 16)
            sp.dma_start(w2s[:], w2.rearrange("e (k f) c -> f e k c", f=P)).then_inc(s["w_ld"], 16)

            def load_expert(e):
                need(sp, s["fbias_mm"], e)
                sp.dma_start(w1s[:], w1_t[bass.ds(e, 1)].rearrange("o (k f) d -> f (o k) d", f=P)
                             ).then_inc(s["fold_ld"], 16)
                for n, w in enumerate((wg, wv)):
                    sp.dma_start(wgv[:, :, n * FF:(n + 1) * FF],
                                 w[bass.ds(e, 1)].rearrange("o (k f) n -> f (o k) n", f=P)
                                 ).then_inc(s["fold_ld"], 16)
                sp.dma_start(b1s[:], b1[bass.ds(e, 1)].rearrange("o f k -> (o f) k")).then_inc(s["fold_ld"], 16)
                need(sp, s["bias_ok"], e)
                for n, v in enumerate((bg, bv2)):
                    sp.dma_start(bgv[:, n * FF:(n + 1) * FF], v[e].partition_broadcast(P)).then_inc(s["bgv_ld"], 16)

            sp.dma_start(slots[E * SLOTS:, :].rearrange("(t p) c -> t p c", p=P), pad[E:]).then_inc(s["pad_st"], 16)
            load_expert(0)

            def step(t, p):
                b, q = t - 4, p
                if live(b):
                    ring = b % RING if isinstance(b, int) else sp.snap(b % RING)
                    done(sp, s["mT_ok"], b + 1)
                    for part in range(3):
                        d = qst[STACK + part:STACK + part + 1, bass.ds(ring, 1), :]
                        sp.dma_start(d.rearrange("p o (r t) -> p (o r) t", t=P),
                                     mrow[q][part * H * TPB:(part + 1) * H * TPB, :]
                                     ).then_inc(s["mrow_ld"], 16)
                b = t - 2
                if live(b):
                    ring = b % RING if isinstance(b, int) else sp.snap(b % RING)
                    done_after(sp, (s["x_ld0"], 16), (s["parts_st"], b + 1, 16),
                               (s["ex_mm"], b - RING + 1, H))
                    src = scr[bass.ds(b, 1)].rearrange("o a (d h) t -> (o a d) h t", h=H)
                    for dst, runs in ((qst, ((0, 3), (0, 2), (0, 1))), (kst, ((3, 6), (4, 6), (5, 6)))):
                        row = 0
                        for lo, hi in runs:
                            n = (hi - lo) * HD
                            sp.dma_start(dst[row:row + n, bass.ds(ring, 1), :].rearrange("p o (h t) -> p (o h) t", h=H),
                                         src[lo * HD:hi * HD]).then_inc(s["stack_ld"], 16)
                            row += n
                b, q = t - 1, 1 - p
                if live(b):
                    done(sp, s["hi_ok"], b + 1)
                    done(sp, s["mid_ok"], b + 1)
                    done(sp, s["lo_ok"], b + 1)
                    sp.dma_start(scr[bass.ds(b, 1)].rearrange("o a p t -> (o p) a t"),
                                 parts[q][:]).then_inc(s["parts_st"], 16)
                if folds(t) and folds(t + 1):
                    load_expert(t + 1)

            steps(sp, step, B + 5)
            pad_slots(sp, range(E // 2), "pad_st")

            sp.wait_ge(s["vk_mm"], B)
            sp.wait_ge(s["pad_st"], 16 * (E // 2 + 1))
            sp.wait_ge(s["pad2_st"], 16 * (E // 2))
            for p in range(2):
                sp.wait_ge(s[f"row_st{p}"], 16 * 4 * B // 2)
            sp.wait_ge(s["tab_ok"], 2)

            def load_tile(j, r):
                need(sp, s["xT_mm"], j - 3)
                need(sp, s["tags_ok"], j - 3)
                first = sp.value_load(table_b[0:1, bass.ds(j, 1)], min_val=0, max_val=E * SLOTS + (SPARE - 1) * P)
                sp.dma_start(xt[r % 4], slots[bass.ds(first, P), :]).then_inc(s[f"slot_ld{r % 4}"], 16)

            tiles(sp, load_tile, 0)

            for lane in range(4):
                sp.wait_ge(s[f"res_st{lane}"], 16 * ST // 4)
            sp.wait_ge(s["xs_ok"], B)
            sp.wait_ge(s["pv_mm"], 2 * B)
            for g in range(4):
                for n, y in enumerate((y0, y1)):
                    sp.dma_start(y[:, g * (NT // 4):(g + 1) * (NT // 4), :],
                                 res[n * TOK + g * (TOK // 4):n * TOK + (g + 1) * (TOK // 4), :].rearrange(
                                     "(t p) c -> p t c", p=P)).then_inc(s[f"y_ld{g}"], 16)

            for g in range(B // 2):
                b = 2 * g % (B // 2)
                sp.wait_ge(s["fin_ok"], g + 1)
                sp.dma_start(out[2 * g:2 * g + 2].rearrange("b c n -> c b n"),
                             fin[2 * g // (B // 2)][:, b:b + 2, :]).then_inc(s["out_st"], 16)
            sp.wait_ge(s["out_st"], 16 * B // 2)

        @block.gpsimd
        def _(pool):
            for p in range(2):
                pool.memset(vaug[p][:], 0.0).then_inc(s["z_pool"], 1)
            pool.wait_ge(s["z_pool"], 2)
            for p in range(2):
                pool.memset(vaug[p][:, :, :, HD:HD + 1], 1.0).then_inc(s["z_pool"], 1)
            pool.memset(neg_half[:], -0.5).then_inc(s["z_pool"], 1)
            pool.wait_ge(s["z_pool"], 5)
            pool.memset(kst[STACK:P, :, :], 1.0).then_inc(s["z_pool"], 1)
            pool.wait_ge(s["z_pool"], 6)
            pool.memset(ones[:], 1.0).then_inc(s["ones_ok"], 1)

            def group_roots(lo, hi, again):
                pool.wait_ge(s["g_eps"], again + 1)
                pool.tensor_tensor(grstd[:, lo:hi], gvar[:, lo:hi], neg_half[:, lo:hi],
                                   ALU.pow).then_inc(s["g_rstd"], 1)

            group_roots(0, GN_FIRST, 0)
            met = (s["z_pool"], 6)

            def rounded(o, i):
                return pool.tensor_scalar(o, i, 1.0, 0.0, ALU.mult, ALU.add)

            flat = b2r[:].rearrange("p e c -> p (e c)")
            low = slice(2 * PART, 2 * PART + 1)
            pool.memset(b2r[:], 0.0).then_inc(s["z_b2"], 1)
            pool.wait_ge(s["b2_ld"], 16)
            rounded(b2_parts[0], b2s).then_inc(s["b2_ok"], 1)
            pool.wait_ge(s["b2_ok"], 1)
            pool.tensor_tensor(b2_rest, b2s, b2_parts[0], ALU.subtract).then_inc(s["b2_ok"], 1)
            pool.wait_ge(s["b2_ok"], 2)
            rounded(b2_parts[1], b2_rest).then_inc(s["b2_ok"], 1)
            pool.wait_ge(s["b2_ok"], 3)
            pool.wait_ge(s["z_b2"], 1)
            rounded(flat[0:1], b2_parts[0][0:1]).then_inc(s["b2_ok"], 1)
            rounded(flat[PART:PART + 1], b2_parts[1][PART:PART + 1]).then_inc(s["b2_ok"], 1)
            pool.tensor_tensor(flat[low], b2_rest[low], b2_parts[1][low], ALU.subtract).then_inc(s["b2_ok"], 1)
            pool.wait_ge(s["b2_ok"], 6)

            def scatter_rows(b, q, n):
                done_after(pool, met, (s["route"], b + 1, ROUTE), (s["copy_ok"], b + 1),
                           (s["tag_ok"], b + 1), (s["gate_ok"], b + 1))
                for k in range(TPB):
                    pool.indirect_dma_start(
                        out=slots, out_offset=bass.IndirectOffsetOnAxis(ap=dest[q][:, n, k:k + 1], axis=0),
                        in_=rows[q][:, n, k, :], in_offset=None).then_inc(s[f"row_st{q}"], 16)

            def step(t, p):
                o = 1 - p
                b, q = t - 5, o
                if live(b):
                    done(pool, s["rden_ok"], b + 1)
                    done(pool, s["ao_ok"], b - 1)
                    pool.tensor_tensor(onrm[q][:], oT[q][:],
                                       rden[q][:].rearrange("p (a o) -> p a o", o=1).broadcast_to([P, 16, 32]),
                                       ALU.mult).then_inc(s["onrm_ok"], 1)
                if live(t - 7):
                    scatter_rows(t - 7, o, 0)
                b, q = t - 1, o
                if live(b):
                    done(pool, s["mid_ok"], b + 1)
                    done(pool, s["parts_st"], b - 1, 16)
                    pool.tensor_tensor(part(parts[q], 2), halves(rest[q]), part(parts[q], 1),
                                       ALU.subtract).then_inc(s["lo_ok"], 1)
                if live(t - 7):
                    scatter_rows(t - 7, o, 1)
                b, q = t - 3, o
                if live(b):
                    m = mneg[q][:].rearrange("p h k -> p (h k)")
                    done_after(pool, met, (s["mx_ok"], b + 1, H), (s["mT_mm"], b - 1))
                    pool.tensor_scalar(mparts[q][:, 0, :], m, 1.0, 0.0, ALU.mult, ALU.add).then_inc(s["mp0"], 1)
                    done(pool, s["mp0"], b + 1)
                    pool.tensor_tensor(mrest[q][:], m, mparts[q][:, 0, :], ALU.subtract).then_inc(s["mr0"], 1)
                    done_after(pool, met, (s["mr0"], b + 1))
                    pool.tensor_scalar(mparts[q][:, 1, :], mrest[q][:], 1.0, 0.0, ALU.mult,
                                       ALU.add).then_inc(s["mp1"], 1)
                    done(pool, s["mp1"], b + 1)
                    pool.tensor_tensor(mparts[q][:, 2, :], mrest[q][:], mparts[q][:, 1, :],
                                       ALU.subtract).then_inc(s["mp2"], 1)
                if at_step(t, 2):
                    group_roots(GN_FIRST, B, 1)
                b, q = t, p
                if live(b):
                    root(b, q, nm1, ve1, rs1, nb1, "nm1_ok", "ve1_ok", "rs1_ok", "nb1_ok", "tn1_ok")
                b, q = t - 5, o
                if live(b):
                    root(b, q, nm2, ve2, rs2, nb2, "nm2_ok", "ve2_ok", "rs2_ok", "nb2_ok", "tn2_ok")

            def root(b, q, nm, ve, rs, nb, nm_ok, ve_ok, rs_ok, nb_ok, used):
                done(pool, s[used], b - 1, TPB)
                done(pool, s[ve_ok], b + 1)
                pool.tensor_tensor(rs[q][:], ve[q][:], neg_half[:, 0:TPB], ALU.pow).then_inc(s[rs_ok], 1)
                done(pool, s[nm_ok], b + 1)
                done(pool, s[rs_ok], b + 1)
                pool.tensor_tensor(nb[q][:], nm[q][:], rs[q][:], ALU.mult).then_inc(s[nb_ok], 1)

            steps(pool, step, B + 7)

            def scatter(j, r):
                if within(j):
                    need_after(pool, met, (s["tags_ok"], j + 1))
                    pool.tensor_scalar(ttarget[:, r:r + 1], tag[:, r, 1:2], 1.0, 0.0, ALU.mult,
                                       ALU.add).then_inc(s["ttarget_ok"], 1)
                    need_after(pool, met, (s["ys_ok"], j + 1), (s["ttarget_ok"], j + 1))
                    pool.indirect_dma_start(
                        out=res, out_offset=bass.IndirectOffsetOnAxis(ap=ttarget[:, r:r + 1], axis=0),
                        in_=ys[r % 4], in_offset=None).then_inc(s[f"res_st{r % 4}"], 16)

            tiles(pool, scatter, 0)

        @block.scalar
        def _(act):
            act.dma_start(cs[:, 0:N_FIRST], cols[:, 0:N_FIRST]).then_inc(s["f_ld"], 16)
            act.dma_start(cs[:, N_FIRST:], cols[:, N_FIRST:]).then_inc(s["c_ld"], 16)

            def head_exp(b, h):
                done(act, s["ex_mm"], b, H, h + 1)
                done(act, s["pv_mm"], b - 1, 2, h // 4 + 1)
                act.activation(prob[:, h, :, :], EX[h % 2][:], ACT.Exp, scale=SCALE).then_inc(s["ex_ok"], 1)

            def norm_x(b, p):
                if at_step(b, GN_FIRST):
                    act.wait_ge(s["g_shift"], 4)
                done(act, s["q_mm"], b - 1)
                act.activation(xn[p][:], pick(X, b), ACT.Identity, scale=grstd[:, bass.ds(b, 1)],
                               bias=gshift[:, bass.ds(b, 1)]).then_inc(s["xn_ok"], 1)

            def norm_plus_x(b, p):
                done(act, s["x1_ok"], b - 1)
                act.activation(xs[p][:], pick(X, b), ACT.Identity, scale=grstd1[:, bass.ds(b, 1)],
                               bias=gshift[:, bass.ds(b, 1)]).then_inc(s["xs_ok"], 1)

            def layer_norm(b, q, rs, nb, tn, nb_ok, tn_ok, used):
                done_after(act, (s["c_ld"], 16), (s[nb_ok], b + 1), (s[used], b - 1))
                for k in range(TPB):
                    act.activation(tn[:, k, :], pick(T, TPB * b + k), ACT.Identity, scale=rs[q][:, k:k + 1],
                                   bias=nb[q][:, k:k + 1]).then_inc(s[tn_ok], 1)

            def step(t, p):
                o = 1 - p
                e = live(t - 4)
                if live(t - 1):
                    layer_norm(t - 1, o, rs1, nb1, tn1[o], "nb1_ok", "tn1_ok", "t2_mm")
                b, q = t - 6, p
                if live(b):
                    rows_sent(act, b - 2, q)
                    done(act, s["gate_ok"], b - 1)
                    layer_norm(b, q, rs2, nb2, rows2[q], "nb2_ok", "tn2_ok", "t3_mm")
                b, q = t - 1, o
                if live(b):
                    done(act, s["t2_mm"], b + 1)
                    done(act, s["v_mm"], b - 1)
                    act.copy(xnT[q][:], W[0][:, 0:N]).then_inc(s["xnT_ok"], 1)
                b, q = t, p
                if live(b):
                    done(act, s["vk_mm"], b + 1)
                    done(act, s["out_mm"], b - 1)
                    act.activation(vkz[q][0:KD, :], W[1][0:KD, 0:C], ACT.Copy,
                                   scale=gamma_c).then_inc(s["vk_ok"], 1)
                b, q = t - 6, p
                if live(b):
                    done(act, s["t3_mm"], b + 1)
                    done(act, s["rt_mm"], b - 1)
                    act.copy(x2T[q][:], W[2][:, 0:N]).then_inc(s["x2T_ok"], 1)
                b, q = t - 1, o
                if live(b):
                    done(act, s["qk_mm"], b + 1)
                    done(act, s["parts_st"], b - 1, 16)
                    act.copy(part(parts[q], 0), halves(W[0])).then_inc(s["hi_ok"], 1)
                b, q = t, p
                if live(b):
                    done(act, s["q_mm"], b + 1)
                    act.activation(qz[q][0:KD, :], W[2][0:KD, 0:N], ACT.Identity,
                                   bias=bq_c).then_inc(s["q_ok"], 1)
                b, q = t - 6, p
                if live(b):
                    done(act, s["tn2_ok"], b + 1, TPB)
                    act.copy(rows[q][:, 1, :, 0:C], rows[q][:, 0, :, 0:C]).then_inc(s["copy_ok"], 1)
                    act.copy(rows[q][:, :, :, C + 1], tgt[:, :, bass.ds(TPB * b, TPB)]).then_inc(s["tag_ok"], 1)
                b, q = t - 1, o
                if live(b):
                    done(act, s["rest_ok"], b + 1)
                    act.copy(part(parts[q], 1), halves(rest[q])).then_inc(s["mid_ok"], 1)
                b, q = t - 4, p
                if live(b):
                    done(act, s["v_ok"], b + 1)
                    done(act, s["pv_mm"], b - 1, 2)
                    act.copy(vaug[q][:, :, :, 0:HD].rearrange("p k h d -> p (k h) d"),
                             pick(vring, b % RING).rearrange("p (r d) -> p r d", d=HD)
                             ).then_inc(s["vaug_ok"], 1)
                b, q = t - 1, o
                if live(b):
                    done(act, s["v_mm"], b + 1)
                    done(act, s["vaug_ok"], b - RING + 1)
                    act.copy(pick(vring, b % RING), W[2][:, 0:N]).then_inc(s["v_ok"], 1)
                b, q = t - 6, p
                if live(b):
                    done(act, s["route"], b, ROUTE, 1)
                    for k in range(TPB):
                        act.activation(lexp[q][:, k, :], lg[q][:, k, :], ACT.Exp,
                                       bias=lneg[q][:, k, :]).then_inc(s["lexp_ok"], 1)
                if isinstance(t, int) and t == 4:
                    act.wait_ge(s["b2_ok"], 6)
                if e:
                    for h in range(3):
                        head_exp(t - 4, h)
                b, q = t, p
                if live(b):
                    done(act, s["t1_mm"], b + 1)
                    act.copy(pick(T, TPB * b, TPB), W[2][:, 0:N]).then_inc(s["T_ok"], 1)
                if e:
                    head_exp(t - 4, 3)
                    head_exp(t - 4, 4)
                if folds(t):
                    need(act, s["fold_mm"], t + 1)
                    act.copy(pick(Ah, t), W[1][:]).then_inc(s["Ah_ok"], 1)
                if e:
                    head_exp(t - 4, 5)
                if live(t + 1):
                    norm_x(t + 1, o)
                if e:
                    head_exp(t - 4, 6)
                if e:
                    head_exp(t - 4, 7)
                if live(t + 1):
                    norm_plus_x(t + 1, o)
                b, q = t - 3, o
                if live(b):
                    done(act, s["mT_mm"], b + 1)
                    done(act, s["mrow_ld"], b - 1, 48)
                    act.copy(mrow[q][:], W[2][0:3 * H * TPB, 0:P // 2].bitcast(BF16)).then_inc(s["mT_ok"], 1)

            act.wait_ge(s["f_ld"], 16)
            act.wait_ge(s["c_ld"], 16)
            act.wait_ge(s["g_shift"], 2)
            norm_x(0, 0)
            norm_plus_x(0, 0)
            steps(act, step, B + 6)

            pad_slots(act, range(E // 2, E), "pad2_st")

            def tile(j, r):
                p = r % 2
                i, q = j + 1, 1 - p
                if within(i):
                    need(act, s["xT_mm"], i + 1)
                    need(act, s["gv_mm"], i - 1)
                    act.copy(xh[q][:], MX[q][:, 0, 0:P]).then_inc(s["xh_ok"], 1)
                    need(act, s["ttarget_ok"], i - 7)
                    act.copy(tag[:, (r + 1) % 8, :], xt[(r + 1) % 4][:, C:C + 2]).then_inc(s["tags_ok"], 1)
                i, q = j - 1, 1 - p
                if within(i):
                    need(act, s["gt_ok"], i - 1)
                    need(act, s["first_ok"], i + 1)
                    act.activation(sg[q][:], hb[q][:, 0:FF], ACT.Silu).then_inc(s["sg_ok"], 1)
                i, q = j - 2, p
                if within(i):
                    need(act, s["y_mm"], i - 1)
                    need(act, s["gT_mm"], i + 1)
                    act.copy(gT[q][:], (PV[:, 0, :], W[0][:, 0:FF])[q]).then_inc(s["gT_ok"], 1)
                i, q = j - 3, (r + 1) % 4
                if within(i):
                    if not isinstance(i, int) or i >= 4:
                        act.wait_ge(s[f"res_st{q}"], in_lane(i - 4, q))
                    need(act, s["y_mm"], i + 1)
                    act.activation(ys[q], W[1 + q % 2][:, 0:C], ACT.Copy, scale=tag[:, (r + 5) % 8, 0:1]
                                   ).then_inc(s["ys_ok"], 1)

            tiles(act, tile, 3, -1)

            for n, bank in enumerate(banks):
                act.wait_ge(s["fin_mm"], n + 1)
                act.copy(pick(fin[n // 4], 2 * (n % 4), 2), bank).then_inc(s["fin_ok"], 1)

        @block.vector
        def _(dve):
            for z in (qz[0], qz[1], vkz[0], vkz[1]):
                dve.memset(z[:], 0.0).then_inc(s["z_dve"], 1)
            for z in (cum[1], mask[1]):
                dve.memset(z[:], 0.0).then_inc(s["z_cum"], 1)

            def channel_stats(lo, hi):
                for b in range(lo, hi):
                    if b % 4 == 0:
                        dve.wait_ge(s[f"x_ld{b // 4}"], 16)
                    dve.bn_stats(gstat[:, b, :], X[:, b, :]).then_inc(s["g_bn"], 1)

            def channel_moments(lo, hi, again):
                dve.wait_ge(s["g_bn"], hi)
                for b in range(lo, hi):
                    dve.bn_aggr(gagg[:, b, :], gstat[:, b, :]).then_inc(s["g_ag"], 1)
                dve.wait_ge(s["g_ag"], hi)
                v = slice(lo, hi)
                dve.tensor_tensor(gtmp[:, v], gagg[:, v, 0], gagg[:, v, 0], ALU.mult).then_inc(s["g_sq"], 1)
                dve.wait_ge(s["g_sq"], again + 1)
                dve.tensor_tensor(gagg[:, v, 1], gagg[:, v, 1], gtmp[:, v], ALU.add).then_inc(s["g_m2"], 1)

            def group_variance(lo, hi, again):
                v = slice(lo, hi)
                dve.wait_ge(s["g_mm"], again + 1)
                dve.tensor_copy(gall[:, v, :].rearrange("p b k -> p (b k)"), MX[0][:, 0, 2 * lo:2 * hi]
                                ).then_inc(s["g_all"], 1)
                dve.wait_ge(s["g_all"], again + 1)
                dve.tensor_tensor(gtmp[:, v], gall[:, v, 0], gall[:, v, 0], ALU.mult).then_inc(s["g_sqm"], 1)
                dve.wait_ge(s["g_sqm"], again + 1)
                dve.tensor_tensor(gvar[:, v], gall[:, v, 1], gtmp[:, v], ALU.subtract).then_inc(s["g_var"], 1)
                dve.wait_ge(s["g_var"], again + 1)
                dve.tensor_scalar(gvar[:, v], gvar[:, v], GN_EPS, None, ALU.add).then_inc(s["g_eps"], 1)

            def group_scales(lo, hi, again):
                v = slice(lo, hi)
                dve.wait_ge(s["g_rstd"], again + 1)
                dve.scalar_tensor_tensor(gshift[:, v], gall[:, v, 0], -1.0, grstd[:, v], ALU.mult,
                                         ALU.mult).then_inc(s["g_shift"], 1)
                dve.tensor_scalar(grstd1[:, v], grstd[:, v], 1.0, None, ALU.add).then_inc(s["g_shift"], 1)

            channel_stats(0, GN_FIRST)
            channel_moments(0, GN_FIRST, 0)
            group_variance(0, GN_FIRST, 0)
            dve.wait_ge(s["f_ld"], 16)
            dve.tensor_copy(idb[:], ident).then_inc(s["idb_ok"], 1)
            group_scales(0, GN_FIRST, 0)
            dve.wait_ge(s["c_ld"], 16)
            dve.tensor_copy(tri[:], col["lower"]).then_inc(s["idb_ok"], 1)
            dve.wait_ge(s["z_cum"], 2)

            def over(v, n):
                return v.broadcast_to([P, v.shape[1], n])

            def along(v, k):
                return v.rearrange("p (o n) -> p o n", o=1).broadcast_to([P, k, v.shape[1]])

            def router(b, q):
                n = [0]

                def did(ins):
                    n[0] += 1
                    ins.then_inc(s["route"], 1)

                def wait():
                    done(dve, s["route"], b, ROUTE, n[0])

                did(dve.tensor_reduce(lneg[q][:], lg[q][:], AX.X, ALU.max, negate=True))
                yield
                done(dve, s["lexp_ok"], b + 1, TPB)
                did(dve.tensor_reduce(lsum[q][:], lexp[q][:], AX.X, ALU.add))
                yield
                wait()
                did(dve.reciprocal(linv[q][:], lsum[q][:]))
                yield
                wait()
                did(dve.tensor_tensor(prb[q][:, 0], lexp[q][:], over(linv[q][:], E), ALU.mult))
                for c in range(2):
                    yield
                    wait()
                    if c == 1:
                        did(dve.scalar_tensor_tensor(prb[q][:, 1], onehot[q][:, 0], -2.0, prb[q][:, 0],
                                                     ALU.mult, ALU.add))
                        yield
                    wait()
                    did(dve.tensor_reduce(gates[q][:, c], prb[q][:, c], AX.X, ALU.max))
                    yield
                    wait()
                    did(dve.tensor_tensor(hit[q][:, c], prb[q][:, c], over(gates[q][:, c], E), ALU.is_equal))
                    yield
                    wait()
                    did(dve.tensor_tensor(pickd[q][:, c], hit[q][:, c], along(prefer, TPB), ALU.mult))
                    yield
                    wait()
                    did(dve.tensor_reduce(best[q][:, c], pickd[q][:, c], AX.X, ALU.max))
                    yield
                    wait()
                    did(dve.tensor_tensor(onehot[q][:, c], pickd[q][:, c], over(best[q][:, c], E), ALU.is_equal))
                yield
                wait()
                did(dve.tensor_tensor(mask[q][:], onehot[q][:, 0], onehot[q][:, 1], ALU.add))
                did(dve.tensor_tensor(cum[q][:, 0], cum[1 - q][:, 1], mask[1 - q][:, 1], ALU.add))
                yield
                wait()
                did(dve.tensor_tensor(cum[q][:, 1], cum[q][:, 0], mask[q][:, 0], ALU.add))
                done(dve, s["copy_ok"], b + 1)
                dve.tensor_copy(rows[q][:, :, :, C], gates[q][:].rearrange("p c k o -> p c (k o)")
                                ).then_inc(s["gate_ok"], 1)
                assert n[0] == ROUTE - 4
                yield

            def send_to_slots(b, q):
                done(dve, s["rank_mm"], b + 1)
                dve.tensor_tensor(slot[q][:], W[2][:, 0:TPB * E].rearrange("p (k e) -> p k e", k=TPB),
                                  along(first_slot, TPB), ALU.add).then_inc(s["route"], 1)
                done(dve, s["route"], b, ROUTE, ROUTE - 3)
                for c in range(2):
                    dve.tensor_tensor(pickd[q][:, c], onehot[q][:, c], slot[q][:], ALU.mult).then_inc(s["route"], 1)
                rows_sent(dve, b - 2, q)
                done(dve, s["route"], b, ROUTE, ROUTE - 1)
                with nc.allow_low_precision(reason="slots are whole numbers, summed in float32"):
                    dve.tensor_reduce(dest[q][:].rearrange("p c k -> p (c k)"),
                                      pickd[q][:].rearrange("p c k e -> p (c k) e"), AX.X,
                                      ALU.add).then_inc(s["route"], 1)

            met = (s["x_ld0"], 16)

            def row_max(b, p, c):
                k, pair = c // 4, c % 4
                done(dve, s["mx_mm"], b, H, c + 1)
                if c == 0:
                    done(dve, s["mp2"], b - 1)
                dve.tensor_reduce(mneg[p][:, 2 * pair:2 * pair + 2, k], MX[c % 2][:], AX.X, ALU.max,
                                  negate=True).then_inc(s["mx_ok"], 1)

            def stats(b, q, st, ag, ve, nm, ready, bn, agg, ve_ok, nm_ok, used, route):
                done_after(dve, met, (s[ready], b + 1))
                for k in range(TPB):
                    dve.bn_stats(st[q][:, k, :], pick(T, TPB * b + k)).then_inc(s[bn], 1)
                next(route, None)
                for k in range(TPB):
                    done_after(dve, met, (s[used], b - 1), (s[bn], b, TPB, k + 1))
                    dve.bn_aggr(ag[q][:, k, :], st[q][:, k, :]).then_inc(s[agg], 1)
                next(route, None)
                done(dve, s[agg], b + 1, TPB)
                dve.tensor_scalar(ve[q][:], ag[q][:, :, 1], LN_EPS, None, ALU.add).then_inc(s[ve_ok], 1)
                dve.tensor_scalar(nm[q][:], ag[q][:, :, 0], -1.0, None, ALU.mult).then_inc(s[nm_ok], 1)

            def step(t, p):
                o = 1 - p
                m = live(t - 3)

                def row_maxima(*cs):
                    if m:
                        for c in cs:
                            row_max(t - 3, o, c)

                row_maxima(0)
                b, q = t, p
                if live(b):
                    done(dve, s["kv_mm"], b + 1)
                    done(dve, s["vk_mm"], b - 1)
                    dve.tensor_tensor(kvT[q][:], W[1][:, 0:TPB * (C + KD)].rearrange("p (k n) -> p k n", k=TPB),
                                      bkv_b.rearrange("p (o n) -> p o n", o=1).broadcast_to([P, TPB, C + KD]),
                                      ALU.add).then_inc(s["kv_ok"], 1)
                b, q = t - 5, o
                if live(b):
                    done(dve, s["pv_mm"], b + 1, 2)
                    done(dve, s["onrm_ok"], b - 1)
                    dve.transpose(oT[q][:].rearrange("p a r -> p (a r)"),
                                  PV[:].rearrange("p a n -> p (a n)")).then_inc(s["oT_ok"], 1)
                    done(dve, s["oT_ok"], b + 1)
                    dve.reciprocal(rden[q][:], oT[q][:, :, HD]).then_inc(s["rden_ok"], 1)
                if live(t - 7):
                    send_to_slots(t - 7, o)
                row_maxima(1, 2)
                b, q = t - 5, o
                if live(b):
                    done(dve, s["onrm_ok"], b + 1)
                    done(dve, s["wo_mm"], b - 1)
                    dve.transpose(ao[q][:].rearrange("p a n -> p (a n)"),
                                  onrm[q][:].rearrange("p a r -> p (a r)")).then_inc(s["ao_ok"], 1)
                if at_step(t, 2):
                    group_variance(GN_FIRST, B, 1)
                b, q = t - 1, o
                if live(b):
                    done(dve, s["hi_ok"], b + 1)
                    done(dve, s["lo_ok"], b - 1)
                    dve.tensor_tensor(halves(rest[q]), halves(W[0]), part(parts[q], 0),
                                      ALU.subtract).then_inc(s["rest_ok"], 1)
                b, q = t - 6, p
                if live(b):
                    done(dve, s["rt_mm"], b + 1)
                    dve.tensor_tensor(lg[q][:], W[1][:, 0:TPB * E].rearrange("p (k e) -> p k e", k=TPB),
                                      along(rb_b, TPB), ALU.add).then_inc(s["lg_ok"], 1)
                    done(dve, s["lg_ok"], b + 1)
                    route = router(b, q)
                else:
                    route = iter(())

                def maximum(c):
                    next(route, None)
                    row_maxima(c)
                    next(route, None)

                next(route, None)
                row_maxima(3, 4)
                b, q = t, p
                if live(b):
                    done(dve, s["out_mm"], b + 1)
                    done(dve, s["xs_ok"], b + 1)
                    done(dve, s["t1_mm"], b - 1)
                    dve.tensor_tensor(x1[q][:], W[1][:, 0:N], xs[q][:], ALU.add).then_inc(s["x1_ok"], 1)
                maximum(5)
                next(route, None)
                b, q = t - 5, o
                if live(b):
                    done(dve, s["wo_mm"], b + 1)
                    dve.tensor_tensor(pick(T, TPB * b, TPB), pick(T, TPB * b, TPB), W[0][:, 0:N],
                                      ALU.add).then_inc(s["t2_ok"], 1)
                maximum(6)
                next(route, None)
                maximum(7)
                b, q = t, p
                if live(b):
                    stats(b, q, st1, ag1, ve1, nm1, "T_ok", "bn1", "agg1", "ve1_ok", "nm1_ok", "nb1_ok", route)
                b, q = t - 5, o
                if live(b):
                    stats(b, q, st2, ag2, ve2, nm2, "t2_ok", "bn2", "agg2", "ve2_ok", "nm2_ok", "nb2_ok", route)
                if at_step(t, 0):
                    channel_stats(GN_FIRST, B)
                if at_step(t, 1):
                    channel_moments(GN_FIRST, B, 1)
                if at_step(t, 2):
                    group_scales(GN_FIRST, B, 1)
                if folds(t):
                    need(dve, s["Ah_ok"], t + 1)
                    dve.tensor_tensor(pick(Al, t), W[1][:], pick(Ah, t).bitcast(F32),
                                      ALU.subtract).then_inc(s["Al_ok"], 1)
                for _ in route:
                    pass
                if folds(t):
                    need(dve, s["fbias_mm"], t + 1)
                    dve.wait_ge(s["bgv_ld"], (t + 1) * 32)
                    dve.tensor_tensor(pick(bias, t), W[0][:], bgv[:], ALU.add).then_inc(s["bias_ok"], 1)

            steps(dve, step, B + 7)

            n_tab = [0]
            dve.memset(four[:], 0.0).then_inc(s["z_four"], 1)
            dve.wait_ge(s["z_four"], 1)

            def tab(ins):
                n_tab[0] += 1
                ins.then_inc(s["tab"], 1)
                dve.wait_ge(s["tab"], n_tab[0])

            dve.tensor_tensor(cend[:], cum[1][:, 1], mask[1][:, 1], ALU.add).then_inc(s["cend_ok"], 1)
            dve.wait_ge(s["cnt_mm"], 1)
            dve.wait_ge(s["pv_mm"], 2 * B)
            tab(dve.tensor_copy(cnt[:], W[0][:, 0:E]))
            dve.tensor_copy(cnt_i[:], cnt[:]).then_inc(s["cnt_ok"], 1)
            tab(dve.tensor_tensor(cmp_, cnt[:].rearrange("p (e o) -> p e o", o=1).broadcast_to([P, E, MAXT]),
                                  along(step128, E), ALU.is_gt))
            tab(dve.tensor_reduce(tiles_e[:], cmp_, AX.X, ALU.add))
            tab(dve.tensor_tensor(upto[:], along(tiles_e[:], E), upto_c.rearrange("p (a b) -> p a b", a=E),
                                  ALU.mult))
            tab(dve.tensor_reduce(ends[:], upto[:], AX.X, ALU.add))
            tab(dve.tensor_tensor(past, tile_no.rearrange("p (j o) -> p j o", o=1).broadcast_to([P, ST, E]),
                                  along(ends[:], ST), ALU.is_ge))
            tab(dve.tensor_reduce(te[:], past, AX.X, ALU.add))
            tab(dve.tensor_tensor(pastn, past, along(tiles_e[:], ST), ALU.mult))
            tab(dve.tensor_reduce(tstart[:], pastn, AX.X, ALU.add))
            tab(dve.tensor_tensor(toff[:], tile_no, tstart[:], ALU.subtract))
            tab(dve.tensor_scalar(toff2[:], toff[:], float(P), None, ALU.mult))
            dve.scalar_tensor_tensor(table_b[:], te[:], float(SLOTS), toff2[:], ALU.mult,
                                     ALU.add).then_inc(s["tab_ok"], 1)
            tab(dve.tensor_scalar(te1[:], te[:], float(E - 1), None, ALU.min))
            tab(dve.tensor_tensor(te4[:], te1[:].rearrange("p (g u) -> p g u", u=4), along(powers, ST // 4), ALU.mult))
            tab(dve.tensor_reduce(four[:, 1:ST // 4 + 1], te4[:], AX.X, ALU.add))
            dve.scalar_tensor_tensor(packed[:], four[:, 1:], float(E ** 4), four[:, 0:ST // 4 + 1], ALU.mult,
                                     ALU.add).then_inc(s["tab_ok"], 1)
            dve.wait_ge(s["tab_ok"], 2)

            def tile(j, r, experts):
                p = r % 2
                i, q = j - 1, 1 - p
                if within(i):
                    e = expert_of(experts, r, 1)
                    need(dve, s["gv_mm"], i + 1)
                    for n, ok in enumerate(("first_ok", "second_ok")):
                        v = slice(n * FF, (n + 1) * FF)
                        dve.tensor_tensor(hb[q][:, v], EX[q][:, n, :], pick(bias, e)[:, v], ALU.add).then_inc(s[ok], 1)
                i, q = j + 1, 1 - p
                if within(i):
                    need(dve, s["gv_mm"], i - 1)
                    need(dve, s["xh_ok"], i + 1)
                    dve.tensor_tensor(xl[q][:], MX[q][:, 0, 0:P], xh[q][:].bitcast(F32),
                                      ALU.subtract).then_inc(s["xl_ok"], 1)
                i, q = j - 1, 1 - p
                if within(i):
                    need(dve, s["gT_mm"], i - 1)
                    need(dve, s["second_ok"], i + 1)
                    need(dve, s["sg_ok"], i + 1)
                    dve.tensor_tensor(gt[q][:], sg[q][:], hb[q][:, FF:], ALU.mult).then_inc(s["gt_ok"], 1)

            dve.wait_ge(s["mid_ok"], B)
            dve.wait_ge(s["lo_ok"], B)
            tiles_by_four(dve, tile, packed, 1, -1)

            for g in range(8):
                if g % 2 == 0:
                    dve.wait_ge(s[f"y_ld{g // 2}"], 32)
                v = slice(g * (NT // 8), (g + 1) * (NT // 8))
                dve.tensor_tensor(y0[:, v, :], y0[:, v, :], y1[:, v, :], ALU.add).then_inc(s["sum"], 1)

        @block.tensor
        def _(pe):
            def group_means(lo, hi, again):
                pe.wait_ge(s["g_m2"], again + 1)
                pe.matmul(MX[0][:, 0, 2 * lo:2 * hi], gavg, gagg[:, lo:hi, :].rearrange("p b k -> p (b k)"),
                          start=True, stop=True).then_inc(s["g_mm"], 1)

            pe.wait_ge(s["f_ld"], 16)
            group_means(0, GN_FIRST, 0)
            pe.wait_ge(s["z_pool"], 6)
            pe.wait_ge(s["z_dve"], 4)
            pe.wait_ge(s["c_ld"], 16)
            pe.wait_ge(s["ones_ok"], 1)
            pe.wait_ge(s["idb_ok"], 2)

            def stack(t, b, h, lo=0, n=N, rows=STACK):
                v = t[0:rows, bass.ds(b % RING, 1), h * N + lo:h * N + lo + n]
                return v.rearrange("p o n -> p (o n)")

            def max_scores(b, c):
                k, pair = c // 4, c % 4
                if c == 0:
                    done(pe, s["stack_ld"], b + 1, 16 * LOADS)
                done(pe, s["mx_ok"], b, H, c - 1)
                if at_step(b, 0) and c == 0:
                    pe.wait_ge(s["g_all"], 2)
                for u in range(2):
                    h = 2 * pair + u
                    mm = pe.matmul(MX[c % 2][:, u, :], stack(qst, b, h, k * P, P), stack(kst, b, h),
                                   start=True, stop=True)
                mm.then_inc(s["mx_mm"], 1)

            def exp_scores(b, h):
                if h == 0:
                    done(pe, s["mrow_ld"], b + 1, 48)
                done(pe, s["ex_ok"], b, H, h - 1)
                for k in range(TPB):
                    mm = pe.matmul(EX[h % 2][:, k, :], stack(kst, b, h, k * P, P, QROWS),
                                   stack(qst, b, h, rows=QROWS), start=True, stop=True)
                mm.then_inc(s["ex_mm"], 1)

            def weigh(b, q, g):
                if g == 0:
                    done(pe, s["vaug_ok"], b + 1)
                    done(pe, s["oT_ok"], b)
                done(pe, s["ex_ok"], b, H, 4 * g + 4)
                for k in range(TPB):
                    for j in range(4):
                        mm = pe.matmul(PV[32 * j:32 * j + 32, g, :], vaug[q][:, k, 4 * g + j, :],
                                       prob[:, 4 * g + j, k, :], start=(k == 0), stop=(k == TPB - 1))
                mm.then_inc(s["pv_mm"], 1)

            def folded(ok, t, per=1):
                need(pe, ok, t if isinstance(t, int) else E, per, E)

            def step(t, p):
                o = 1 - p

                def maxima(*cs):
                    if live(t - 3):
                        for c in cs:
                            max_scores(t - 3, c)

                def exps(*hs):
                    if live(t - 4):
                        for h in hs:
                            exp_scores(t - 4, h)

                maxima(0)
                b, q = t, p
                if live(b):
                    done(pe, s["xn_ok"], b + 1)
                    done(pe, s["x1_ok"], t)
                    folded(s["Al_ok"], t)
                    for k in range(TPB):
                        mm = pe.matmul(W[1][:, k * (C + KD):(k + 1) * (C + KD)], xn[q][:, k * P:(k + 1) * P],
                                       wkv, start=True, stop=True)
                    mm.then_inc(s["kv_mm"], 1)
                b, q = t - 4, p
                if live(b):
                    done_after(pe, (s["c_ld"], 16), (s["mp2"], b + 1), (s["T_ok"], t), (s["v_ok"], t - 1))
                    pe.transpose(W[2][0:3 * H * TPB, 0:P // 2].bitcast(BF16),
                                 mparts[q][:].rearrange("p a r -> p (a r)"), idb[:]).then_inc(s["mT_mm"], 1)
                if live(t - 5):
                    weigh(t - 5, o, 1)
                b, q = t - 7, o
                if live(b):
                    done(pe, s["route"], b, ROUTE, ROUTE - 4)
                    done(pe, s["T_ok"], t)
                    done(pe, s["mT_ok"], t - 3)
                    pe.matmul(W[2][:, 0:TPB * E], tri[:], mask[q][:].rearrange("p k e -> p (k e)"),
                              start=True, stop=False)
                    pe.matmul(W[2][:, 0:TPB * E], ones[:], cum[q][:].rearrange("p k e -> p (k e)"),
                              start=False, stop=True).then_inc(s["rank_mm"], 1)
                if at_step(t, 2):
                    group_means(GN_FIRST, B, 1)
                b, q = t - 1, o
                if live(b):
                    done(pe, s["tn1_ok"], b + 1, TPB)
                    done(pe, s["t2_ok"], t - 5)
                    folded(s["bias_ok"], t)
                    for k in range(TPB):
                        mm = pe.transpose(W[0][:, k * P:(k + 1) * P], tn1[q][:, k, :], ident)
                    mm.then_inc(s["t2_mm"], 1)
                maxima(1)
                b, q = t, p
                if live(b):
                    done(pe, s["kv_ok"], b + 1)
                    for k in range(TPB):
                        mm = pe.matmul(W[1][0:KD, 0:C], kvT[q][:, k, C:C + KD], kvT[q][:, k, 0:C],
                                       start=(k == 0), stop=(k == TPB - 1))
                    mm.then_inc(s["vk_mm"], 1)
                maxima(2)
                b, q = t - 6, p
                if live(b):
                    done(pe, s["tn2_ok"], b + 1, TPB)
                    done(pe, s["T_ok"], t)
                    done(pe, s["mT_ok"], t - 3)
                    done(pe, s["route"], t - 7, ROUTE, ROUTE - 3)
                    for k in range(TPB):
                        mm = pe.transpose(W[2][:, k * P:(k + 1) * P], rows2[q][:, k, :], ident)
                    mm.then_inc(s["t3_mm"], 1)
                b, q = t - 1, o
                if live(b):
                    done(pe, s["xnT_ok"], b + 1)
                    pe.matmul(W[0][:, 0:N], awq, xnT[q][:], start=True, stop=True)
                    pe.matmul(W[0][:, N:2 * N], awk, xnT[q][:], start=True, stop=True).then_inc(s["qk_mm"], 1)
                b, q = t, p
                if live(b):
                    done(pe, s["x2T_ok"], t - 5)
                    done(pe, s["T_ok"], t)
                    done(pe, s["mT_ok"], t - 3)
                    pe.matmul(W[2][0:KD, 0:N], wq, xn[q][:], start=True, stop=True).then_inc(s["q_mm"], 1)
                b, q = t - 6, p
                if live(b):
                    done(pe, s["x2T_ok"], b + 1)
                    done(pe, s["vk_ok"], t + 1)
                    done(pe, s["x1_ok"], t)
                    folded(s["Al_ok"], t)
                    for k in range(TPB):
                        mm = pe.matmul(W[1][:, k * E:(k + 1) * E], x2T[q][:, k * P:(k + 1) * P], rw,
                                       start=True, stop=True)
                    mm.then_inc(s["rt_mm"], 1)
                maxima(3)
                b, q = t - 1, o
                if live(b):
                    done(pe, s["q_ok"], t + 1)
                    done(pe, s["x2T_ok"], t - 5)
                    for k in range(TPB):
                        mm = pe.matmul(W[2][:, k * C:(k + 1) * C], xnT[q][:, k * P:(k + 1) * P], awv,
                                       start=True, stop=True)
                    mm.then_inc(s["v_mm"], 1)
                maxima(4)
                exps(0)
                b, q = t, p
                if live(b):
                    done(pe, s["vk_ok"], b + 1)
                    done(pe, s["lg_ok"], t - 5)
                    done(pe, s["q_ok"], b + 1)
                    pe.matmul(W[1][:, 0:N], vkz[q][:], qz[q][:], start=True, stop=True).then_inc(s["out_mm"], 1)
                exps(1)
                maxima(5)
                b, q = t - 5, o
                if live(b):
                    done(pe, s["ao_ok"], b + 1)
                    done(pe, s["rest_ok"], t)
                    done(pe, s["t2_ok"], b)
                    for k in range(TPB):
                        for g in range(2):
                            mm = pe.matmul(W[0][:, k * C:(k + 1) * C], ao[q][:, g, k * P:(k + 1) * P],
                                           awo[:, g, :], start=(g == 0), stop=(g == 1))
                    mm.then_inc(s["wo_mm"], 1)
                exps(2)
                maxima(6)
                b, q = t, p
                if live(b):
                    done(pe, s["x1_ok"], b + 1)
                    done(pe, s["v_ok"], t)
                    for k in range(TPB):
                        mm = pe.transpose(W[2][:, k * P:(k + 1) * P], x1[q][:, k * P:(k + 1) * P], ident)
                    mm.then_inc(s["t1_mm"], 1)
                exps(3)
                maxima(7)
                if folds(t):
                    pe.wait_ge(s["fold_ld"], (t + 1) * 64)
                    done(pe, s["x1_ok"], t + 1)
                    for k in range(FF // P):
                        mm = pe.matmul(W[1][:], w1s[:, k, :], wgv[:, k, :], start=(k == 0), stop=(k == FF // P - 1))
                    mm.then_inc(s["fold_mm"], 1)
                exps(4, 5)
                if live(t - 4):
                    weigh(t - 4, p, 0)
                exps(6, 7)
                if folds(t):
                    done(pe, s["t2_ok"], t - 4)
                    done(pe, s["rest_ok"], t)
                    for k in range(FF // P):
                        mm = pe.matmul(W[0][:], b1s[:, k:k + 1].broadcast_to([P, P]), wgv[:, k, :],
                                       start=(k == 0), stop=(k == FF // P - 1))
                    mm.then_inc(s["fbias_mm"], 1)

            steps(pe, step, B + 7)

            pe.wait_ge(s["cend_ok"], 1)
            pe.wait_ge(s["t2_ok"], B)
            pe.matmul(W[0][:, 0:E], ones[:], cend[:], start=True, stop=True).then_inc(s["cnt_mm"], 1)
            pe.wait_ge(s["tab_ok"], 2)
            pe.wait_ge(s["w_ld"], 16)
            pe.wait_ge(s["b2_ok"], 6)
            pe.wait_ge(s["bias_ok"], E)

            def tile(j, r, experts):
                p = r % 2
                i, q = j + 2, (r + 2) % 4
                if within(i):
                    pe.wait_ge(s[f"slot_ld{q}"], in_lane(i, q))
                    need(pe, s["xl_ok"], i - 1)
                    pe.transpose(MX[q % 2][:, 0, 0:P], xt[q][:, 0:C], ident).then_inc(s["xT_mm"], 1)
                i, q = j - 3, 1 - p
                if within(i):
                    e = expert_of(experts, r, 3)
                    need(pe, s["ys_ok"], i - 1)
                    need(pe, s["gT_ok"], i + 1)
                    o = W[1 + q][:, 0:C]
                    pe.matmul(o, ones[:], pick(b2r, e), start=True, stop=False)
                    for k in range(FF // P):
                        mm = pe.matmul(o, gT[q][:, k * P:(k + 1) * P],
                                       w2s[:, bass.ds(e, 1), k, :].rearrange("p o c -> p (o c)"),
                                       start=False, stop=(k == FF // P - 1))
                    mm.then_inc(s["y_mm"], 1)
                i, q = j - 2, p
                if within(i):
                    need(pe, s["gT_ok"], i - 1)
                    need(pe, s["gt_ok"], i + 1)
                    for k in range(FF // P):
                        o = (PV[:, 0, :], W[0][:, 0:FF])[q]
                        mm = pe.transpose(o[:, k * P:(k + 1) * P], gt[q][:, k * P:(k + 1) * P], ident)
                    mm.then_inc(s["gT_mm"], 1)
                i, q = j, p
                if within(i):
                    e = expert_of(experts, r)
                    need(pe, s["second_ok"], i - 1)
                    need(pe, s["xl_ok"], i + 1)
                    o = EX[q][:].rearrange("p a n -> p (a n)")
                    pe.matmul(o, xh[q][:], pick(Ah, e), start=True, stop=False)
                    pe.matmul(o, xh[q][:], pick(Al, e), start=False, stop=False)
                    pe.matmul(o, xl[q][:], pick(Ah, e), start=False, stop=True).then_inc(s["gv_mm"], 1)

            tiles_by_four(pe, tile, packed, 3, -2)

            free = ("xl_ok", "gt_ok", "gT_ok", "ys_ok")
            for n, bank in enumerate(banks):
                pe.wait_ge(s[free[n // 2]], ST)
                for k in range(4):
                    pe.matmul(bank[:, k * P:(k + 1) * P], T[:, 4 * n + k, :], ident, start=(k == 0), stop=False)
            for n, bank in enumerate(banks):
                pe.wait_ge(s["sum"], n + 1)
                for k in range(4):
                    mm = pe.matmul(bank[:, k * P:(k + 1) * P], y0[:, 4 * n + k, :], ident, start=False, stop=(k == 3))
                mm.then_inc(s["fin_mm"], 1)


def kernel(**inputs):
    import concourse.bacc as _bacc
    from concourse.bass_utils import run_bass_kernel_spmd as _run

    a = {k: np.asarray(v) for k, v in inputs.items()}
    tables, pad = constants()

    def by_head(w):
        return w.T.reshape(C, H, HD).transpose(0, 2, 1).reshape(C, C)

    wo = np.zeros((4, 32, 2, C), np.float32)
    wo[:, 0:HD] = a["L1_attn_Wo"].T.reshape(2, 4, HD, C).transpose(1, 2, 0, 3)
    bq = np.zeros((P, 1), np.float32)
    bq[0:KD, 0] = a["L0_conv_bq"]
    small = {
        "wkv": np.concatenate([a["L0_conv_Wv"].T, a["L0_conv_Wk"].T], axis=1), "wq": a["L0_conv_Wq"].T,
        "bkv": np.concatenate([a["L0_conv_bv"], a["L0_conv_bk"]]), "bq": bq, "gamma": a["L0_conv_gamma"],
        "awq": by_head(a["L1_attn_Wq"]), "awk": by_head(a["L1_attn_Wk"]), "awv": a["L1_attn_Wv"].T,
        "awo": wo.reshape(P, 2 * C), "rw": a["L1_ffn_router_w"], "rb": a["L1_ffn_router_b"], **tables,
    }
    cols = np.concatenate([np.broadcast_to(small[k], (P, n)) for k, n in FIRST_COLS + LATER_COLS], axis=1)
    arrays = {
        "x": a["x"].reshape(B, C, N), "cols": cols,
        "w1_t": a["L1_ffn_w1"].transpose(0, 2, 1), "b1": a["L1_ffn_b1"].reshape(E, FF // P, P).transpose(0, 2, 1),
        "wg": a["L1_ffn_wg"], "bg": a["L1_ffn_bg"], "wv": a["L1_ffn_wv"], "bv2": a["L1_ffn_bv"],
        "w2": a["L1_ffn_w2"], "b2": a["L1_ffn_b2"], "pad": pad,
    }
    nc = _bacc.Bacc("TRN2", target_bir_lowering=False, num_devices=1)
    aps = {}
    for name, v in arrays.items():
        arrays[name] = v = np.ascontiguousarray(v)
        aps[name] = nc.dram_tensor(f"in_{name}", v.shape, mybir.dt.from_np(v.dtype), kind="ExternalInput").ap()
    out = nc.dram_tensor("out_0_dram", (B, C, N), F32, kind="ExternalOutput").ap()
    hybrid_block(nc, out=out, **aps)
    r = _run(nc, [{f"in_{name}": v for name, v in arrays.items()}], core_ids=[0])
    return r.results[0]["out_0_dram"].reshape(B, C, 16, 16)
```
